# Optimizing a Trainium2 kernel written in Bass

```python
import numpy as np
import jax
import jax.numpy as jnp

def _softmax(x, axis=-1):
    return jax.nn.softmax(x, axis=axis)

def _gelu(x):
    return jax.nn.gelu(x, approximate=True)

def _silu(x):
    return jax.nn.silu(x)

def _sigmoid(x):
    return jax.nn.sigmoid(x)

def _layernorm(x, axis=-1, eps=1e-05):
    m = jnp.mean(x, axis=axis, keepdims=True)
    v = jnp.var(x, axis=axis, keepdims=True)
    return (x - m) / jnp.sqrt(v + eps)

def _scatter_add(tgt, idx, src, axis=0):
    return tgt.at[idx].add(src)

def _segment_sum(src, seg, n):
    return jax.ops.segment_sum(src, seg, n)
kernel_name = 'mk_adaln_attn_ffn_d2_seqx_r8_71c9fd'

def setup_inputs(seed: int=0):
    np.random.seed(seed)
    _w = jnp.asarray

    def _rec_inputs():
        import jax
        import jax.numpy as jnp
        _rk = jax.random.key(seed)
        x = -0.0003929 + 0.9999 * jax.random.normal(jax.random.fold_in(_rk, 1), (64, 32, 512), jnp.float32)
        _lenS = 32 - jax.random.randint(jax.random.fold_in(_rk, 7), (64,), 0, max(1, 32 // 4) + 1, jnp.int32)
        _lenS2 = 32 - jax.random.randint(jax.random.fold_in(_rk, 8), (64,), 0, max(1, 32 // 4) + 1, jnp.int32)
        itok_B_78_3631 = jax.random.randint(jax.random.fold_in(_rk, 11), (64,), 78, 454, jnp.int32)
        itok_B_0_4 = jax.random.randint(jax.random.fold_in(_rk, 12), (64,), 0, 5, jnp.int32)
        itok_B_6_15 = jax.random.randint(jax.random.fold_in(_rk, 13), (64,), 6, 16, jnp.int32)
        itok_B_0_7 = jax.random.randint(jax.random.fold_in(_rk, 14), (64,), 0, 8, jnp.int32)
        return (x, itok_B_78_3631, itok_B_0_4, itok_B_6_15, itok_B_0_7)
    x, itok_B_78_3631, itok_B_0_4, itok_B_6_15, itok_B_0_7 = _rec_inputs()

    def _L0_cond_setup():
        import math
        import jax, jax.numpy as jnp
        import numpy as np
        B, H, N, L = (16, 32, 64, 512)
        DT_MIN, DT_MAX = (0.001, 0.1)

        def _get_kernel(log_dt, C, log_A_real, A_imag, length):
            dt = jnp.exp(log_dt)
            Cc = C[..., 0] + 1j * C[..., 1]
            A = -jnp.exp(log_A_real) + 1j * A_imag
            dtA = A * dt[:, None]
            Ct = Cc * (jnp.exp(dtA) - 1.0) / A
            P = dtA[:, :, None] * jnp.arange(length, dtype=jnp.float32)
            K = 2.0 * jnp.einsum('hn,hnl->hl', Ct, jnp.exp(P)).real
            return K
        key = jax.random.key(seed)
        ks = jax.random.split(key, 5)
        u = jax.random.normal(ks[0], (B, H, L), dtype=jnp.float32)
        log_dt = jax.random.uniform(ks[1], (H,), dtype=jnp.float32) * (math.log(DT_MAX) - math.log(DT_MIN)) + math.log(DT_MIN)
        C = jax.random.normal(ks[2], (H, N, 2), dtype=jnp.float32)
        log_A_real = jnp.log(0.5 * jnp.ones((H, N), dtype=jnp.float32))
        A_imag = math.pi * jnp.broadcast_to(jnp.arange(N, dtype=jnp.float32), (H, N))
        D = jax.random.normal(ks[3], (H,), dtype=jnp.float32)
        length = jax.random.randint(ks[4], (B,), 1, L + 1, dtype=jnp.int32)
        return {'u': u, 'log_dt': log_dt, 'C': C, 'log_A_real': log_A_real, 'A_imag': A_imag, 'D': D, 'length': length}
    _L0_cond_all = _L0_cond_setup()
    _L0_cond_in = {k: v for k, v in _L0_cond_all.items() if k in ('log_dt', 'C', 'log_A_real', 'A_imag', 'D')}
    del _L0_cond_all

    def _L0_attn_setup():
        import jax, jax.numpy as jnp
        import numpy as np
        H = 32
        DN = 128
        DR = 64
        DV = 128
        DQ = DN + DR
        HID = 512
        NEG_INF = -1e+30
        key = jax.random.key(seed)
        k0, k1, k2, k3 = jax.random.split(key, 4)
        B, S = (4, 128)
        hidden_states = jax.random.normal(k0, (B, S, HID), dtype=jnp.float32)
        wq = jax.random.normal(k1, (HID, H * DQ), dtype=jnp.float32) * 0.02
        wkv = jax.random.normal(k2, (HID, H * (DN + DV) + DR), dtype=jnp.float32) * 0.02
        wo = jax.random.normal(k3, (H * DV, HID), dtype=jnp.float32) * 0.02
        return {'hidden_states': hidden_states, 'wq': wq, 'wkv': wkv, 'wo': wo}
    _L0_attn_all = _L0_attn_setup()
    _L0_attn_in = {k: v for k, v in _L0_attn_all.items() if k in ('wq', 'wkv', 'wo')}
    del _L0_attn_all

    def _L0_cond2_setup():
        import jax, jax.numpy as jnp
        import numpy as np
        B, S, D_IN, D_OUT = (8, 256, 512, 512)
        R, NUM_LABELERS = (32, 5)
        LORA_SCALING = 16 / 32
        key = jax.random.key(seed)
        k1, k2, k3, k4, k5, k6 = jax.random.split(key, 6)
        inp = {'input': jax.random.normal(k1, (B, S, D_IN), dtype=jnp.float32), 'weight': jax.random.normal(k2, (D_OUT, D_IN), dtype=jnp.float32) * 0.02, 'bias': jax.random.normal(k3, (D_OUT,), dtype=jnp.float32) * 0.02, 'lora_A': jax.random.normal(k4, (NUM_LABELERS, D_IN, R), dtype=jnp.float32) * 0.02, 'lora_B': jax.random.normal(k5, (D_OUT, R), dtype=jnp.float32) * 0.02, 'labeler_index': jax.random.randint(k6, (B,), 0, NUM_LABELERS, dtype=jnp.int64) if jax.config.jax_enable_x64 else jax.random.randint(k6, (B,), 0, NUM_LABELERS, dtype=jnp.int32)}
        return inp
    _L0_cond2_all = _L0_cond2_setup()
    _L0_cond2_in = {k: v for k, v in _L0_cond2_all.items() if k in ('weight', 'bias', 'lora_A', 'lora_B')}
    del _L0_cond2_all

    def _L0_ffn_setup():
        import jax, jax.numpy as jnp
        import numpy as np
        _TRIPLES = [(1, 2, 3), (1, 4, 5), (1, 7, 6), (2, 4, 6), (2, 5, 7), (3, 4, 7), (3, 6, 5)]

        def _oct_struct():
            S = np.zeros((8, 8, 8), np.float32)
            S[0, 0, 0] = 1.0
            for i in range(1, 8):
                S[0, i, i] = 1.0
                S[i, 0, i] = 1.0
                S[i, i, 0] = -1.0
            for a, b, c in _TRIPLES:
                for x, y, z in ((a, b, c), (b, c, a), (c, a, b)):
                    S[x, y, z] = 1.0
                    S[y, x, z] = -1.0
            return jnp.asarray(S)
        S_OCT = _oct_struct()
        N_EMBD = 512
        HIDDEN = 1366

        def ternary_dequant(W):
            scale = jnp.mean(jnp.abs(W))
            Wq = scale * jnp.clip(jnp.round(W / scale), -1.0, 1.0)
            return W + jax.lax.stop_gradient(Wq - W)

        def oct_ternary_linear(xp, W):
            Wq = ternary_dequant(W)
            M = jnp.einsum('jik,jod->koid', S_OCT, Wq)
            return jnp.einsum('...id,koid->...ko', xp, M)
        key = jax.random.key(seed)
        k1, k2, k3, k4 = jax.random.split(key, 4)
        B, T = (2, 256)
        d8, h8 = (N_EMBD // 8, HIDDEN // 8)
        std_in = 1.0 / np.sqrt(N_EMBD)
        std_h = 1.0 / np.sqrt(HIDDEN)
        return {'x': jax.random.normal(k1, (B, T, N_EMBD), jnp.float32), 'w_gate': jax.random.normal(k2, (8, h8, d8), jnp.float32) * std_in, 'w_up': jax.random.normal(k3, (8, h8, d8), jnp.float32) * std_in, 'w_down': jax.random.normal(k4, (8, d8, h8), jnp.float32) * std_h}
    _L0_ffn_all = _L0_ffn_setup()
    _L0_ffn_in = {k: v for k, v in _L0_ffn_all.items() if k in ('w_gate', 'w_up', 'w_down')}
    del _L0_ffn_all

    def _L1_cond_setup():
        import jax, jax.numpy as jnp
        import numpy as np
        B, S, D_IN, D_OUT = (4, 256, 512, 512)
        RANK, MAX_LORAS = (16, 32)
        key = jax.random.key(seed)
        ks = jax.random.split(key, 6)
        x = jax.random.normal(ks[0], (B, S, D_IN), dtype=jnp.float32)
        adapter_ids = jax.random.randint(ks[1], (B,), 0, MAX_LORAS)
        base_weight = jax.random.normal(ks[2], (D_OUT, D_IN), dtype=jnp.float32) * D_IN ** (-0.5)
        base_bias = jax.random.normal(ks[3], (D_OUT,), dtype=jnp.float32) * 0.01
        lora_A_w = jax.random.normal(ks[4], (MAX_LORAS, RANK, D_IN), dtype=jnp.float32) * D_IN ** (-0.5)
        lora_B_w = jax.random.normal(ks[5], (MAX_LORAS, D_OUT, RANK), dtype=jnp.float32) * RANK ** (-0.5)
        return {'x': x, 'adapter_ids': adapter_ids, 'base_weight': base_weight, 'base_bias': base_bias, 'lora_A_w': lora_A_w, 'lora_B_w': lora_B_w}
    _L1_cond_all = _L1_cond_setup()
    _L1_cond_in = {k: v for k, v in _L1_cond_all.items() if k in ('base_weight', 'base_bias', 'lora_A_w', 'lora_B_w')}
    del _L1_cond_all

    def _L1_attn_setup():
        import jax, jax.numpy as jnp
        import numpy as np
        HDC_DIM = 512
        N_HEADS = 4
        HEAD_DIM = HDC_DIM // N_HEADS

        def _ste_sign(w):
            alpha = jnp.mean(jnp.abs(w), axis=-1, keepdims=True)
            hard = alpha * jnp.sign(w)
            hard = jnp.where(hard == 0, alpha, hard)
            return jax.lax.stop_gradient(hard - w) + w
        key = jax.random.key(seed)
        kx, kq, kk, kv = jax.random.split(key, 4)
        B, T = (4, 256)
        x = jax.random.normal(kx, (B, T, HDC_DIM), dtype=jnp.float32)
        bv_q = jax.random.normal(kq, (N_HEADS, HEAD_DIM), dtype=jnp.float32) * 0.02
        bv_k = jax.random.normal(kk, (N_HEADS, HEAD_DIM), dtype=jnp.float32) * 0.02
        bv_v = jax.random.normal(kv, (N_HEADS, HEAD_DIM), dtype=jnp.float32) * 0.02
        return {'x': x, 'bv_q': bv_q, 'bv_k': bv_k, 'bv_v': bv_v}
    _L1_attn_all = _L1_attn_setup()
    _L1_attn_in = {k: v for k, v in _L1_attn_all.items() if k in ('bv_q', 'bv_k', 'bv_v')}
    del _L1_attn_all

    def _L1_cond2_setup():
        import jax, jax.numpy as jnp
        import numpy as np
        TOP_K = 2
        LANG_BIAS = 5.0
        SCALING = 32.0 / 16.0
        LANGUAGE_PAD_ID = -1
        key = jax.random.key(seed)
        ks = jax.random.split(key, 6)
        B, T, D, O, E, R = (4, 256, 512, 512, 8, 16)
        x = jax.random.normal(ks[0], (B, T, D), dtype=jnp.float32)
        language_ids = jax.random.randint(ks[1], (B,), 0, E).astype(jnp.int64)
        W = jax.random.normal(ks[2], (O, D), dtype=jnp.float32) * (1.0 / np.sqrt(D))
        Wr = jax.random.normal(ks[3], (E, D), dtype=jnp.float32) * (1.0 / np.sqrt(D))
        A = jax.random.normal(ks[4], (E, R, D), dtype=jnp.float32) * (1.0 / np.sqrt(D))
        Bm = jax.random.normal(ks[5], (O, R), dtype=jnp.float32) * 0.0
        Bm = jnp.broadcast_to(Bm, (E, O, R)) + jax.random.normal(ks[5], (E, O, R), dtype=jnp.float32) * 0.02
        return {'x': x, 'language_ids': language_ids, 'W': W, 'Wr': Wr, 'A': A, 'B': Bm}
    _L1_cond2_all = _L1_cond2_setup()
    _L1_cond2_in = {k: v for k, v in _L1_cond2_all.items() if k in ('W', 'Wr', 'A', 'B')}
    del _L1_cond2_all

    def _L1_ffn_setup():
        import jax, jax.numpy as jnp
        import numpy as np

        def sparsemax(z):
            E = z.shape[-1]
            z_sorted = -jnp.sort(-z, axis=-1)
            z_cum = jnp.cumsum(z_sorted, axis=-1)
            k = jnp.arange(1, E + 1, dtype=z.dtype)
            support = 1.0 + k * z_sorted > z_cum
            k_z = jnp.sum(support, axis=-1, keepdims=True)
            tau_sum = jnp.take_along_axis(z_cum, k_z.astype(jnp.int32) - 1, axis=-1)
            tau = (tau_sum - 1.0) / k_z.astype(z.dtype)
            return jnp.maximum(z - tau, 0.0)
        key = jax.random.key(seed)
        ks = jax.random.split(key, 6)
        B, S, D_IN, D_OUT, E, R = (8, 256, 512, 512, 8, 16)
        x = jax.random.normal(ks[0], (B, S, D_IN), dtype=jnp.float32)
        W_base = jax.random.normal(ks[1], (D_OUT, D_IN), dtype=jnp.float32) * D_IN ** (-0.5)
        b_base = jax.random.normal(ks[2], (D_OUT,), dtype=jnp.float32) * 0.01
        W_router = jax.random.normal(ks[3], (E, D_IN), dtype=jnp.float32) * D_IN ** (-0.5)
        b_router = jnp.zeros((E,), dtype=jnp.float32)
        lora_A = jax.random.normal(ks[4], (E, D_IN, R), dtype=jnp.float32) * D_IN ** (-0.5)
        lora_B = jnp.zeros((E, R, D_OUT), dtype=jnp.float32)
        return {'x': x, 'W_base': W_base, 'b_base': b_base, 'W_router': W_router, 'b_router': b_router, 'lora_A': lora_A, 'lora_B': lora_B}
    _L1_ffn_all = _L1_ffn_setup()
    _L1_ffn_in = {k: v for k, v in _L1_ffn_all.items() if k in ('W_base', 'b_base', 'W_router', 'b_router', 'lora_A', 'lora_B')}
    del _L1_ffn_all
    return {'x': x, 'itok_B_78_3631': itok_B_78_3631, 'itok_B_0_4': itok_B_0_4, 'itok_B_6_15': itok_B_6_15, 'itok_B_0_7': itok_B_0_7, 'L0_cond_log_dt': _L0_cond_in['log_dt'], 'L0_cond_C': _L0_cond_in['C'], 'L0_cond_log_A_real': _L0_cond_in['log_A_real'], 'L0_cond_A_imag': _L0_cond_in['A_imag'], 'L0_cond_D': _L0_cond_in['D'], 'L0_attn_wq': _L0_attn_in['wq'], 'L0_attn_wkv': _L0_attn_in['wkv'], 'L0_attn_wo': _L0_attn_in['wo'], 'L0_cond2_weight': _L0_cond2_in['weight'], 'L0_cond2_bias': _L0_cond2_in['bias'], 'L0_cond2_lora_A': _L0_cond2_in['lora_A'], 'L0_cond2_lora_B': _L0_cond2_in['lora_B'], 'L0_ffn_w_gate': _L0_ffn_in['w_gate'], 'L0_ffn_w_up': _L0_ffn_in['w_up'], 'L0_ffn_w_down': _L0_ffn_in['w_down'], 'L1_cond_base_weight': _L1_cond_in['base_weight'], 'L1_cond_base_bias': _L1_cond_in['base_bias'], 'L1_cond_lora_A_w': _L1_cond_in['lora_A_w'], 'L1_cond_lora_B_w': _L1_cond_in['lora_B_w'], 'L1_attn_bv_q': _L1_attn_in['bv_q'], 'L1_attn_bv_k': _L1_attn_in['bv_k'], 'L1_attn_bv_v': _L1_attn_in['bv_v'], 'L1_cond2_W': _L1_cond2_in['W'], 'L1_cond2_Wr': _L1_cond2_in['Wr'], 'L1_cond2_A': _L1_cond2_in['A'], 'L1_cond2_B': _L1_cond2_in['B'], 'L1_ffn_W_base': _L1_ffn_in['W_base'], 'L1_ffn_b_base': _L1_ffn_in['b_base'], 'L1_ffn_W_router': _L1_ffn_in['W_router'], 'L1_ffn_b_router': _L1_ffn_in['b_router'], 'L1_ffn_lora_A': _L1_ffn_in['lora_A'], 'L1_ffn_lora_B': _L1_ffn_in['lora_B']}

def reference(x, itok_B_78_3631, itok_B_0_4, itok_B_6_15, itok_B_0_7, L0_cond_log_dt, L0_cond_C, L0_cond_log_A_real, L0_cond_A_imag, L0_cond_D, L0_attn_wq, L0_attn_wkv, L0_attn_wo, L0_cond2_weight, L0_cond2_bias, L0_cond2_lora_A, L0_cond2_lora_B, L0_ffn_w_gate, L0_ffn_w_up, L0_ffn_w_down, L1_cond_base_weight, L1_cond_base_bias, L1_cond_lora_A_w, L1_cond_lora_B_w, L1_attn_bv_q, L1_attn_bv_k, L1_attn_bv_v, L1_cond2_W, L1_cond2_Wr, L1_cond2_A, L1_cond2_B, L1_ffn_W_base, L1_ffn_b_base, L1_ffn_W_router, L1_ffn_b_router, L1_ffn_lora_A, L1_ffn_lora_B):
    import jax
    import jax.numpy as jnp

    def _L0_cond_ref(u, log_dt, C, log_A_real, A_imag, D, length):
        import math
        import jax, jax.numpy as jnp
        import numpy as np
        B, H, N, L = (16, 32, 64, 512)
        DT_MIN, DT_MAX = (0.001, 0.1)

        def _get_kernel(log_dt, C, log_A_real, A_imag, length):
            dt = jnp.exp(log_dt)
            Cc = C[..., 0] + 1j * C[..., 1]
            A = -jnp.exp(log_A_real) + 1j * A_imag
            dtA = A * dt[:, None]
            Ct = Cc * (jnp.exp(dtA) - 1.0) / A
            P = dtA[:, :, None] * jnp.arange(length, dtype=jnp.float32)
            K = 2.0 * jnp.einsum('hn,hnl->hl', Ct, jnp.exp(P)).real
            return K
        Bq, Hq, Lq = u.shape
        K = _get_kernel(log_dt, C, log_A_real, A_imag, Lq)
        n = 2 * Lq
        kf = jnp.fft.rfft(K, n=n)
        uf = jnp.fft.rfft(u, n=n)
        y = jnp.fft.irfft(uf * kf[None], n=n)[..., :Lq]
        y = y + u * D[:, None]
        mask = (jnp.arange(Lq)[None, :] < length[:, None]).astype(u.dtype)
        return y * mask[:, None, :]

    def _L0_attn_ref(hidden_states, wq, wkv, wo):
        import jax, jax.numpy as jnp
        import numpy as np
        H = 32
        DN = 128
        DR = 64
        DV = 128
        DQ = DN + DR
        HID = 512
        NEG_INF = -1e+30
        B, S, D = hidden_states.shape
        q = jnp.einsum('bsd,de->bse', hidden_states, wq).reshape(B, S, H, DQ)
        kv = jnp.einsum('bsd,de->bse', hidden_states, wkv)
        k = kv[..., :H * DN].reshape(B, S, H, DN)
        v = kv[..., H * DN:H * (DN + DV)].reshape(B, S, H, DV)
        scale = DQ ** (-0.5)
        scores = jnp.einsum('bqhd,bkhd->bhqk', q[..., :DN], k) * scale
        causal = jnp.tril(jnp.ones((S, S), dtype=bool))
        scores = jnp.where(causal[None, None], scores, NEG_INF)
        probs = jax.nn.softmax(scores, axis=-1)
        attn = jnp.einsum('bhqk,bkhd->bqhd', probs, v).reshape(B, S, H * DV)
        return jnp.einsum('bse,ed->bsd', attn, wo)

    def _L0_cond2_ref(input, weight, bias, lora_A, lora_B, labeler_index):
        import jax, jax.numpy as jnp
        import numpy as np
        B, S, D_IN, D_OUT = (8, 256, 512, 512)
        R, NUM_LABELERS = (32, 5)
        LORA_SCALING = 16 / 32
        base = jnp.einsum('bsi,oi->bso', input, weight) + bias
        labelers_A = lora_A[labeler_index]
        ax = jnp.einsum('bsi,bir->bsr', input, labelers_A)
        delta = jnp.einsum('bsr,or->bso', ax, lora_B)
        return base + delta * LORA_SCALING

    def _L0_ffn_ref(x, w_gate, w_up, w_down):
        import jax, jax.numpy as jnp
        import numpy as np
        _TRIPLES = [(1, 2, 3), (1, 4, 5), (1, 7, 6), (2, 4, 6), (2, 5, 7), (3, 4, 7), (3, 6, 5)]

        def _oct_struct():
            S = np.zeros((8, 8, 8), np.float32)
            S[0, 0, 0] = 1.0
            for i in range(1, 8):
                S[0, i, i] = 1.0
                S[i, 0, i] = 1.0
                S[i, i, 0] = -1.0
            for a, b, c in _TRIPLES:
                for x, y, z in ((a, b, c), (b, c, a), (c, a, b)):
                    S[x, y, z] = 1.0
                    S[y, x, z] = -1.0
            return jnp.asarray(S)
        S_OCT = _oct_struct()
        N_EMBD = 512
        HIDDEN = 1366

        def ternary_dequant(W):
            scale = jnp.mean(jnp.abs(W))
            Wq = scale * jnp.clip(jnp.round(W / scale), -1.0, 1.0)
            return W + jax.lax.stop_gradient(Wq - W)

        def oct_ternary_linear(xp, W):
            Wq = ternary_dequant(W)
            M = jnp.einsum('jik,jod->koid', S_OCT, Wq)
            return jnp.einsum('...id,koid->...ko', xp, M)
        B, T, D = x.shape
        xp = x.reshape(B, T, 8, D // 8)
        gate = oct_ternary_linear(xp, w_gate).reshape(B, T, -1)
        up = oct_ternary_linear(xp, w_up).reshape(B, T, -1)
        h = jax.nn.silu(gate) * up
        hp = h.reshape(B, T, 8, h.shape[-1] // 8)
        out = oct_ternary_linear(hp, w_down).reshape(B, T, D)
        return out

    def _L1_cond_ref(x, adapter_ids, base_weight, base_bias, lora_A_w, lora_B_w):
        import jax, jax.numpy as jnp
        import numpy as np
        B, S, D_IN, D_OUT = (4, 256, 512, 512)
        RANK, MAX_LORAS = (16, 32)
        result = jnp.einsum('bsd,od->bso', x, base_weight) + base_bias
        A = lora_A_w[adapter_ids]
        Bw = lora_B_w[adapter_ids]
        h = jnp.einsum('bsd,brd->bsr', x, A)
        lora_out = jnp.einsum('bsr,bor->bso', h, Bw)
        result = result + lora_out
        return result.astype(x.dtype)

    def _L1_attn_ref(x, bv_q, bv_k, bv_v):
        import jax, jax.numpy as jnp
        import numpy as np
        HDC_DIM = 512
        N_HEADS = 4
        HEAD_DIM = HDC_DIM // N_HEADS

        def _ste_sign(w):
            alpha = jnp.mean(jnp.abs(w), axis=-1, keepdims=True)
            hard = alpha * jnp.sign(w)
            hard = jnp.where(hard == 0, alpha, hard)
            return jax.lax.stop_gradient(hard - w) + w
        B, T, D = x.shape
        H, HD = (N_HEADS, HEAD_DIM)
        scale = HD ** (-0.5)
        q_bind = _ste_sign(bv_q)
        k_bind = _ste_sign(bv_k)
        v_bind = _ste_sign(bv_v)
        xh = x.reshape(B, T, H, HD)
        Q = xh * q_bind
        K = xh * k_bind
        V = xh * v_bind
        scores = jnp.einsum('bthd,bshd->bhts', Q, K) * scale
        causal = jnp.tril(jnp.ones((T, T), dtype=bool))
        attn = jnp.where(causal, jax.nn.sigmoid(scores * 4.0), 0.0)
        out = jnp.einsum('bhts,bshd->bthd', attn, V)
        return out.reshape(B, T, D)

    def _L1_cond2_ref(x, language_ids, W, Wr, A, B):
        import jax, jax.numpy as jnp
        import numpy as np
        TOP_K = 2
        LANG_BIAS = 5.0
        SCALING = 32.0 / 16.0
        LANGUAGE_PAD_ID = -1
        base = jnp.einsum('btd,od->bto', x, W)
        E = Wr.shape[0]
        logits = jnp.einsum('btd,ed->bte', x.astype(jnp.float32), Wr.astype(jnp.float32))
        expert_targets = language_ids
        valid = expert_targets >= 0
        tgt = jnp.where(valid, expert_targets, 0)
        bias = jax.nn.one_hot(tgt, E, dtype=logits.dtype) * LANG_BIAS
        bias = jnp.where(valid[:, None], bias, 0.0)
        logits = logits + bias[:, None, :]
        topw, topi = jax.lax.top_k(logits, TOP_K)
        weights = jax.nn.softmax(topw, axis=-1)
        gates = jnp.sum(jax.nn.one_hot(topi, E, dtype=weights.dtype) * weights[..., None], axis=-2)
        gates = gates.astype(x.dtype)
        h = jnp.einsum('btd,erd->bter', x, A)
        lora_out = jnp.einsum('bter,bte,eor->bto', h, gates, B)
        return base + SCALING * lora_out

    def _L1_ffn_ref(x, W_base, b_base, W_router, b_router, lora_A, lora_B):
        import jax, jax.numpy as jnp
        import numpy as np

        def sparsemax(z):
            E = z.shape[-1]
            z_sorted = -jnp.sort(-z, axis=-1)
            z_cum = jnp.cumsum(z_sorted, axis=-1)
            k = jnp.arange(1, E + 1, dtype=z.dtype)
            support = 1.0 + k * z_sorted > z_cum
            k_z = jnp.sum(support, axis=-1, keepdims=True)
            tau_sum = jnp.take_along_axis(z_cum, k_z.astype(jnp.int32) - 1, axis=-1)
            tau = (tau_sum - 1.0) / k_z.astype(z.dtype)
            return jnp.maximum(z - tau, 0.0)
        base_out = jnp.einsum('bsd,od->bso', x, W_base) + b_base
        logits = jnp.einsum('bsd,ed->bse', x, W_router) + b_router
        weights = sparsemax(logits)
        h = jnp.einsum('bsd,edr->bser', x, lora_A)
        expert_out = jnp.einsum('bser,bse,ero->bso', h, weights, lora_B)
        return base_out + expert_out
    x = x + _L0_attn_ref(_L0_cond_ref(x, L0_cond_log_dt, L0_cond_C, L0_cond_log_A_real, L0_cond_A_imag, L0_cond_D, itok_B_78_3631), L0_attn_wq, L0_attn_wkv, L0_attn_wo)
    x = x + _L0_ffn_ref(_L0_cond2_ref(x, L0_cond2_weight, L0_cond2_bias, L0_cond2_lora_A, L0_cond2_lora_B, itok_B_0_4), L0_ffn_w_gate, L0_ffn_w_up, L0_ffn_w_down)
    x = x + _L1_attn_ref(_L1_cond_ref(x, itok_B_6_15, L1_cond_base_weight, L1_cond_base_bias, L1_cond_lora_A_w, L1_cond_lora_B_w), L1_attn_bv_q, L1_attn_bv_k, L1_attn_bv_v)
    x = x + _L1_ffn_ref(_L1_cond2_ref(x, itok_B_0_7, L1_cond2_W, L1_cond2_Wr, L1_cond2_A, L1_cond2_B), L1_ffn_W_base, L1_ffn_b_base, L1_ffn_W_router, L1_ffn_b_router, L1_ffn_lora_A, L1_ffn_lora_B)
    return x

_drawn_inputs = setup_inputs


def setup_inputs(seed=0):
    import zlib

    import numpy as np

    out = dict(_drawn_inputs(seed))
    spreads = {'L0_cond_log_A_real': (-0.6931471824645996, 0.6),
     'L1_ffn_b_router': (0.0, 0.1),
     'L1_ffn_lora_B': (0.0, 0.1)}
    factors = {'L0_cond2_bias': 8.0,
     'L0_cond2_lora_A': 8.0,
     'L0_cond2_lora_B': 8.0,
     'L1_cond_base_bias': 43.305,
     'L1_attn_bv_q': 64.0,
     'L1_attn_bv_k': 64.0,
     'L1_cond2_Wr': 4.615,
     'L1_ffn_b_base': 8.0}
    for name, (base, spread) in spreads.items():
        noise = np.random.default_rng([zlib.crc32(name.encode()), seed]).standard_normal(out[name].shape)
        drawn = base * np.exp(spread * noise) if base else spread * noise
        out[name] = jnp.asarray(drawn.astype(out[name].dtype))
    for name, factor in factors.items():
        out[name] = (out[name] * factor).astype(out[name].dtype)
    return out
```

```python
from contextlib import ExitStack

import numpy as np
import concourse.bass as bass
from concourse import mybir

F32 = mybir.dt.float32
F32R = mybir.dt.float32r
I32 = mybir.dt.int32
U32 = mybir.dt.uint32
ACT = mybir.ActivationFunctionType
ALU = mybir.AluOpType
AX_X = mybir.AxisListType.X

P = 128
BATCH, SEQ, DIM = 64, 32, 512
TOK = BATCH * SEQ
KC = DIM // P
TT = 512
NT = TOK // TT
SUBS = TT // P
BPT = TT // SEQ
HEADS, DH, DQ = 32, 128, 192
GH = 2
GROUPS = HEADS // GH
GW = 3 * KC * GH * DH + GH * DIM
PIECE = GW // NT
QOFF, KOFF, VOFF, OOFF = 0, KC * GH * DH, 2 * KC * GH * DH, 3 * KC * GH * DH
NST = 64
LI, LJ = 16, 32
RROW = DIM + P
OCT, OH, OD = 8, 170, 64
HID = OCT * OH
HT = -(-HID // P)
LAB, LR = 5, 32
ADA, AR = 32, 16
NE, ER = 8, 16
BIND_HEADS = 4
SCALE0 = float(DQ) ** -0.5
SCALE1 = float(P) ** -0.5 * 4.0
NEG = -1e30
MAGIC = 12582912.0
LN2_HI, LN2_LO = 0.693359375, -2.12194440e-4
TWO_PI = (6.28125, 1.9350051879882812e-3, 3.019915978e-7)
PI_IN = 3.1415925


def octonion_table():
    s = np.zeros((8, 8, 8), np.float32)
    s[0, 0, 0] = 1.0
    for i in range(1, 8):
        s[0, i, i] = s[i, 0, i] = 1.0
        s[i, i, 0] = -1.0
    for a, b, c in [(1, 2, 3), (1, 4, 5), (1, 7, 6), (2, 4, 6), (2, 5, 7), (3, 4, 7), (3, 6, 5)]:
        for x, y, z in ((a, b, c), (b, c, a), (c, a, b)):
            s[x, y, z] = 1.0
            s[y, x, z] = -1.0
    return np.abs(s).argmax(0), s.sum(0)


def constant_table():
    p = np.arange(P)
    part = p // NST
    li = LJ * (LI - 1 - np.arange(LI))
    lj = LJ - 1 - np.arange(LJ)
    lags = np.concatenate([li, li, lj])
    quarter = np.zeros((P, 2 * LI + LJ))
    quarter[:, :LI] = (1 + part)[:, None]
    quarter[:, LI:2 * LI] = (2 + part)[:, None]
    quarter[:, 2 * LI:] = (1 - part)[:, None]
    q = p % SEQ
    j_of, sign = octonion_table()
    sign_up = np.stack([np.stack([-sign[2 * c + x // OD] for x in p]) for c in range(KC)], 1)
    unit = np.minimum(p[:, None] + P * np.arange(HT)[None], HID - 1)
    sign_down = -sign[unit // OH]
    fields = {
        "lags": np.broadcast_to(lags, (P, len(lags))),
        "turns": quarter / 4,
        "angles": quarter * (np.pi / 2),
        "feature": P * np.arange(KC)[None] + (P - 1 - p)[:, None],
        "causal_add": np.where(np.arange(SEQ)[None] <= q[:, None], 0.0, NEG),
        "causal_mul": (p[:, None] // SEQ == p[None] // SEQ) * (p[:, None] <= p[None]),
        "ident": np.eye(P),
        "ones": np.ones((P, P)),
        "labeler": (p // LR)[:, None] + np.array([[0, P // LR]]),
        "adapter": (p // AR)[:, None] + (P // AR) * np.arange(4)[None],
        "iota": np.broadcast_to(np.arange(NE), (P, NE)),
        "count": np.broadcast_to(1 + np.arange(NE), (P, NE)),
        "sign_up": sign_up.reshape(P, -1),
        "sign_down": sign_down.reshape(P, -1),
    }
    at, n = {}, 0
    for name, a in fields.items():
        at[name] = (n, n + a.shape[1])
        n += a.shape[1]
    return np.concatenate(list(fields.values()), 1).astype(np.float32), at


L1_BLOCKS = [("Wc", KC * DIM), ("Ac", KC * DIM), ("Bc", KC * DIM), ("W2", KC * DIM), ("Wf", KC * DIM),
             ("A2", KC * P), ("B2", DIM), ("Af", KC * P), ("Bf", DIM), ("R2", KC * NE), ("Rf", KC * NE)]
L1_AT, _n = {}, 0
for _name, _w in L1_BLOCKS:
    L1_AT[_name] = _n
    _n += _w
L1_COLS = _n
L1_PIECES = [(a, min(a + KC * DIM, L1_COLS)) for a in range(0, L1_COLS, KC * DIM)]
C2_COLS = KC * DIM + KC * 2 * P + DIM


def build_program(nc, t):
    _, CONST = constant_table()
    ctx = ExitStack()
    with ctx:
        def sb(stack, name, shape, dt=F32):
            return stack.enter_context(nc.sbuf_tensor(name, shape, dt))

        def sem(stack, name):
            return stack.enter_context(nc.semaphore(name))

        resid = sb(ctx, "resid", [P, KC, TOK])
        consts = sb(ctx, "consts", [P, t["consts"].shape[1]])
        psum = ctx.enter_context(nc.psum_tensor("psum", [P, 8, TT], F32))
        kernel_rows = nc.dram_tensor("kernel_rows", [SEQ, RROW], F32, kind="Internal").ap()

        def const(name):
            a, b = CONST[name]
            return consts[:, a:b]

        def mm3(pe, out, w, x, start, stop):
            pe.matmul(out, w[0], x[0], start=start, stop=False)
            pe.matmul(out, w[0], x[1], start=False, stop=False)
            return pe.matmul(out, w[1], x[0], start=False, stop=stop)

        attn = ctx.enter_context(ExitStack())
        y_hi = sb(attn, "y_hi", [P, KC, TOK], F32R)
        y_lo = sb(attn, "y_lo", [P, KC, TOK], F32R)
        wraw = sb(attn, "wraw", [P, GW])
        raw_loaded = [sem(attn, f"raw_loaded{i}") for i in range(NT)]
        s4d_and_convolution(nc, t, sb, sem, const, consts, resid, psum, kernel_rows, y_hi, y_lo, wraw, raw_loaded)
        attention(nc, t, sb, sem, const, mm3, resid, psum, y_hi, y_lo, wraw, raw_loaded)
        attn.close()
        octonion_ffn(nc, t, sb, sem, const, mm3, resid, psum)
        layer_one(nc, t, sb, sem, const, mm3, resid, psum)


def wait_apart(engine, semaphore, value, passed):
    engine.wait_ge(semaphore, value)
    engine.sem_inc(passed, 1)


def s4d_and_convolution(nc, t, sb, sem, const, consts, resid, psum, kernel_rows, y_hi, y_lo, wraw, raw_loaded):
    ctx = ExitStack()
    with ctx:
        NW = 2 * LI + LJ
        NB = 4
        RND = TT // BATCH
        prm = sb(ctx, "prm", [P, 5, SEQ])
        sk = sb(ctx, "sk", [P, 24, 2 * SEQ])
        lensi = sb(ctx, "lensi", [P, BATCH], I32)
        lens = sb(ctx, "lens", [P, BATCH])
        mask = sb(ctx, "mask", [P, KC, BATCH])
        theta = sb(ctx, "theta", [P, SEQ, NW])
        turns = sb(ctx, "turns", [P, SEQ, NW])
        mag = sb(ctx, "mag", [P, SEQ, LI + LJ])
        left = sb(ctx, "left", [P, SEQ, LI])
        right = sb(ctx, "right", [P, SEQ, LJ])
        skip = sb(ctx, "skip", [LI, SEQ * LJ])
        rows = sb(ctx, "rows", [LI, SEQ * LJ])
        hankel = sb(ctx, "hankel", [P, NB, DIM])
        ymask = sb(ctx, "ymask", [P, 2, TT])

        params_in, x_in, const_in = sem(ctx, "params_in"), sem(ctx, "x_in"), sem(ctx, "const_in")
        step = sem(ctx, "s4d_step")
        trig_ready, trig_done = sem(ctx, "trig_ready"), sem(ctx, "trig_done")
        mag_ready, mag_done = sem(ctx, "mag_ready"), sem(ctx, "mag_done")
        factors_ready, kernels_done = sem(ctx, "factors_ready"), sem(ctx, "kernels_done")
        rows_ready, rows_stored = sem(ctx, "rows_ready"), sem(ctx, "rows_stored")
        hankel_in = [sem(ctx, f"hankel_in{i}") for i in range(NB)]
        hankel_free = sem(ctx, "hankel_free")
        mask_ready = sem(ctx, "mask_ready")
        conv_done, bank_free = sem(ctx, "conv_done"), sem(ctx, "bank_free")
        masked, y_hi_done, ymask_free = sem(ctx, "masked"), sem(ctx, "y_hi_done"), sem(ctx, "ymask_free")
        overlapping = bass.AP(tensor=kernel_rows.tensor, offset=0, ap=[[RROW, SEQ], [1, P], [1, DIM]])
        block = ctx.enter_context(nc.Block())

        @block.sync
        def _(sp):
            sp.dma_start(prm[:], t["s4d"]).then_inc(params_in, 16)
            sp.dma_start(consts[:], t["consts"]).then_inc(const_in, 16)
            sp.dma_start(skip[:], t["skip"]).then_inc(params_in, 16)
            sp.dma_start(lensi[:], t["lengths"]).then_inc(params_in, 16)
            sp.dma_start(kernel_rows[:, DIM:RROW], t["zeros"]).then_inc(rows_stored, 16)
            for c in range(KC):
                sp.dma_start(resid[:, c, :], t["xT"][c * P:(c + 1) * P, :]).then_inc(x_in, 16)
            for p in range(NT):
                sp.dma_start(wraw[:, p * PIECE:(p + 1) * PIECE],
                             t["attn_w"][0, :, p * PIECE:(p + 1) * PIECE]).then_inc(raw_loaded[p], 16)
            sp.wait_ge(rows_ready, 1)
            sp.dma_start(kernel_rows[:, 0:DIM].rearrange("h (i j) -> i h j", i=LI),
                         rows[:].rearrange("i (h j) -> i h j", h=SEQ)).then_inc(rows_stored, 16)
            sp.wait_ge(rows_stored, 32)
            with sp.Fori(0, SEQ // NB) as it:
                for b in range(NB):
                    sp.wait_ge(hankel_free, it * NB + (b + 1))
                    h = it * NB + b
                    src = overlapping[bass.ds(h, 1), :, :].rearrange("h p n -> (h p) n")
                    sp.dma_start(hankel[:, b, :], src).then_inc(hankel_in[b], 16)

        @block.vector
        def _(dve):
            n = [0]

            def then(ins):
                n[0] += 1
                ins.then_inc(step, 1)
                dve.wait_ge(step, n[0])

            def tt(out, a, b, op):
                then(dve.tensor_tensor(out, a, b, op))

            def ts(out, a, s1, s2, op0, op1=None):
                if op1 is None:
                    then(dve.tensor_scalar(out, a, s1, None, op0))
                else:
                    then(dve.tensor_scalar(out, a, s1, s2, op0, op1))

            def stt(out, a, s, b, op0, op1):
                then(dve.scalar_tensor_tensor(out=out, in0=a, scalar=s, in1=b, op0=op0, op1=op1))

            def expm1(x, em1, two_k, w, t0, t1, t2):
                ts(t0, x, 1.4426950408889634, MAGIC, ALU.mult, ALU.add)
                ts(t0, t0, MAGIC, None, ALU.subtract)
                stt(t1, t0, -LN2_HI, x, ALU.mult, ALU.add)
                stt(t1, t0, -LN2_LO, t1, ALU.mult, ALU.add)
                ts(t0, t0, 127.0, 8388608.0, ALU.add, ALU.mult)
                then(dve.tensor_copy(two_k.bitcast(I32), t0))
                ts(t2, t1, 1 / 40320.0, 1 / 5040.0, ALU.mult, ALU.add)
                for c in (1 / 720.0, 1 / 120.0, 1 / 24.0, 1 / 6.0, 0.5, 1.0):
                    tt(t2, t2, t1, ALU.mult)
                    ts(t2, t2, c, None, ALU.add)
                tt(t2, t2, t1, ALU.mult)
                tt(t2, t2, two_k, ALU.mult)
                ts(t0, two_k, 1.0, None, ALU.subtract)
                tt(em1, t2, t0, ALU.add)

            dve.wait_ge(params_in, 48)
            v = [sk[:, i, 0:SEQ] for i in range(24)]
            wide = [sk[:, i, :] for i in range(20, 24)]
            logs = prm[:, 0:2, :].rearrange("p a h -> p (a h)")
            expm1(logs, wide[3], wide[2], 2 * SEQ, wide[0], wide[1], sk[:, 19, :])
            ts(wide[3], wide[3], 1.0, None, ALU.add)
            dt, ar = sk[:, 23, 0:SEQ], sk[:, 23, SEQ:2 * SEQ]
            ai, cr, ci = prm[:, 2, :], prm[:, 3, :], prm[:, 4, :]
            da, db = v[0], v[1]
            stt(da, ar, -1.0, dt, ALU.mult, ALU.mult)
            tt(db, ai, dt, ALU.mult)

            def reduce_angle(out, x, k, c_ap=None):
                for part in TWO_PI:
                    stt(out, k, -part, x if part == TWO_PI[0] else out, ALU.mult, ALU.add)

            dve.wait_ge(const_in, 16)
            tt(theta[:], db.unsqueeze(2).broadcast_to([P, SEQ, NW]),
               const("lags").unsqueeze(1).broadcast_to([P, SEQ, NW]), ALU.mult)
            then(dve.tensor_tensor(mag[:], da.unsqueeze(2).broadcast_to([P, SEQ, LI + LJ]),
                                   const("lags")[:, LI:].unsqueeze(1).broadcast_to([P, SEQ, LI + LJ]), ALU.mult))
            dve.sem_inc(mag_ready, 1)
            stt(turns[:], theta[:], 0.15915494309189535,
                const("turns").unsqueeze(1).broadcast_to([P, SEQ, NW]), ALU.mult, ALU.add)
            ts(turns[:], turns[:], MAGIC, MAGIC, ALU.add, ALU.subtract)
            reduce_angle(theta[:], theta[:], turns[:])
            tt(theta[:], theta[:], const("angles").unsqueeze(1).broadcast_to([P, SEQ, NW]), ALU.add)
            ts(theta[:], theta[:], PI_IN, -PI_IN, ALU.min, ALU.max)
            ang, kk = sk[:, 2, :], sk[:, 3, :]
            then(dve.tensor_copy(ang[:, 0:SEQ], db))
            ts(ang[:, SEQ:], db, 0.5, None, ALU.mult)
            ts(kk, ang, 0.15915494309189535, MAGIC, ALU.mult, ALU.add)
            ts(kk, kk, MAGIC, None, ALU.subtract)
            reduce_angle(ang, ang, kk)
            ts(ang, ang, PI_IN, -PI_IN, ALU.min, ALU.max)
            dve.sem_inc(trig_ready, 1)
            em1 = v[4]
            expm1(da, em1, v[5], SEQ, v[6], v[7], v[8])
            dve.wait_ge(trig_done, 2)
            s1, s2 = sk[:, 9, 0:SEQ], sk[:, 9, SEQ:]
            vers, e1r, e1i, cosb = v[10], v[11], v[12], v[13]
            tt(vers, s2, s2, ALU.mult)
            ts(cosb, vers, -2.0, 1.0, ALU.mult, ALU.add)
            tt(e1r, em1, cosb, ALU.mult)
            stt(e1r, vers, -2.0, e1r, ALU.mult, ALU.add)
            stt(e1i, em1, 1.0, s1, ALU.add, ALU.mult)
            ur, ui, a, b, inv = v[14], v[15], v[16], v[17], v[18]
            tt(ur, cr, e1r, ALU.mult)
            tt(a, ci, e1i, ALU.mult)
            tt(ur, ur, a, ALU.subtract)
            tt(ui, cr, e1i, ALU.mult)
            tt(a, ci, e1r, ALU.mult)
            tt(ui, ui, a, ALU.add)
            tt(a, ar, ar, ALU.mult)
            tt(b, ai, ai, ALU.mult)
            tt(a, a, b, ALU.add)
            then(dve.reciprocal(inv, a))
            ctr, cti = v[19], v[20]
            tt(a, ui, ai, ALU.mult)
            tt(b, ur, ar, ALU.mult)
            tt(a, a, b, ALU.subtract)
            stt(ctr, a, 2.0, inv, ALU.mult, ALU.mult)
            tt(a, ur, ai, ALU.mult)
            tt(b, ui, ar, ALU.mult)
            tt(a, a, b, ALU.add)
            stt(cti, a, -2.0, inv, ALU.mult, ALU.mult)
            tt(left[:], theta[:, :, 0:LI], ctr.unsqueeze(2).broadcast_to([P, SEQ, LI]), ALU.mult)
            tt(turns[:, :, 0:LI], theta[:, :, LI:2 * LI], cti.unsqueeze(2).broadcast_to([P, SEQ, LI]), ALU.mult)
            tt(left[:], left[:], turns[:, :, 0:LI], ALU.add)
            dve.wait_ge(mag_done, 1)
            tt(left[:], left[:], mag[:, :, 0:LI], ALU.mult)
            tt(right[:], theta[:, :, 2 * LI:], mag[:, :, LI:], ALU.mult)
            dve.sem_inc(factors_ready, 1)
            then(dve.tensor_copy(lens[:], lensi[:]))
            for c in range(KC):
                ts(mask[:, c, :], lens[:], const("feature")[:, c:c + 1], None, ALU.is_gt)
            dve.wait_ge(kernels_done, 1)
            tt(rows[:], psum[0:LI, 0:2, :].rearrange("p b n -> p (b n)"), skip[:], ALU.add)
            dve.sem_inc(rows_ready, 1)
            dve.sem_inc(bank_free, 8)
            with dve.Fori(0, SEQ // (2 * RND)) as it:
                for r in range(2):
                    for L in range(KC):
                        k = r * KC + L
                        dve.wait_ge(conv_done, it * 8 + (k + 1))
                        dve.wait_ge(ymask_free, it * 8 + (k + 1))
                        dve.tensor_tensor(
                            ymask[:, k % 2, :].rearrange("p (s b) -> p s b", b=BATCH),
                            psum[:, k, :].rearrange("p (s b) -> p s b", b=BATCH),
                            mask[:, L, :].unsqueeze(1).broadcast_to([P, RND, BATCH]),
                            ALU.mult).then_inc(masked, 1)
                        dve.wait_ge(masked, it * 8 + (k + 1))
                        dve.sem_inc(bank_free, 1)

        @block.scalar
        def _(act):
            act.wait_ge(mag_ready, 1)
            act.activation(mag[:], mag[:], ACT.Exp).then_inc(mag_done, 1)
            act.wait_ge(trig_ready, 1)
            act.activation(theta[:], theta[:], ACT.Sin).then_inc(trig_done, 1)
            act.activation(sk[:, 9, :], sk[:, 2, :], ACT.Sin).then_inc(trig_done, 1)
            with act.Fori(0, SEQ // (2 * RND)) as it:
                for r in range(2):
                    for L in range(KC):
                        k = r * KC + L
                        act.wait_ge(masked, it * 8 + (k + 1))
                        dst = y_hi[:, L, :].rearrange("p (b s) -> p s b", s=SEQ)[:, bass.ds(it * 16 + r * RND, RND), :]
                        act.activation(dst, ymask[:, k % 2, :].rearrange("p (s b) -> p s b", b=BATCH),
                                       ACT.Copy).then_inc(y_hi_done, 1)

        @block.gpsimd
        def _(pool):
            pool.sem_inc(ymask_free, 2)
            with pool.Fori(0, SEQ // (2 * RND)) as it:
                for r in range(2):
                    for L in range(KC):
                        k = r * KC + L
                        pool.wait_ge(y_hi_done, it * 8 + (k + 1))
                        where = bass.ds(it * 16 + r * RND, RND)
                        hi = y_hi[:, L, :].bitcast(F32).rearrange("p (b s) -> p s b", s=SEQ)[:, where, :]
                        lo = y_lo[:, L, :].rearrange("p (b s) -> p s b", s=SEQ)[:, where, :]
                        pool.tensor_tensor(lo, ymask[:, k % 2, :].rearrange("p (s b) -> p s b", b=BATCH),
                                           hi, ALU.subtract).then_inc(ymask_free, 1)

        @block.tensor
        def _(pe):
            pe.sem_inc(hankel_free, NB)
            pe.wait_ge(factors_ready, 1)
            for h in range(SEQ):
                mm = pe.matmul(psum[0:LI, h // 16, (h % 16) * LJ:(h % 16 + 1) * LJ],
                               left[:, h, :], right[:, h, :], start=True, stop=True)
            mm.then_inc(kernels_done, 1)
            pe.wait_ge(x_in, 16 * KC)
            with pe.Fori(0, SEQ // (2 * RND)) as it:
                for r in range(2):
                    for L in range(KC):
                        pe.wait_ge(bank_free, it * 8 + (r * KC + L + 1))
                    for s in range(RND):
                        h = r * RND + s
                        pe.wait_ge(hankel_in[h % NB], it * (16 * 2 * RND // NB) + 16 * (h // NB + 1))
                        for L in range(KC):
                            for m in range(L + 1):
                                w0 = (KC - 1 - (L - m)) * P
                                u = resid[:, m, :].rearrange("p (b s) -> p s b", s=SEQ)[:, bass.ds(it * 16 + h, 1), :]
                                mm = pe.matmul(psum[:, r * KC + L, s * BATCH:(s + 1) * BATCH],
                                               hankel[:, h % NB, w0:w0 + P], u.rearrange("p a b -> p (a b)"),
                                               start=(m == 0), stop=(m == L))
                            if s == RND - 1:
                                mm.then_inc(conv_done, 1)
                        if s < RND - 1:
                            mm.then_inc(hankel_free, 1)
                        else:
                            pe.drain().then_inc(hankel_free, 1)


def attention(nc, t, sb, sem, const, mm3, resid, psum, y_hi, y_lo, wraw, raw_loaded):
    STEPS = 2 * NT
    TURNS = GROUPS // 2
    NPJ, NTL = 6, 6
    ctx = ExitStack()
    with ctx:
        w_hi = [sb(ctx, f"w_hi{i}", [P, GW], F32R) for i in range(2)]
        w_lo = [sb(ctx, f"w_lo{i}", [P, GW], F32R) for i in range(2)]
        qT = sb(ctx, "qT", [P, GH, TT])
        kT = sb(ctx, "kT", [P, GH, TT])
        v_tok = sb(ctx, "v_tok", [P, SUBS, GH * DH])
        NBK = GH * SUBS
        sc = sb(ctx, "sc", [P, NBK, SEQ])
        ex = sb(ctx, "ex", [P, NBK, SEQ])
        stat = sb(ctx, "stat", [P, 3, NBK])
        probT = sb(ctx, "probT", [P, NBK, P])
        o_hi = sb(ctx, "o_hi", [P, GH, TT], F32R)
        o_lo = sb(ctx, "o_lo", [P, GH, TT], F32R)

        hi_split, lo_split = sem(ctx, "hi_split"), sem(ctx, "lo_split")
        cleared = sem(ctx, "cleared")
        proj_done, proj_free = sem(ctx, "proj_done"), sem(ctx, "proj_free")
        scores_done = sem(ctx, "scores_done")
        shifted, exp_done = sem(ctx, "shifted"), sem(ctx, "exp_done")
        prob_ready, soft_step = sem(ctx, "prob_ready"), sem(ctx, "soft_step")
        pv_done, out_done = sem(ctx, "pv_done"), sem(ctx, "out_done")
        o_hi_done, tail_free = sem(ctx, "o_hi_done"), sem(ctx, "tail_free")
        block = ctx.enter_context(nc.Block())

        def weight(par, off, n=P):
            return w_hi[par][:, off:off + n], w_lo[par][:, off:off + n]

        @block.sync
        def _(sp):
            with sp.Fori(1, GROUPS) as g:
                for p in range(NT):
                    sp.wait_ge(lo_split, g * NT + (p + 1 - NT))
                    sp.dma_start(wraw[:, p * PIECE:(p + 1) * PIECE],
                                 t["attn_w"][bass.ds(g, 1), :, p * PIECE:(p + 1) * PIECE]
                                 .rearrange("g p n -> (g p) n")).then_inc(raw_loaded[p], 16)

        def split_hi(act, group, par, p):
            act.wait_ge(raw_loaded[p], group * 16 + 16)
            act.activation(w_hi[par][:, p * PIECE:(p + 1) * PIECE], wraw[:, p * PIECE:(p + 1) * PIECE],
                           ACT.Copy).then_inc(hi_split, 1)

        @block.gpsimd
        def _(pool):
            pool.memset(probT[:], 0.0).then_inc(cleared, 1)
            pool.memset(v_tok[:], 0.0).then_inc(cleared, 1)
            pool.memset(w_hi[1][:, OOFF:].bitcast(F32), 0.0).then_inc(cleared, 1)
            pool.memset(w_lo[1][:, OOFF:].bitcast(F32), 0.0).then_inc(cleared, 1)

            def split_lo(group, par, p):
                pool.wait_ge(hi_split, group * NT + (p + 1))
                cols = slice(p * PIECE, (p + 1) * PIECE)
                pool.tensor_tensor(w_lo[par][:, cols], wraw[:, cols], w_hi[par][:, cols].bitcast(F32),
                                   ALU.subtract).then_inc(lo_split, 1)

            for p in range(NT):
                split_lo(0, 0, p)
            with pool.Fori(0, TURNS - 1) as it:
                for j in range(STEPS):
                    split_lo(it * 2 + (j // NT + 1), (j // NT + 1) % 2, j % NT)
            for j in range(NT):
                split_lo(GROUPS - 1, 1, j)

        @block.scalar
        def _(act):
            def evac_proj(S, e, dst):
                bank = e % 3
                act.wait_ge(proj_done, S * NPJ + (e + 1))
                act.activation(dst, psum[:, bank, :], ACT.Copy).then_inc(proj_free, 1)

            def o_high(S, a):
                act.wait_ge(pv_done, S * GH + (a + 1))
                act.activation(o_hi[:, a, :], psum[:, 5 + a, :], ACT.Copy).then_inc(o_hi_done, 1)

            def steps(it, steps_of, last):
                for j in steps_of:
                    S = it * STEPS + j
                    evac_proj(S, 0, qT[:, 0, :])
                    evac_proj(S, 1, kT[:, 0, :])
                    o_high(S, 0)
                    o_high(S, 1)
                    evac_proj(S, 2, qT[:, 1, :])
                    if not (last and j >= NT):
                        split_hi(act, it * 2 + (j // NT + 1), (j // NT + 1) % 2, j % NT)
                    evac_proj(S, 3, kT[:, 1, :])
                    evac_proj(S, 4, v_tok[:, 0:2, :].rearrange("p s n -> p (s n)"))
                    act.wait_ge(shifted, S + 1)
                    act.activation(ex[:], sc[:], ACT.Exp).then_inc(exp_done, 1)
                    evac_proj(S, 5, v_tok[:, 2:4, :].rearrange("p s n -> p (s n)"))

            for p in range(NT):
                split_hi(act, 0, 0, p)
            act.sem_inc(proj_free, 3)
            act.wait_ge(cleared, 2)
            with act.Fori(0, TURNS - 1) as it:
                steps(it, range(STEPS), False)
            steps(TURNS - 1, range(STEPS), True)
            o_high(TURNS * STEPS, 0)
            o_high(TURNS * STEPS, 1)

        @block.vector
        def _(dve):
            NSOFT = 5

            def tail(S, tile):
                for a in range(GH):
                    dve.wait_ge(o_hi_done, S * GH + (a + 1))
                    dve.tensor_tensor(o_lo[:, a, :], psum[:, 5 + a, :], o_hi[:, a, :].bitcast(F32),
                                      ALU.subtract).then_inc(tail_free, 1)
                for m in range(KC):
                    bank = 5 + (GH + m) % 3
                    dve.wait_ge(out_done, S * KC + (m + 1))
                    part = resid[:, m, tile * TT:(tile + 1) * TT]
                    dve.tensor_tensor(part, psum[:, bank, :], part, ALU.add).then_inc(tail_free, 1)

            def softmax(S):
                n = [0]

                def then(ins):
                    n[0] += 1
                    ins.then_inc(soft_step, 1)
                    dve.wait_ge(soft_step, S * NSOFT + n[0])

                dve.wait_ge(scores_done, S + 1)
                blocks = psum[:, 3:5, :].rearrange("p a (s n) -> p (a s) n", n=P)
                for b in range(P // SEQ):
                    q = slice(b * SEQ, (b + 1) * SEQ)
                    ins = dve.scalar_tensor_tensor(
                        out=sc[q, :, :], in0=blocks[q, :, b * SEQ:(b + 1) * SEQ], scalar=SCALE0,
                        in1=const("causal_add")[q, :].unsqueeze(1).broadcast_to([SEQ, NBK, SEQ]),
                        op0=ALU.mult, op1=ALU.add)
                then(ins)
                top, total, inv = stat[:, 0, :], stat[:, 1, :], stat[:, 2, :]
                then(dve.tensor_reduce(top, sc[:], AX_X, ALU.max))
                dve.tensor_tensor(sc[:], sc[:], top.unsqueeze(2).broadcast_to([P, NBK, SEQ]),
                                  ALU.subtract).then_inc(shifted, 1)
                dve.wait_ge(exp_done, S + 1)
                then(dve.tensor_reduce(total, ex[:], AX_X, ALU.add))
                then(dve.reciprocal(inv, total))
                then(dve.tensor_tensor(ex[:], ex[:], inv.unsqueeze(2).broadcast_to([P, NBK, SEQ]), ALU.mult))
                for b in range(P // SEQ):
                    q = slice(b * SEQ, (b + 1) * SEQ)
                    ins = dve.transpose(probT[q, :, b * SEQ:(b + 1) * SEQ], ex[q, :, :])
                ins.then_inc(prob_ready, 1)
                assert n[0] == NSOFT

            dve.sem_inc(tail_free, 3)
            dve.wait_ge(cleared, 1)
            dve.sem_inc(prob_ready, 1)
            with dve.Fori(0, TURNS) as it:
                for j in range(STEPS):
                    tail(it * STEPS + j, (j - 1) % NT)
                    softmax(it * STEPS + j)
            tail(TURNS * STEPS, NT - 1)

        @block.tensor
        def _(pe):
            def proj_bank(S, e):
                pe.wait_ge(proj_free, S * NPJ + (e + 1))
                return psum[:, e % 3, :]

            def project(S, e, par, off, tile):
                bank = proj_bank(S, e)
                cols = slice(tile * TT, (tile + 1) * TT)
                for c in range(KC):
                    mm = mm3(pe, bank, weight(par, off + c * GH * DH), (y_hi[:, c, cols], y_lo[:, c, cols]),
                             c == 0, c == KC - 1)
                mm.then_inc(proj_done, 1)

            def values(S, e, par, tile, half):
                bank = proj_bank(S, e)
                for i in range(2):
                    at = tile * TT + (2 * half + i) * P
                    for c in range(KC):
                        out = bank[:, i * GH * DH:(i + 1) * GH * DH]
                        mm = mm3(pe, out, (y_hi[:, c, at:at + P], y_lo[:, c, at:at + P]),
                                 weight(par, VOFF + c * GH * DH, GH * DH), c == 0, c == KC - 1)
                mm.then_inc(proj_done, 1)

            def scores(S, a, e):
                pe.wait_ge(proj_free, S * NPJ + (3 + e + 1))
                for i in range(SUBS):
                    tok = slice(i * P, (i + 1) * P)
                    mm = pe.matmul(psum[:, 3 + a, tok], qT[:, a, tok], kT[:, a, tok], start=True, stop=True)
                if a == GH - 1:
                    mm.then_inc(scores_done, 1)

            def prob_times_v(S):
                for a in range(GH):
                    pe.wait_ge(tail_free, S * NTL + (a + 1))
                    if a == 0:
                        pe.wait_ge(prob_ready, S + 1)
                        pe.wait_ge(proj_free, S * NPJ + 3)
                    for i in range(SUBS):
                        mm = pe.matmul(psum[:, 5 + a, i * P:(i + 1) * P], v_tok[:, i, a * DH:(a + 1) * DH],
                                       probT[:, a * SUBS + i, :], start=True, stop=True)
                    mm.then_inc(pv_done, 1)

            def output(S, par):
                pe.wait_ge(tail_free, S * NTL + (3 + GH))
                for m in range(KC):
                    pe.wait_ge(tail_free, S * NTL + (GH + m + 1))
                    for a in range(GH):
                        mm = mm3(pe, psum[:, 5 + (GH + m) % 3, :], weight(par, OOFF + a * DIM + m * P),
                                 (o_hi[:, a, :], o_lo[:, a, :]), a == 0, a == GH - 1)
                    mm.then_inc(out_done, 1)

            pe.wait_ge(cleared, 4)
            with pe.Fori(0, TURNS) as it:
                for j in range(STEPS):
                    S, par, tile = it * STEPS + j, j // NT, j % NT
                    if tile == 0:
                        pe.wait_ge(lo_split, it * (2 * NT) + (par + 1) * NT)
                    project(S, 0, par, QOFF, tile)
                    project(S, 1, par, KOFF, tile)
                    prob_times_v(S)
                    project(S, 2, par, QOFF + DH, tile)
                    scores(S, 0, 1)
                    output(S, ((j - 1) // NT) % 2)
                    project(S, 3, par, KOFF + DH, tile)
                    values(S, 4, par, tile, 0)
                    scores(S, 1, 3)
                    values(S, 5, par, tile, 1)
            prob_times_v(TURNS * STEPS)
            output(TURNS * STEPS, 1)


def octonion_ffn(nc, t, sb, sem, const, mm3, resid, psum):
    ctx = ExitStack()
    with ctx:
        c2_hi, c2_lo = (sb(ctx, f"c2_{x}", [P, C2_COLS], F32R) for x in ("hi", "lo"))
        up = sb(ctx, "up", [P, 2, KC, HID], F32R)
        down = sb(ctx, "down", [P, HT, DIM], F32R)
        small = sb(ctx, "small", [P, 32])
        label_i = sb(ctx, "label_i", [P, BATCH], I32)
        label_mask = sb(ctx, "label_mask", [P, 2, BATCH])
        prep = ctx.enter_context(ExitStack())

        weights_in, c2_hi_done, c2_ready = sem(ctx, "weights_in"), sem(ctx, "c2_hi_done"), sem(ctx, "c2_ready")
        base_in = sem(ctx, "base_in")
        tern_in = [sem(ctx, f"tern_in{i}") for i in range(2)]
        sums_ready, sums_done, scale_ready = (sem(ctx, n) for n in ("sums_ready", "sums_done", "scale_ready"))
        tern_step, signed = sem(ctx, "tern_step"), sem(ctx, "signed")
        x_hi_done, x_ready = sem(ctx, "x_hi_done"), sem(ctx, "x_ready")
        rank_done, masked, rank_hi_done, rank_ready = (sem(ctx, n) for n in ("rank_done", "masked", "rank_hi_done", "rank_ready"))
        z_done, z_hi_done, z_ready = (sem(ctx, n) for n in ("z_done", "z_hi_done", "z_ready"))
        up_done, gate_done, hid_done, h_hi_done, h_ready = (
            sem(ctx, n) for n in ("up_done", "gate_done", "hid_done", "h_hi_done", "h_ready"))
        down_done, down_free = sem(ctx, "down_done"), sem(ctx, "down_free")
        A_OFF, B_OFF = KC * DIM, KC * DIM + KC * 2 * P
        TC = [(w, c) for c in range(KC) for w in range(2)]
        TD = [(a, min(a + 2, HT)) for a in range(0, HT, 2)]

        def c2(off, n=P):
            return c2_hi[:, off:off + n], c2_lo[:, off:off + n]

        c2_raw = sb(prep, "c2_raw", [P, C2_COLS])
        base = sb(prep, "base", [P, 3, OCT * OH * OD // P])
        raw = sb(prep, "raw", [P, 2, HID])
        above = sb(prep, "above", [P, HID])
        tern = sb(prep, "tern", [P, 2, HID])
        with nc.Block() as block:
            @block.sync
            def _(sp):
                sp.dma_start(small[:, 0:4], t["c2_bias"]).then_inc(base_in, 16)
                sp.dma_start(base[:], t["oct_base"]).then_inc(base_in, 16)
                sp.dma_start(label_i[:], t["labels"]).then_inc(base_in, 16)
                sp.dma_start(c2_raw[:], t["c2_w"]).then_inc(weights_in, 16)
                for n, (w, c) in enumerate(TC):
                    if n >= 2:
                        sp.wait_ge(signed, n - 1)
                    sp.dma_start(raw[:, n % 2, :], t["oct_up"][w, c * P:(c + 1) * P, :]).then_inc(tern_in[n % 2], 16)
                for n, (a, b) in enumerate(TD, len(TC)):
                    sp.wait_ge(signed, n - 1)
                    sp.dma_start(raw[:, n % 2, 0:(b - a) * DIM].rearrange("p (a n) -> p a n", n=DIM),
                                 t["oct_down"][a * P:b * P, :].rearrange("(a p) n -> p a n", p=P)
                                 ).then_inc(tern_in[n % 2], 16)

            @block.scalar
            def _(act):
                act.wait_ge(weights_in, 16)
                act.activation(c2_hi[:], c2_raw[:], ACT.Copy).then_inc(c2_hi_done, 1)

            @block.tensor
            def _(pe):
                pe.wait_ge(sums_ready, 1)
                pe.matmul(psum[:, 0, 0:3], const("ones"), small[:, 4:7],
                          start=True, stop=True).then_inc(sums_done, 1)

            @block.vector
            def _(dve):
                n = [0]

                def then(ins):
                    n[0] += 1
                    ins.then_inc(tern_step, 1)
                    dve.wait_ge(tern_step, n[0])

                dve.wait_ge(base_in, 48)
                then(dve.tensor_reduce(small[:, 4:7], base[:], AX_X, ALU.add, apply_absolute_value=True))
                dve.sem_inc(sums_ready, 1)
                dve.wait_ge(sums_done, 1)
                count = float(OCT * OH * OD)
                then(dve.tensor_scalar(small[:, 10:13], psum[:, 0, 0:3], 1.0 / count, None, ALU.mult))
                then(dve.tensor_scalar(small[:, 13:16], small[:, 10:13], 0.5, None, ALU.mult))
                then(dve.tensor_scalar(small[:, 16:19], small[:, 10:13], -0.5, None, ALU.mult))
                then(dve.tensor_copy(label_mask[:, 0, :], label_i[:]))
                for k in (1, 0):
                    then(dve.tensor_scalar(label_mask[:, k, :], label_mask[:, 0, :], const("labeler")[:, k:k + 1],
                                           0.5, ALU.is_equal, ALU.mult))
                for k, (w, width) in enumerate([(w, HID) for w, _ in TC] + [(2, (b - a) * DIM) for a, b in TD]):
                    dve.wait_ge(tern_in[k % 2], 16 * (k // 2 + 1))
                    src = raw[:, k % 2, 0:width]
                    then(dve.tensor_scalar(above[:, 0:width], src, small[:, 13 + w:14 + w], None, ALU.is_gt))
                    if k >= 2:
                        dve.wait_ge(signed, k - 1)
                    then(dve.scalar_tensor_tensor(out=tern[:, k % 2, 0:width], in0=src, scalar=small[:, 16 + w:17 + w],
                                                  in1=above[:, 0:width], op0=ALU.is_lt, op1=ALU.subtract))
                    dve.sem_inc(scale_ready, 1)

            @block.gpsimd
            def _(pool):
                pool.wait_ge(c2_hi_done, 1)
                pool.tensor_tensor(c2_lo[:], c2_raw[:], c2_hi[:].bitcast(F32), ALU.subtract).then_inc(c2_ready, 1)
                for k, (w, c) in enumerate(TC):
                    pool.wait_ge(scale_ready, k + 1)
                    sign = const("sign_up")[:, c * OCT:(c + 1) * OCT].unsqueeze(2).broadcast_to([P, OCT, OH])
                    pool.tensor_tensor(up[:, w, c, :].rearrange("p (k o) -> p k o", o=OH),
                                       tern[:, k % 2, :].rearrange("p (k o) -> p k o", o=OH), sign,
                                       ALU.mult).then_inc(signed, 1)
                for k, (a, b) in enumerate(TD, len(TC)):
                    pool.wait_ge(scale_ready, k + 1)
                    sign = const("sign_down")[:, a * OCT:b * OCT].unsqueeze(2).broadcast_to([P, (b - a) * OCT, OD])
                    pool.tensor_tensor(down[:, a:b, :].rearrange("p a (k o) -> p (a k) o", o=OD),
                                       tern[:, k % 2, 0:(b - a) * DIM].rearrange("p (k o) -> p k o", o=OD), sign,
                                       ALU.mult).then_inc(signed, 1)
        prep.close()
        x_hi, x_lo, z_hi, z_lo = (sb(ctx, n, [P, KC, TT], F32R) for n in ("x_hi", "x_lo", "z_hi", "z_lo"))
        rank = sb(ctx, "rank", [P, 2, TT])
        rank_hi, rank_lo = sb(ctx, "rank_hi", [P, 2, TT], F32R), sb(ctx, "rank_lo", [P, 2, TT], F32R)
        gate = sb(ctx, "gate", [P, 2, TT])
        hid = sb(ctx, "hid", [P, 2, TT])
        h_hi, h_lo = sb(ctx, "h_hi", [P, 2, TT], F32R), sb(ctx, "h_lo", [P, 2, TT], F32R)

        s_gate, s_up, s_down = small[:, 10:11], small[:, 11:12], small[:, 12:13]
        with nc.Block() as block:
            @block.scalar
            def _(act):
                with act.Fori(0, NT) as tile:
                    for c in range(KC):
                        act.activation(x_hi[:, c, :], resid[:, c, bass.ds(tile * TT, TT)], ACT.Copy).then_inc(x_hi_done, 1)
                    for k in range(2):
                        act.wait_ge(masked, tile * 2 + (k + 1))
                        act.activation(rank_hi[:, k, :], rank[:, k, :], ACT.Copy).then_inc(rank_hi_done, 1)
                    for m in range(KC):
                        act.wait_ge(z_done, tile * KC + (m + 1))
                        act.activation(z_hi[:, m, :], psum[:, 4 + m, :], ACT.Identity, bias=small[:, m:m + 1]).then_inc(z_hi_done, 1)
                    for h in range(HT):
                        r = min(P, HID - h * P)
                        act.wait_ge(up_done, tile * HT + (h + 1))
                        act.activation(gate[0:r, h % 2, :], psum[0:r, 2 * (h % 2), :], ACT.Silu,
                                       scale=s_gate[0:r, :]).then_inc(gate_done, 1)
                        act.wait_ge(hid_done, tile * HT + (h + 1))
                        act.activation(h_hi[0:r, h % 2, :], hid[0:r, h % 2, :], ACT.Copy).then_inc(h_hi_done, 1)

            @block.vector
            def _(dve):
                dve.sem_inc(down_free, KC)
                with dve.Fori(0, NT) as tile:
                    for c in range(KC):
                        dve.wait_ge(x_hi_done, tile * KC + (c + 1))
                        dve.tensor_tensor(x_lo[:, c, :], resid[:, c, bass.ds(tile * TT, TT)],
                                          x_hi[:, c, :].bitcast(F32), ALU.subtract).then_inc(x_ready, 1)
                    for k in range(2):
                        dve.wait_ge(rank_done, tile * 2 + (k + 1))
                        own = label_mask[:, k, bass.ds(tile * BPT, BPT)].unsqueeze(2).broadcast_to([P, BPT, SEQ])
                        dve.tensor_tensor(rank[:, k, :].rearrange("p (b s) -> p b s", s=SEQ),
                                          psum[:, k, :].rearrange("p (b s) -> p b s", s=SEQ), own,
                                          ALU.mult).then_inc(masked, 1)
                        dve.wait_ge(rank_hi_done, tile * 2 + (k + 1))
                        dve.tensor_tensor(rank_lo[:, k, :], rank[:, k, :], rank_hi[:, k, :].bitcast(F32),
                                          ALU.subtract).then_inc(rank_ready, 1)
                    for m in range(KC):
                        dve.wait_ge(z_hi_done, tile * KC + (m + 1))
                        dve.scalar_tensor_tensor(out=z_lo[:, m, :], in0=psum[:, 4 + m, :], scalar=small[:, m:m + 1],
                                                 in1=z_hi[:, m, :].bitcast(F32), op0=ALU.add,
                                                 op1=ALU.subtract).then_inc(z_ready, 1)
                    for h in range(HT):
                        r = min(P, HID - h * P)
                        dve.wait_ge(gate_done, tile * HT + (h + 1))
                        dve.scalar_tensor_tensor(out=hid[0:r, h % 2, :], in0=psum[0:r, 2 * (h % 2) + 1, :],
                                                 scalar=s_up[0:r, :], in1=gate[0:r, h % 2, :],
                                                 op0=ALU.mult, op1=ALU.mult).then_inc(hid_done, 1)
                        dve.wait_ge(h_hi_done, tile * HT + (h + 1))
                        dve.tensor_tensor(h_lo[0:r, h % 2, :], hid[0:r, h % 2, :], h_hi[0:r, h % 2, :].bitcast(F32),
                                          ALU.subtract).then_inc(h_ready, 1)
                    for m in range(KC):
                        dve.wait_ge(down_done, tile + 1)
                        part = resid[:, m, bass.ds(tile * TT, TT)]
                        dve.scalar_tensor_tensor(out=part, in0=psum[:, 4 + m, :], scalar=s_down, in1=part,
                                                 op0=ALU.mult, op1=ALU.add).then_inc(down_free, 1)

            @block.tensor
            def _(pe):
                with pe.Fori(0, NT) as tile:
                    for c in range(KC):
                        pe.wait_ge(x_ready, tile * KC + (c + 1))
                        x = x_hi[:, c, :], x_lo[:, c, :]
                        for k in range(2):
                            mm = mm3(pe, psum[:, k, :], c2(A_OFF + c * 2 * P + k * P), x, c == 0, c == KC - 1)
                            if c == KC - 1:
                                mm.then_inc(rank_done, 1)
                    for c in range(KC):
                        x = x_hi[:, c, :], x_lo[:, c, :]
                        for m in range(KC):
                            if c == 0:
                                pe.wait_ge(down_free, tile * KC + (m + 1))
                            mm3(pe, psum[:, 4 + m, :], c2(c * DIM + m * P), x, c == 0, False)
                    for k in range(2):
                        pe.wait_ge(rank_ready, tile * 2 + (k + 1))
                        for m in range(KC):
                            mm = mm3(pe, psum[:, 4 + m, :], c2(B_OFF + m * P), (rank_hi[:, k, :], rank_lo[:, k, :]),
                                     False, k == 1)
                            if k == 1:
                                mm.then_inc(z_done, 1)

                    def gate_up(h):
                        r = min(P, HID - h * P)
                        for c in range(KC):
                            if h == 0:
                                pe.wait_ge(z_ready, tile * KC + (c + 1))
                            for w in range(2):
                                out = psum[0:r, 2 * (h % 2) + w, :]
                                wt = up[:, w, c, h * P:h * P + r]
                                pe.matmul(out, wt, z_hi[:, c, :], start=(c == 0), stop=False)
                                mm = pe.matmul(out, wt, z_lo[:, c, :], start=False, stop=(c == KC - 1))
                        mm.then_inc(up_done, 1)

                    def down_product(h):
                        r = min(P, HID - h * P)
                        pe.wait_ge(h_ready, tile * HT + (h + 1))
                        for m in range(KC):
                            wt = down[0:r, h, m * P:(m + 1) * P]
                            pe.matmul(psum[:, 4 + m, :], wt, h_hi[0:r, h % 2, :], start=(h == 0), stop=False)
                            mm = pe.matmul(psum[:, 4 + m, :], wt, h_lo[0:r, h % 2, :], start=False, stop=(h == HT - 1))
                        if h == HT - 1:
                            mm.then_inc(down_done, 1)

                    gate_up(0)
                    for h in range(1, HT):
                        gate_up(h)
                        down_product(h - 1)
                    down_product(HT - 1)


def layer_one(nc, t, sb, sem, const, mm3, resid, psum):
    ctx = ExitStack()
    with ctx:
        w_hi, w_lo = (sb(ctx, f"w1_{x}", [P, L1_COLS], F32R) for x in ("hi", "lo"))
        x_hi, x_lo = (sb(ctx, n, [P, KC, TT], F32R) for n in ("x1_hi", "x1_lo"))
        r_hi, r_lo = (sb(ctx, n, [P, KC, TT], F32R) for n in ("r_hi", "r_lo"))
        wide = sb(ctx, "wide", [P, KC, TT])
        misc = sb(ctx, "misc", [P, 8, TT])
        rank, bound, tok, att = misc[:, 0:2, :], misc[:, 2:4, :], misc[:, 4:6, :], misc[:, 6:8, :]
        gate_T = rank[:, 1, :]
        small = sb(ctx, "small1", [P, 96])
        ids_i = sb(ctx, "ids_i", [P, BATCH + TOK // P], I32)
        ids = sb(ctx, "ids", [P, BATCH + TOK // P])
        adapter_mask = sb(ctx, "adapter_mask", [P, KC, BATCH])
        lang = sb(ctx, "lang", [P, TOK // P, NE])
        gat = sb(ctx, "gat", [P, 12, SUBS * NE])
        gat_i = sb(ctx, "gat_i", [P, SUBS * NE], U32)
        spread = sb(ctx, "spread", [P, SUBS, NE, ER])

        small_in, piece_in = sem(ctx, "small_in"), [sem(ctx, f"piece_in{i}") for i in range(2)]
        l1_hi_done, l1_ready = sem(ctx, "l1_hi_done"), [sem(ctx, f"l1_ready{i}") for i in range(2)]
        prep_step = sem(ctx, "prep_step")
        x_hi_done, x_ready = sem(ctx, "x1_hi_done"), sem(ctx, "x1_ready")
        rank_done, rank_masked = sem(ctx, "rank1_done"), sem(ctx, "rank_masked")
        r_hi_done, r_ready = sem(ctx, "r_hi_done"), sem(ctx, "r_ready")
        base_done, wide_done, bound_done = sem(ctx, "base_done"), sem(ctx, "wide_done"), sem(ctx, "bound_done")
        turned, tok_done, s_done, sig_done, att_done = (
            sem(ctx, n) for n in ("turned", "tok_done", "s_done", "sig_done", "att_done"))
        pv_done, resid_done = sem(ctx, "pv1_done"), sem(ctx, "resid_done")
        logits_done, gate_step, e_done = sem(ctx, "logits_done"), sem(ctx, "gate_step"), sem(ctx, "e_done")
        spread_done, gateT_done, gateT_copied = sem(ctx, "spread_done"), sem(ctx, "gateT_done"), sem(ctx, "gateT_copied")
        h_done, gated, g_hi_done, g_ready = (sem(ctx, n) for n in ("h_done", "gated", "g_hi_done", "g_ready"))
        moe_done, c_hi_done, c_ready = sem(ctx, "moe_done"), sem(ctx, "c_hi_done"), sem(ctx, "c_ready")
        out_ready, out_stored = sem(ctx, "out_ready"), sem(ctx, "out_stored")
        banks_free = sem(ctx, "banks_free")
        act_passed, dve_passed = sem(ctx, "act_passed"), sem(ctx, "dve_passed")

        def wt(block, off, n=P):
            a = L1_AT[block] + off
            return w_hi[:, a:a + n], w_lo[:, a:a + n]

        with nc.Block() as block:
            stage = [wide[:].rearrange("p a n -> p (a n)"), misc[:, 0:4, :].rearrange("p a n -> p (a n)")]

            @block.sync
            def _(sp):
                sp.dma_start(small[:, 0:32], t["l1_small"]).then_inc(small_in, 16)
                sp.dma_start(small[:, 68:76], t["router_bias"]).then_inc(small_in, 16)
                sp.dma_start(ids_i[:], t["l1_ids"]).then_inc(small_in, 16)
                for n, (a, b) in enumerate(L1_PIECES):
                    if n >= 2:
                        sp.wait_ge(l1_ready[n % 2], n // 2)
                    sp.dma_start(stage[n % 2][:, 0:b - a], t["l1_w"][:, a:b]).then_inc(piece_in[n % 2], 16)

            @block.scalar
            def _(act):
                for n, (a, b) in enumerate(L1_PIECES):
                    act.wait_ge(piece_in[n % 2], 16 * (n // 2 + 1))
                    act.activation(w_hi[:, a:b], stage[n % 2][:, 0:b - a], ACT.Copy).then_inc(l1_hi_done, 1)

            @block.gpsimd
            def _(pool):
                for n, (a, b) in enumerate(L1_PIECES):
                    if n % 2 == 0:
                        pool.wait_ge(l1_hi_done, n + 1)
                        pool.tensor_tensor(w_lo[:, a:b], stage[0][:, 0:b - a], w_hi[:, a:b].bitcast(F32),
                                           ALU.subtract).then_inc(l1_ready[0], 1)

            @block.tensor
            def _(pe):
                pe.wait_ge(prep_step, 1)
                pe.matmul(psum[:, 0, 0:12], const("ones"), small[:, 32:44],
                          start=True, stop=True).then_inc(turned, 1)

            @block.vector
            def _(dve):
                n = [0]

                def then(ins):
                    n[0] += 1
                    ins.then_inc(prep_step, 1)
                    dve.wait_ge(prep_step, n[0])

                dve.wait_ge(small_in, 48)
                then(dve.scalar_tensor_tensor(out=small[:, 32:44], in0=small[:, 20:32], scalar=-1.0,
                                              in1=small[:, 20:32], op0=ALU.mult, op1=ALU.max))
                then(dve.tensor_scalar(small[:, 44:56], small[:, 20:32], 0.0, 2.0, ALU.is_ge, ALU.mult))
                then(dve.tensor_scalar(small[:, 44:56], small[:, 44:56], 1.0, None, ALU.subtract))
                dve.wait_ge(turned, 1)
                then(dve.scalar_tensor_tensor(out=small[:, 56:68], in0=psum[:, 0, 0:12], scalar=1.0 / P,
                                              in1=small[:, 44:56], op0=ALU.mult, op1=ALU.mult))
                then(dve.tensor_tensor(small[:, 8:12], small[:, 56:60], small[:, 60:64], ALU.mult))
                then(dve.tensor_copy(small[:, 12:16], small[:, 64:68]))
                then(dve.tensor_copy(ids[:], ids_i[:]))
                for r in range(KC):
                    then(dve.tensor_scalar(adapter_mask[:, r, :], ids[:, 0:BATCH], const("adapter")[:, r:r + 1],
                                           None, ALU.is_equal))
                then(dve.tensor_tensor(lang[:], ids[:, BATCH:].unsqueeze(2).broadcast_to([P, TOK // P, NE]),
                                       const("iota").unsqueeze(1).broadcast_to([P, TOK // P, NE]), ALU.is_equal))
                then(dve.tensor_scalar(lang[:], lang[:], 5.0, None, ALU.mult))
                for k, (a, b) in enumerate(L1_PIECES):
                    if k % 2:
                        dve.wait_ge(l1_hi_done, k + 1)
                        dve.tensor_tensor(w_lo[:, a:b], stage[1][:, 0:b - a], w_hi[:, a:b].bitcast(F32),
                                          ALU.subtract).then_inc(l1_ready[1], 1)

        def mine(tile, m):
            return resid[:, m, bass.ds(tile * TT, TT)]

        NG, NS = 19, 20
        NM = 2
        with nc.Block() as block:
            @block.sync
            def _(sp):
                with sp.Fori(0, NT) as tile:
                    for m in range(KC):
                        sp.wait_ge(out_ready, tile * KC + (m + 1))
                        sp.dma_start(t["out"][m * P:(m + 1) * P, bass.ds(tile * TT, TT)], wide[:, m, :]).then_inc(out_stored, 16)
                sp.wait_ge(out_stored, 16 * KC * NT)

            @block.scalar
            def _(act):
                with act.Fori(0, NT) as tile:
                    for c in range(KC):
                        act.activation(x_hi[:, c, :], mine(tile, c), ACT.Copy).then_inc(x_hi_done, 1)
                    for r in range(KC):
                        act.wait_ge(rank_masked, tile * KC + (r + 1))
                        act.activation(r_hi[:, r, :], rank[:, r % 2, :], ACT.Copy).then_inc(r_hi_done, 1)
                    for m in range(KC):
                        act.wait_ge(base_done, tile * KC + (m + 1))
                        if m == 0:
                            act.wait_ge(banks_free, tile + 1)
                        act.activation(wide[:, m, :], psum[:, 4 + m, :], ACT.Identity,
                                       bias=small[:, m:m + 1]).then_inc(wide_done, 1)
                    for m in range(KC):
                        act.wait_ge(turned, tile * KC + (m + 2))
                        act.activation(tok[:, m % 2, :], psum[:, m % 2, :], ACT.Copy).then_inc(tok_done, 1)
                        act.wait_ge(s_done, tile * KC + (m + 1))
                        act.activation(att[:, m % 2, :], psum[:, 2 + m % 2, :], ACT.Sigmoid,
                                       scale=SCALE1).then_inc(sig_done, 1)
                    for m in range(KC):
                        wait_apart(act, resid_done, tile * KC + (m + 1), act_passed)
                        act.activation(x_hi[:, m, :], mine(tile, m), ACT.Copy).then_inc(x_hi_done, 1)
                    for layer in range(NM):
                        if layer == 0:
                            act.wait_ge(gate_step, tile * (NG + NS) + 11)
                            act.activation(gat[:, 2, 0:SUBS], gat[:, 2, 0:SUBS], ACT.Exp).then_inc(e_done, 1)
                        act.wait_ge(gateT_done, tile * NM + (layer + 1))
                        act.activation(gate_T, psum[:, 2, :], ACT.Copy).then_inc(gateT_copied, 1)
                        act.wait_ge(gated, tile * NM + (layer + 1))
                        act.activation(r_hi[:, 0, :], rank[:, 0, :], ACT.Copy).then_inc(g_hi_done, 1)
                        if layer == 0:
                            for m in range(KC):
                                act.wait_ge(moe_done, tile * KC * NM + (m + 1))
                                act.activation(x_hi[:, m, :], psum[:, 4 + m, :], ACT.Copy).then_inc(c_hi_done, 1)
                    act.wait_ge(moe_done, tile * KC * NM + 2 * KC)

            @block.vector
            def _(dve):
                def gate_chain(tile, first):
                    k = [0]

                    def then(*several):
                        for ins in several:
                            k[0] += 1
                            ins.then_inc(gate_step, 1)
                        dve.wait_ge(gate_step, tile * (NG + NS) + (first + k[0]))
                    return then, k

                def g(i, n=NE):
                    return gat[:, i, 0:SUBS * n].rearrange("p (s e) -> p s e", s=SUBS)

                def per(a):
                    return a.unsqueeze(2).broadcast_to([P, SUBS, NE])

                def row(a):
                    return a.unsqueeze(1).broadcast_to([P, SUBS, NE])

                def tt(then, out, a, b, op):
                    then(dve.tensor_tensor(out, a, b, op))

                def top2_gates(tile):
                    then, k = gate_chain(tile, 0)
                    dve.wait_ge(logits_done, tile * NM + 1)
                    lg, top, hot, gates = g(0), g(1), g(4), g(5)
                    tt(then, lg, psum[:, 0, 0:SUBS * NE].rearrange("p (s e) -> p s e", s=SUBS),
                       lang[:, bass.ds(tile * SUBS, SUBS), :], ALU.add)
                    dve.sem_inc(dve_passed, 1)
                    then(*[dve.max(top[:, s, :], lg[:, s, :]) for s in range(SUBS)])
                    dve.sem_inc(dve_passed, 1)
                    then(*[dve.max_index(gat_i[:, s * NE:(s + 1) * NE], top[:, s, :], lg[:, s, :]) for s in range(SUBS)])
                    then(dve.tensor_copy(g(6), gat_i[:].rearrange("p (s e) -> p s e", s=SUBS)))
                    e2, w1, w2 = gat[:, 2, 0:SUBS], gat[:, 3, 0:SUBS], gat[:, 3, SUBS:2 * SUBS]
                    tt(then, e2, top[:, :, 1], top[:, :, 0], ALU.subtract)
                    dve.wait_ge(e_done, tile + 1)
                    then(dve.tensor_scalar(w1, e2, 1.0, 0.5, ALU.add, ALU.mult))
                    then(dve.reciprocal(w1, w1))
                    tt(then, w2, w1, e2, ALU.mult)
                    tt(then, hot, row(const("iota")), per(g(6)[:, :, 0]), ALU.is_equal)
                    tt(then, gates, hot, per(w1), ALU.mult)
                    tt(then, hot, row(const("iota")), per(g(6)[:, :, 1]), ALU.is_equal)
                    tt(then, hot, hot, per(w2), ALU.mult)
                    tt(then, gates, gates, hot, ALU.add)
                    assert k[0] == NG, k
                    return gates

                def sparsemax_gates(tile):
                    then, k = gate_chain(tile, NG)
                    dve.wait_ge(logits_done, tile * NM + 2)
                    z, srt, cum, alt, sup = g(0), g(1), g(4), g(5), g(6)
                    tt(then, z, psum[:, 0, SUBS * NE:2 * SUBS * NE].rearrange("p (s e) -> p s e", s=SUBS),
                       row(small[:, 68:76]), ALU.add)
                    dve.sem_inc(dve_passed, 1)
                    then(*[dve.max(srt[:, s, :], z[:, s, :]) for s in range(SUBS)])
                    src = srt
                    for d, dst in ((1, cum), (2, alt), (4, cum)):
                        then(dve.tensor_copy(dst[:, :, 0:d], src[:, :, 0:d]))
                        tt(then, dst[:, :, d:], src[:, :, d:], src[:, :, 0:NE - d], ALU.add)
                        src = dst
                    tt(then, alt, srt, row(const("count")), ALU.mult)
                    then(dve.scalar_tensor_tensor(out=sup, in0=alt, scalar=1.0, in1=cum, op0=ALU.add, op1=ALU.is_gt))
                    kz, ts_, tau = gat[:, 2, 0:SUBS], gat[:, 2, SUBS:2 * SUBS], gat[:, 3, 0:SUBS]
                    then(dve.tensor_reduce(kz, sup, AX_X, ALU.add))
                    tt(then, alt, row(const("count")), per(kz), ALU.is_equal)
                    tt(then, alt, alt, cum, ALU.mult)
                    then(dve.tensor_reduce(ts_, alt, AX_X, ALU.add))
                    then(dve.reciprocal(kz, kz))
                    then(dve.scalar_tensor_tensor(out=tau, in0=ts_, scalar=-1.0, in1=kz, op0=ALU.add, op1=ALU.mult))
                    tt(then, z, z, per(tau), ALU.subtract)
                    assert k[0] == NS, k
                    return z

                def mask_att(dve, tile, m):
                    dve.wait_ge(sig_done, tile * KC + (m + 1))
                    dve.tensor_tensor(att[:, m % 2, :].rearrange("p (s n) -> p s n", n=P),
                                      att[:, m % 2, :].rearrange("p (s n) -> p s n", n=P),
                                      const("causal_mul").unsqueeze(1).broadcast_to([P, SUBS, P]),
                                      ALU.mult).then_inc(att_done, 1)

                def add_attention(dve, tile, m):
                    dve.wait_ge(pv_done, tile * KC + (m + 1))
                    dve.scalar_tensor_tensor(out=mine(tile, m), in0=psum[:, 4 + m, :], scalar=small[:, 12 + m:13 + m],
                                             in1=mine(tile, m), op0=ALU.mult, op1=ALU.add).then_inc(resid_done, 1)
                    dve.wait_ge(x_hi_done, tile * 2 * KC + (KC + m + 1))
                    dve.tensor_tensor(x_lo[:, m, :], mine(tile, m), x_hi[:, m, :].bitcast(F32),
                                      ALU.subtract).then_inc(x_ready, 1)

                dve.sem_inc(banks_free, 1)
                with dve.Fori(0, NT) as tile:
                    for c in range(KC):
                        dve.wait_ge(x_hi_done, tile * 2 * KC + (c + 1))
                        dve.tensor_tensor(x_lo[:, c, :], mine(tile, c), x_hi[:, c, :].bitcast(F32),
                                          ALU.subtract).then_inc(x_ready, 1)
                    for r in range(KC):
                        dve.wait_ge(rank_done, tile * KC + (r + 1))
                        own = adapter_mask[:, r, bass.ds(tile * BPT, BPT)].unsqueeze(2).broadcast_to([P, BPT, SEQ])
                        dve.tensor_tensor(rank[:, r % 2, :].rearrange("p (b s) -> p b s", s=SEQ),
                                          psum[:, r, :].rearrange("p (b s) -> p b s", s=SEQ), own,
                                          ALU.mult).then_inc(rank_masked, 1)
                        dve.wait_ge(r_hi_done, tile * KC + (r + 1))
                        dve.tensor_tensor(r_lo[:, r, :], rank[:, r % 2, :], r_hi[:, r, :].bitcast(F32),
                                          ALU.subtract).then_inc(r_ready, 1)
                    for m in range(KC):
                        dve.wait_ge(wide_done, tile * KC + (m + 1))
                        if m >= 2:
                            dve.wait_ge(s_done, tile * KC + (m - 1))
                        dve.tensor_scalar(bound[:, m % 2, :], wide[:, m, :], small[:, 8 + m:9 + m], None,
                                          ALU.mult).then_inc(bound_done, 1)
                        if m >= 1:
                            mask_att(dve, tile, m - 1)
                    mask_att(dve, tile, KC - 1)
                    for m in range(KC):
                        add_attention(dve, tile, m)
                    for layer, gates_of in enumerate((top2_gates, sparsemax_gates)):
                        gates = gates_of(tile)
                        wide_gates = gates.unsqueeze(3).broadcast_to([P, SUBS, NE, ER])
                        if layer == 0:
                            dve.tensor_copy(spread[:], wide_gates).then_inc(spread_done, 1)
                        else:
                            dve.tensor_scalar(spread[:], wide_gates, 0.0, None, ALU.max).then_inc(spread_done, 1)
                        dve.wait_ge(h_done, tile * NM + (layer + 1))
                        dve.wait_ge(gateT_copied, tile * NM + (layer + 1))
                        dve.tensor_tensor(rank[:, 0, :], psum[:, 1, :], gate_T, ALU.mult).then_inc(gated, 1)
                        dve.wait_ge(g_hi_done, tile * NM + (layer + 1))
                        dve.tensor_tensor(r_lo[:, 0, :], rank[:, 0, :], r_hi[:, 0, :].bitcast(F32),
                                          ALU.subtract).then_inc(g_ready, 1)
                        for m in range(KC):
                            if layer == 0:
                                dve.wait_ge(c_hi_done, tile * KC + (m + 1))
                                dve.tensor_tensor(x_lo[:, m, :], psum[:, 4 + m, :], x_hi[:, m, :].bitcast(F32),
                                                  ALU.subtract).then_inc(c_ready, 1)
                            else:
                                dve.wait_ge(moe_done, tile * KC * NM + (KC + m + 1))
                                dve.scalar_tensor_tensor(out=wide[:, m, :], in0=psum[:, 4 + m, :],
                                                         scalar=small[:, 4 + m:5 + m], in1=mine(tile, m),
                                                         op0=ALU.add, op1=ALU.add).then_inc(out_ready, 1)
                    dve.wait_ge(out_stored, tile * (16 * KC) + 16 * KC)
                    dve.sem_inc(banks_free, 1)

            @block.tensor
            def _(pe):
                def xs(c):
                    return x_hi[:, c, :], x_lo[:, c, :]

                with pe.Fori(0, NT) as tile:
                    for c in range(KC):
                        pe.wait_ge(x_ready, tile * 2 * KC + (c + 1))
                        for r in range(KC):
                            mm = mm3(pe, psum[:, r, :], wt("Ac", c * DIM + r * P), xs(c), c == 0, c == KC - 1)
                            if c == KC - 1:
                                mm.then_inc(rank_done, 1)
                    pe.wait_ge(banks_free, tile + 1)
                    for c in range(KC):
                        for m in range(KC):
                            mm3(pe, psum[:, 4 + m, :], wt("Wc", c * DIM + m * P), xs(c), c == 0, False)
                    for r in range(KC):
                        pe.wait_ge(r_ready, tile * KC + (r + 1))
                        for m in range(KC):
                            mm = mm3(pe, psum[:, 4 + m, :], wt("Bc", r * DIM + m * P), (r_hi[:, r, :], r_lo[:, r, :]),
                                     False, r == KC - 1)
                            if r == KC - 1:
                                mm.then_inc(base_done, 1)

                    def turn_and_score(m):
                        if m >= 2:
                            pe.wait_ge(tok_done, tile * KC + (m - 1))
                            pe.wait_ge(sig_done, tile * KC + (m - 1))
                        pe.wait_ge(wide_done, tile * KC + (m + 1))
                        for i in range(SUBS):
                            tr = pe.transpose(psum[:, m % 2, i * P:(i + 1) * P], wide[:, m, i * P:(i + 1) * P], const("ident"))
                        tr.then_inc(turned, 1)
                        pe.wait_ge(bound_done, tile * KC + (m + 1))
                        for i in range(SUBS):
                            cols = slice(i * P, (i + 1) * P)
                            mm = pe.matmul(psum[:, 2 + m % 2, cols], bound[:, m % 2, cols], wide[:, m, cols], start=True, stop=True)
                        mm.then_inc(s_done, 1)

                    def attend(m):
                        pe.wait_ge(tok_done, tile * KC + (m + 1))
                        pe.wait_ge(att_done, tile * KC + (m + 1))
                        for i in range(SUBS):
                            cols = slice(i * P, (i + 1) * P)
                            mm = pe.matmul(psum[:, 4 + m, cols], tok[:, m % 2, cols], att[:, m % 2, cols], start=True, stop=True)
                        mm.then_inc(pv_done, 1)

                    turn_and_score(0)
                    for m in range(1, KC):
                        turn_and_score(m)
                        attend(m - 1)
                    attend(KC - 1)

                    for layer, (W, A, B, R) in enumerate((("W2", "A2", "B2", "R2"), ("Wf", "Af", "Bf", "Rf"))):
                        for c in range(KC):
                            if layer == 0:
                                pe.wait_ge(x_ready, tile * 2 * KC + (KC + c + 1))
                            else:
                                pe.wait_ge(c_ready, tile * KC + (c + 1))
                            mm = mm3(pe, psum[:, 1, :], wt(A, c * P), xs(c), c == 0, c == KC - 1)
                        mm.then_inc(h_done, 1)
                        for i in range(SUBS):
                            cols = slice(i * P, (i + 1) * P)
                            at = (layer * SUBS + i) * NE
                            for c in range(KC):
                                mm = mm3(pe, psum[:, 0, at:at + NE], (x_hi[:, c, cols], x_lo[:, c, cols]),
                                         wt(R, c * NE, NE), c == 0, c == KC - 1)
                        mm.then_inc(logits_done, 1)
                        for c in range(KC):
                            for m in range(KC):
                                mm3(pe, psum[:, 4 + m, :], wt(W, c * DIM + m * P), xs(c), c == 0, False)
                        pe.wait_ge(spread_done, tile * NM + (layer + 1))
                        for i in range(SUBS):
                            tr = pe.transpose(psum[:, 2, i * P:(i + 1) * P], spread[:, i, :, :].rearrange("p e r -> p (e r)"),
                                              const("ident"))
                        tr.then_inc(gateT_done, 1)
                        pe.wait_ge(g_ready, tile * NM + (layer + 1))
                        for m in range(KC):
                            mm3(pe, psum[:, 4 + m, :], wt(B, m * P), (r_hi[:, 0, :], r_lo[:, 0, :]), False, True)\
                                .then_inc(moe_done, 1)


def kernel(**inputs):
    import concourse.bacc as bacc
    from concourse.bass_utils import run_bass_kernel_spmd

    a = {k: np.asarray(v) for k, v in inputs.items()}
    f32 = np.float32

    def chunks(w, width=None):
        return w.reshape(KC, P, -1).transpose(1, 0, 2).reshape(P, -1)

    def flipped(w):
        return w.reshape(KC, P, -1)[:, ::-1].reshape(KC * P, -1)

    def both(w):
        return np.concatenate([w.T, w.T], 0)

    arrays = {}
    arrays["xT"] = a["x"].reshape(TOK, DIM).T
    log_dt = np.broadcast_to(a["L0_cond_log_dt"], (P, SEQ))
    C = a["L0_cond_C"]
    arrays["s4d"] = np.stack([log_dt, both(a["L0_cond_log_A_real"]), both(a["L0_cond_A_imag"]),
                              both(C[..., 0]), both(C[..., 1])], 1)
    skip = np.zeros((LI, SEQ, LJ), f32)
    skip[LI - 1, :, LJ - 1] = a["L0_cond_D"]
    arrays["skip"] = skip.reshape(LI, -1)
    arrays["zeros"] = np.zeros((SEQ, P), f32)
    arrays["lengths"] = np.broadcast_to(a["itok_B_78_3631"].astype(np.int32), (P, BATCH))
    arrays["consts"] = constant_table()[0]

    wq = flipped(a["L0_attn_wq"].reshape(DIM, HEADS, DQ)[:, :, :DH].reshape(DIM, HEADS * DH))
    wkv = flipped(a["L0_attn_wkv"])
    wo = a["L0_attn_wo"].reshape(GROUPS, GH, DH, DIM)

    def grouped(w):
        return w.reshape(KC, P, GROUPS, GH * DH).transpose(2, 1, 0, 3).reshape(GROUPS, P, -1)

    arrays["attn_w"] = np.concatenate([
        grouped(wq), grouped(wkv[:, :HEADS * DH]), grouped(wkv[:, HEADS * DH:2 * HEADS * DH]),
        wo.transpose(0, 2, 1, 3).reshape(GROUPS, P, -1)], 2)

    lora_a = a["L0_cond2_lora_A"].transpose(1, 0, 2).reshape(DIM, LAB * LR)
    lora_a = np.concatenate([lora_a, np.zeros((DIM, 2 * P - LAB * LR), f32)], 1)
    lora_b = np.tile(a["L0_cond2_lora_B"].T, (P // LR, 1))
    arrays["c2_w"] = np.concatenate([chunks(a["L0_cond2_weight"].T), chunks(lora_a), lora_b], 1)
    arrays["c2_bias"] = a["L0_cond2_bias"].reshape(KC, P).T
    arrays["labels"] = np.broadcast_to(a["itok_B_0_4"].astype(np.int32), (P, BATCH))
    j_of, _ = octonion_table()
    ffn = [a["L0_ffn_w_gate"], a["L0_ffn_w_up"], a["L0_ffn_w_down"]]
    arrays["oct_base"] = np.stack([w.reshape(P, -1) for w in ffn], 1)
    arrays["oct_up"] = np.stack([w[j_of].transpose(0, 3, 1, 2).reshape(OCT * OD, HID) for w in ffn[:2]])
    dn = ffn[2][j_of].transpose(0, 3, 1, 2).reshape(HID, DIM)
    arrays["oct_down"] = np.concatenate([dn, np.zeros((HT * P - HID, DIM), f32)], 0)

    ada_a = a["L1_cond_lora_A_w"].transpose(2, 0, 1).reshape(DIM, ADA * AR)
    ada_b = a["L1_cond_lora_B_w"].transpose(0, 2, 1).reshape(ADA * AR, DIM)
    blocks = {
        "Wc": chunks(a["L1_cond_base_weight"].T), "Ac": chunks(ada_a), "Bc": chunks(ada_b),
        "W2": chunks(a["L1_cond2_W"].T), "Wf": chunks(a["L1_ffn_W_base"].T),
        "A2": chunks(a["L1_cond2_A"].reshape(NE * ER, DIM).T),
        "B2": a["L1_cond2_B"].transpose(0, 2, 1).reshape(NE * ER, DIM),
        "Af": chunks(a["L1_ffn_lora_A"].transpose(1, 0, 2).reshape(DIM, NE * ER)),
        "Bf": a["L1_ffn_lora_B"].reshape(NE * ER, DIM),
        "R2": chunks(a["L1_cond2_Wr"].T), "Rf": chunks(a["L1_ffn_W_router"].T),
    }
    arrays["l1_w"] = np.concatenate([blocks[n] for n, _ in L1_BLOCKS], 1)
    small = np.zeros((P, 32), f32)
    small[:, 0:4] = a["L1_cond_base_bias"].reshape(KC, P).T
    small[:, 4:8] = a["L1_ffn_b_base"].reshape(KC, P).T
    small[:, 20:24], small[:, 24:28], small[:, 28:32] = (a[f"L1_attn_bv_{n}"].T for n in "qkv")
    arrays["l1_small"] = small
    arrays["router_bias"] = np.broadcast_to(a["L1_ffn_b_router"], (P, NE))
    by_token = np.repeat(a["itok_B_0_7"].astype(np.int32), SEQ).reshape(TOK // P, P).T
    arrays["l1_ids"] = np.concatenate([np.broadcast_to(a["itok_B_6_15"].astype(np.int32), (P, BATCH)), by_token], 1)

    nc = bacc.Bacc("TRN2", target_bir_lowering=False, num_devices=1)
    given, handles = {}, {}
    for name, v in arrays.items():
        v = np.ascontiguousarray(v)
        given[f"in_{name}"] = v
        handles[name] = nc.dram_tensor(f"in_{name}", v.shape, mybir.dt.from_np(v.dtype), kind="ExternalInput").ap()
    handles["out"] = nc.dram_tensor("outT", (DIM, TOK), F32, kind="ExternalOutput").ap()
    build_program(nc, handles)
    r = run_bass_kernel_spmd(nc, [given], core_ids=[0])
    return r.results[0]["outT"].T.reshape(BATCH, SEQ, DIM)
```

```python
from contextlib import ExitStack

import numpy as np
import concourse.bass as bass
from concourse import mybir

F32 = mybir.dt.float32
F32R = mybir.dt.float32r
I32 = mybir.dt.int32
U32 = mybir.dt.uint32
ACT = mybir.ActivationFunctionType
ALU = mybir.AluOpType
AX_X = mybir.AxisListType.X

P = 128
BATCH, SEQ, DIM = 64, 32, 512
TOK = BATCH * SEQ
KC = DIM // P
TT = 512
NT = TOK // TT
SUBS = TT // P
BPT = TT // SEQ
HEADS, DH, DQ = 32, 128, 192
GH = 2
GROUPS = HEADS // GH
GW = 3 * KC * GH * DH + GH * DIM
PIECE = GW // NT
QOFF, KOFF, VOFF, OOFF = 0, KC * GH * DH, 2 * KC * GH * DH, 3 * KC * GH * DH
NST = 64
LI, LJ = 16, 32
RROW = DIM + P
OCT, OH, OD = 8, 170, 64
HID = OCT * OH
HT = -(-HID // P)
HTP = -(-HT // NT) * NT
TERN_DOWN = HTP // NT * DIM // 2
TERN = [(0, HID), (HID, HID), (2 * HID, TERN_DOWN), (2 * HID + TERN_DOWN, TERN_DOWN)]
TERN_COLS = 2 * HID + 2 * TERN_DOWN
LAB, LR = 5, 32
ADA, AR = 32, 16
ABATCH = P // AR
AGROUPS = BPT // ABATCH
GATHERED = 16 * 2 * AGROUPS
NE, ER = 8, 16
BIND_HEADS = 4
SCALE0 = float(DQ) ** -0.5
SCALE1 = float(P) ** -0.5 * 4.0
NEG = -1e30
MAGIC = 12582912.0
LN2_HI, LN2_LO = 0.693359375, -2.12194440e-4
TWO_PI = (6.28125, 1.9350051879882812e-3, 3.019915978e-7)
PI_IN = 3.1415925


def octonion_table():
    s = np.zeros((8, 8, 8), np.float32)
    s[0, 0, 0] = 1.0
    for i in range(1, 8):
        s[0, i, i] = s[i, 0, i] = 1.0
        s[i, i, 0] = -1.0
    for a, b, c in [(1, 2, 3), (1, 4, 5), (1, 7, 6), (2, 4, 6), (2, 5, 7), (3, 4, 7), (3, 6, 5)]:
        for x, y, z in ((a, b, c), (b, c, a), (c, a, b)):
            s[x, y, z] = 1.0
            s[y, x, z] = -1.0
    return np.abs(s).argmax(0), s.sum(0)


def constant_table():
    p = np.arange(P)
    part = p // NST
    li = LJ * (LI - 1 - np.arange(LI))
    lj = LJ - 1 - np.arange(LJ)
    lags = np.concatenate([li, li, lj])
    quarter = np.zeros((P, 2 * LI + LJ))
    quarter[:, :LI] = (1 + part)[:, None]
    quarter[:, LI:2 * LI] = (2 + part)[:, None]
    quarter[:, 2 * LI:] = (1 - part)[:, None]
    q = p % SEQ
    j_of, sign = octonion_table()
    sign_up = np.stack([np.stack([-sign[2 * c + x // OD] for x in p]) for c in range(KC)], 1)
    unit = np.minimum(p[:, None] + P * np.arange(HTP)[None], HID - 1)
    sign_down = -sign[unit // OH]
    fields = {
        "lags": np.broadcast_to(lags, (P, len(lags))),
        "turns": quarter / 4,
        "angles": quarter * (np.pi / 2),
        "feature": P * np.arange(KC)[None] + (P - 1 - p)[:, None],
        "causal_add": np.where(np.arange(SEQ)[None] <= q[:, None], 0.0, NEG),
        "causal_mul": (p[:, None] // SEQ == p[None] // SEQ) * (p[:, None] <= p[None]),
        "ident": np.eye(P),
        "ones": np.ones((P, P)),
        "labeler": (p // LR)[:, None] + np.array([[0, P // LR]]),
        "own_batch": (p // AR)[:, None] == np.arange(BPT)[None] % ABATCH,
        "adapter_rank": (p % AR)[:, None],
        "iota": np.broadcast_to(np.arange(NE), (P, NE)),
        "count": np.broadcast_to(1 + np.arange(NE), (P, NE)),
        "sign_up": sign_up.reshape(P, -1),
        "sign_down": sign_down.reshape(P, -1),
    }
    at, n = {}, 0
    for name, a in fields.items():
        at[name] = (n, n + a.shape[1])
        n += a.shape[1]
    return np.concatenate(list(fields.values()), 1).astype(np.float32), at


L1_BLOCKS = [("Wc", KC * DIM), ("W2", KC * DIM), ("Wf", KC * DIM), ("A2", KC * P), ("B2", DIM),
             ("Af", KC * P), ("Bf", DIM), ("R2", KC * NE), ("Rf", KC * NE)]
L1_AT, _n = {}, 0
for _name, _w in L1_BLOCKS:
    L1_AT[_name] = _n
    _n += _w
L1_COLS = _n
L1_PIECES = [(a, min(a + KC * DIM, L1_COLS)) for a in range(0, L1_COLS, KC * DIM)]
L1_SPLITS = sum(-(-(b - a) // DIM) for a, b in L1_PIECES)
C2_COLS = KC * DIM + KC * 2 * P + DIM


def build_program(nc, t):
    _, CONST = constant_table()
    ctx = ExitStack()
    with ctx:
        def sb(stack, name, shape, dt=F32):
            return stack.enter_context(nc.sbuf_tensor(name, shape, dt))

        def sem(stack, name):
            return stack.enter_context(nc.semaphore(name))

        def overlaid(stack, name, shape):
            with nc.sbuf_tensor(f"{name}_f32", shape, F32) as plain:
                pass
            return plain, sb(stack, name, shape, F32R)

        resid = sb(ctx, "resid", [P, KC, TOK])
        consts = sb(ctx, "consts", [P, t["consts"].shape[1]])
        psum = ctx.enter_context(nc.psum_tensor("psum", [P, 8, TT], F32))
        kernel_rows = nc.dram_tensor("kernel_rows", [SEQ, RROW], F32, kind="Internal").ap()

        def const(name):
            a, b = CONST[name]
            return consts[:, a:b]

        def mm3(pe, out, w, x, start, stop):
            pe.matmul(out, w[0], x[0], start=start, stop=False)
            pe.matmul(out, w[0], x[1], start=False, stop=False)
            return pe.matmul(out, w[1], x[0], start=False, stop=stop)

        gather_rows = sb(ctx, "gather_rows", [P, BATCH // ABATCH], U32)
        kept_raw, kept = overlaid(ctx, "kept", [P, 2, L1_COLS // 2])
        attn = ctx.enter_context(ExitStack())
        y_hi = sb(attn, "y_hi", [P, KC, TOK], F32R)
        y_lo = sb(attn, "y_lo", [P, KC, TOK], F32R)
        wraw = sb(attn, "wraw", [P, GW])
        raw_loaded = [sem(attn, f"raw_loaded{i}") for i in range(NT)]
        s4d_and_convolution(nc, t, sb, sem, const, consts, resid, psum, kernel_rows, y_hi, y_lo, wraw, raw_loaded)
        attention(nc, t, sb, sem, const, mm3, resid, psum, kept, y_hi, y_lo, wraw, raw_loaded)
        attn.close()
        octonion_ffn(nc, t, sb, sem, overlaid, const, mm3, resid, psum, kept_raw, kept, gather_rows)
        layer_one(nc, t, sb, sem, const, mm3, resid, psum, kept_raw, kept, gather_rows)


def wait_apart(engine, semaphore, value, passed):
    engine.wait_ge(semaphore, value)
    engine.sem_inc(passed, 1)


def chained(engine, semaphore):
    n = [0]

    def then(ins):
        n[0] += 1
        ins.then_inc(semaphore, 1)
        engine.wait_ge(semaphore, n[0])

    def tt(out, a, b, op):
        then(engine.tensor_tensor(out, a, b, op))

    def ts(out, a, s1, s2, op0, op1=None):
        then(engine.tensor_scalar(out, a, s1, s2, op0, *(() if op1 is None else (op1,))))

    def stt(out, a, s, b, op0, op1):
        then(engine.scalar_tensor_tensor(out=out, in0=a, scalar=s, in1=b, op0=op0, op1=op1))

    return then, tt, ts, stt


def exp_minus_1(then, tt, ts, engine, x, em1, two_k, tmp):
    t0, t1, t2 = tmp
    ts(t0, x, 1.4426950408889634, MAGIC, ALU.mult, ALU.add)
    ts(t0, t0, MAGIC, None, ALU.subtract)
    ts(t2, t0, -LN2_HI, None, ALU.mult)
    tt(t1, t2, x, ALU.add)
    ts(t2, t0, -LN2_LO, None, ALU.mult)
    tt(t1, t1, t2, ALU.add)
    ts(t0, t0, 127.0, 8388608.0, ALU.add, ALU.mult)
    then(engine.tensor_copy(two_k.bitcast(I32), t0))
    ts(t2, t1, 1 / 40320.0, 1 / 5040.0, ALU.mult, ALU.add)
    for c in (1 / 720.0, 1 / 120.0, 1 / 24.0, 1 / 6.0, 0.5, 1.0):
        tt(t2, t2, t1, ALU.mult)
        ts(t2, t2, c, None, ALU.add)
    tt(t2, t2, t1, ALU.mult)
    tt(t2, t2, two_k, ALU.mult)
    ts(t0, two_k, 1.0, None, ALU.subtract)
    tt(em1, t2, t0, ALU.add)


def s4d_and_convolution(nc, t, sb, sem, const, consts, resid, psum, kernel_rows, y_hi, y_lo, wraw, raw_loaded):
    ctx = ExitStack()
    with ctx:
        NW = 2 * LI + LJ
        NB = 4
        PB, NCB = TT // (KC * BATCH), 4
        prm = sb(ctx, "prm", [P, 5, SEQ])
        sk = sb(ctx, "sk", [P, 21, 2 * SEQ])
        dt, ar = sk[:, 0, 0:SEQ], sk[:, 0, SEQ:]
        ai, cr, ci = prm[:, 2, :], prm[:, 3, :], prm[:, 4, :]
        da, db, inv = sk[:, 5, 0:SEQ], sk[:, 6, 0:SEQ], sk[:, 18, 0:SEQ]
        ctr, cti = sk[:, 19, 0:SEQ], sk[:, 20, 0:SEQ]
        lensi = sb(ctx, "lensi", [P, BATCH], I32)
        lens = sb(ctx, "lens", [P, BATCH])
        mask = sb(ctx, "mask", [P, KC, BATCH])
        theta = sb(ctx, "theta", [P, SEQ, NW])
        turns = sb(ctx, "turns", [P, SEQ, NW])
        mag = sb(ctx, "mag", [P, SEQ, LI + LJ])
        left = sb(ctx, "left", [P, SEQ, LI])
        right = sb(ctx, "right", [P, SEQ, LJ])
        skip = sb(ctx, "skip", [LI, SEQ * LJ])
        rows = sb(ctx, "rows", [LI, SEQ * LJ])
        hankel = sb(ctx, "hankel", [P, NB, DIM])
        ymask = sb(ctx, "ymask", [P, 2, TT])

        params_in, x_in, const_in = sem(ctx, "params_in"), sem(ctx, "x_in"), sem(ctx, "const_in")
        step, pool_step = sem(ctx, "s4d_step"), sem(ctx, "pool_step")
        small_ready, ct_ready = sem(ctx, "small_ready"), sem(ctx, "ct_ready")
        trig_ready, trig_done = sem(ctx, "trig_ready"), sem(ctx, "trig_done")
        mag_ready, mag_done = sem(ctx, "mag_ready"), sem(ctx, "mag_done")
        factors_ready, kernels_done = sem(ctx, "factors_ready"), sem(ctx, "kernels_done")
        rows_ready, rows_stored = sem(ctx, "rows_ready"), sem(ctx, "rows_stored")
        hankel_in = [sem(ctx, f"hankel_in{i}") for i in range(NB)]
        hankel_free = sem(ctx, "hankel_free")
        mask_ready = sem(ctx, "mask_ready")
        conv_done, bank_free = sem(ctx, "conv_done"), sem(ctx, "bank_free")
        masked, y_hi_done, ymask_free = sem(ctx, "masked"), sem(ctx, "y_hi_done"), sem(ctx, "ymask_free")
        overlapping = bass.AP(tensor=kernel_rows.tensor, offset=0, ap=[[RROW, SEQ], [1, P], [1, DIM]])
        block = ctx.enter_context(nc.Block())

        @block.sync
        def _(sp):
            sp.dma_start(prm[:], t["s4d"]).then_inc(params_in, 16)
            sp.dma_start(consts[:], t["consts"]).then_inc(const_in, 16)
            sp.dma_start(skip[:], t["skip"]).then_inc(params_in, 16)
            sp.dma_start(lensi[:], t["lengths"]).then_inc(params_in, 16)
            sp.dma_start(kernel_rows[:, DIM:RROW], t["zeros"]).then_inc(rows_stored, 16)
            for c in range(KC):
                sp.dma_start(resid[:, c, :], t["xT"][c * P:(c + 1) * P, :]).then_inc(x_in, 16)
            for p in range(NT):
                sp.dma_start(wraw[:, p * PIECE:(p + 1) * PIECE],
                             t["attn_w"][0, :, p * PIECE:(p + 1) * PIECE]).then_inc(raw_loaded[p], 16)
            sp.wait_ge(rows_ready, 1)
            sp.dma_start(kernel_rows[:, 0:DIM].rearrange("h (i j) -> i h j", i=LI),
                         rows[:].rearrange("i (h j) -> i h j", h=SEQ)).then_inc(rows_stored, 16)
            sp.wait_ge(rows_stored, 32)
            def load_hankel(h, b):
                src = overlapping[bass.ds(h, 1), :, :].rearrange("h p n -> (h p) n")
                sp.dma_start(hankel[:, b, :], src).then_inc(hankel_in[b], 16)

            for b in range(NB):
                load_hankel(b, b)
            with sp.Fori(1, SEQ // NB) as it:
                for b in range(NB):
                    used = hankel_free if b % PB < PB - 1 else conv_done
                    sp.wait_ge(used, (it - 1) * (NB // PB) + (b // PB + 1))
                    load_hankel(it * NB + b, b)

        @block.vector
        def _(dve):
            then, tt, ts, stt = chained(dve, step)

            def reduce_angle(out, x, k):
                for part in TWO_PI:
                    stt(out, k, -part, x if part == TWO_PI[0] else out, ALU.mult, ALU.add)

            dve.wait_ge(params_in, 48)
            logs = prm[:, 0:2, :].rearrange("p a h -> p (a h)")
            exp_minus_1(then, tt, ts, dve, logs, sk[:, 0, :], sk[:, 1, :], [sk[:, i, :] for i in (2, 3, 4)])
            ts(sk[:, 0, :], sk[:, 0, :], 1.0, None, ALU.add)
            stt(da, ar, -1.0, dt, ALU.mult, ALU.mult)
            tt(db, ai, dt, ALU.mult)
            ang, turn = sk[:, 7, :], sk[:, 2, :]
            then(dve.tensor_copy(ang[:, 0:SEQ], db))
            ts(ang[:, SEQ:], db, 0.5, None, ALU.mult)
            ts(turn, ang, 0.15915494309189535, MAGIC, ALU.mult, ALU.add)
            ts(turn, turn, MAGIC, None, ALU.subtract)
            reduce_angle(ang, ang, turn)
            ts(ang, ang, PI_IN, -PI_IN, ALU.min, ALU.max)
            tt(sk[:, 3, 0:SEQ], ar, ar, ALU.mult)
            tt(sk[:, 4, 0:SEQ], ai, ai, ALU.mult)
            tt(sk[:, 3, 0:SEQ], sk[:, 3, 0:SEQ], sk[:, 4, 0:SEQ], ALU.add)
            then(dve.reciprocal(inv, sk[:, 3, 0:SEQ]))
            dve.sem_inc(small_ready, 1)

            dve.wait_ge(const_in, 16)
            tt(mag[:], da.unsqueeze(2).broadcast_to([P, SEQ, LI + LJ]),
               const("lags")[:, LI:].unsqueeze(1).broadcast_to([P, SEQ, LI + LJ]), ALU.mult)
            dve.sem_inc(mag_ready, 1)
            tt(theta[:], db.unsqueeze(2).broadcast_to([P, SEQ, NW]),
               const("lags").unsqueeze(1).broadcast_to([P, SEQ, NW]), ALU.mult)
            stt(turns[:], theta[:], 0.15915494309189535,
                const("turns").unsqueeze(1).broadcast_to([P, SEQ, NW]), ALU.mult, ALU.add)
            ts(turns[:], turns[:], MAGIC, MAGIC, ALU.add, ALU.subtract)
            reduce_angle(theta[:], theta[:], turns[:])
            tt(theta[:], theta[:], const("angles").unsqueeze(1).broadcast_to([P, SEQ, NW]), ALU.add)
            ts(theta[:], theta[:], PI_IN, -PI_IN, ALU.min, ALU.max)
            dve.sem_inc(trig_ready, 1)
            dve.wait_ge(mag_done, 1)
            dve.wait_ge(ct_ready, 1)
            dve.wait_ge(trig_done, 2)
            tt(left[:], theta[:, :, 0:LI], ctr.unsqueeze(2).broadcast_to([P, SEQ, LI]), ALU.mult)
            tt(turns[:, :, 0:LI], theta[:, :, LI:2 * LI], cti.unsqueeze(2).broadcast_to([P, SEQ, LI]), ALU.mult)
            tt(left[:], left[:], turns[:, :, 0:LI], ALU.add)
            tt(left[:], left[:], mag[:, :, 0:LI], ALU.mult)
            tt(right[:], theta[:, :, 2 * LI:], mag[:, :, LI:], ALU.mult)
            dve.sem_inc(factors_ready, 1)
            then(dve.tensor_copy(lens[:], lensi[:]))
            for c in range(KC):
                ts(mask[:, c, :], lens[:], const("feature")[:, c:c + 1], None, ALU.is_gt)
            dve.wait_ge(kernels_done, 1)
            tt(rows[:], psum[0:LI, 0:2, :].rearrange("p b n -> p (b n)"), skip[:], ALU.add)
            dve.sem_inc(rows_ready, 1)
            dve.sem_inc(bank_free, NCB)
            with dve.Fori(0, SEQ // (PB * NCB)) as it:
                for k in range(NCB):
                    dve.wait_ge(conv_done, it * NCB + (k + 1))
                    dve.wait_ge(ymask_free, it * NCB + (k + 1))
                    dve.tensor_tensor(ymask[:, k % 2, :].rearrange("p (s n) -> p s n", s=PB),
                                      psum[:, k, :].rearrange("p (s n) -> p s n", s=PB),
                                      mask[:].rearrange("p c b -> p (c b)").unsqueeze(1)
                                      .broadcast_to([P, PB, KC * BATCH]), ALU.mult).then_inc(masked, 1)
                    dve.wait_ge(masked, it * NCB + (k + 1))
                    dve.sem_inc(bank_free, 1)

        @block.scalar
        def _(act):
            act.wait_ge(small_ready, 1)
            act.activation(sk[:, 8, :], sk[:, 7, :], ACT.Sin).then_inc(trig_done, 1)
            act.wait_ge(mag_ready, 1)
            act.activation(mag[:], mag[:], ACT.Exp).then_inc(mag_done, 1)
            act.wait_ge(trig_ready, 1)
            act.activation(theta[:], theta[:], ACT.Sin).then_inc(trig_done, 1)
            with act.Fori(0, SEQ // (PB * NCB)) as it:
                for k in range(NCB):
                    act.wait_ge(masked, it * NCB + (k + 1))
                    for s in range(PB):
                        dst = y_hi[:].rearrange("p c (b s) -> p c b s", s=SEQ)[:, :, :, bass.ds(it * (PB * NCB) + (k * PB + s), 1)]
                        act.activation(dst.rearrange("p c b s -> p c (b s)"), ymask[:, k % 2, s * KC * BATCH:(s + 1) * KC * BATCH]
                                       .rearrange("p (c b) -> p c b", c=KC), ACT.Copy).then_inc(y_hi_done, 1)

        @block.gpsimd
        def _(pool):
            then, tt, ts, _ = chained(pool, pool_step)
            pool.wait_ge(small_ready, 1)
            em1, vers, e1r, e1i, cosb, ur, ui, a, b = (sk[:, i, 0:SEQ] for i in range(9, 18))
            exp_minus_1(then, tt, ts, pool, da, em1, vers, [e1r, e1i, cosb])
            pool.wait_ge(trig_done, 1)
            s1, s2 = sk[:, 8, 0:SEQ], sk[:, 8, SEQ:]
            tt(vers, s2, s2, ALU.mult)
            ts(vers, vers, -2.0, None, ALU.mult)
            ts(cosb, vers, 1.0, None, ALU.add)
            tt(e1r, em1, cosb, ALU.mult)
            tt(e1r, e1r, vers, ALU.add)
            ts(e1i, em1, 1.0, None, ALU.add)
            tt(e1i, e1i, s1, ALU.mult)
            tt(ur, cr, e1r, ALU.mult)
            tt(a, ci, e1i, ALU.mult)
            tt(ur, ur, a, ALU.subtract)
            tt(ui, cr, e1i, ALU.mult)
            tt(a, ci, e1r, ALU.mult)
            tt(ui, ui, a, ALU.add)
            tt(a, ui, ai, ALU.mult)
            tt(b, ur, ar, ALU.mult)
            tt(a, a, b, ALU.subtract)
            tt(a, a, inv, ALU.mult)
            ts(ctr, a, 2.0, None, ALU.mult)
            tt(a, ur, ai, ALU.mult)
            tt(b, ui, ar, ALU.mult)
            tt(a, a, b, ALU.add)
            tt(a, a, inv, ALU.mult)
            ts(cti, a, -2.0, None, ALU.mult)
            pool.sem_inc(ct_ready, 1)
            pool.sem_inc(ymask_free, 2)
            with pool.Fori(0, SEQ // (PB * NCB)) as it:
                for k in range(NCB):
                    for s in range(PB):
                        pool.wait_ge(y_hi_done, it * (PB * NCB) + (k * PB + s + 1))
                        at = bass.ds(it * (PB * NCB) + (k * PB + s), 1)
                        hi = y_hi[:].bitcast(F32).rearrange("p c (b s) -> p c b s", s=SEQ)[:, :, :, at].rearrange("p c b s -> p c (b s)")
                        lo = y_lo[:].rearrange("p c (b s) -> p c b s", s=SEQ)[:, :, :, at].rearrange("p c b s -> p c (b s)")
                        ins = pool.tensor_tensor(lo, ymask[:, k % 2, s * KC * BATCH:(s + 1) * KC * BATCH]
                                                 .rearrange("p (c b) -> p c b", c=KC), hi, ALU.subtract)
                    ins.then_inc(ymask_free, 1)

        @block.tensor
        def _(pe):
            pe.wait_ge(factors_ready, 1)
            for h in range(SEQ):
                mm = pe.matmul(psum[0:LI, h // 16, (h % 16) * LJ:(h % 16 + 1) * LJ],
                               left[:, h, :], right[:, h, :], start=True, stop=True)
            mm.then_inc(kernels_done, 1)
            pe.wait_ge(x_in, 16 * KC)
            with pe.Fori(0, SEQ // (PB * NCB)) as it:
                for k in range(NCB):
                    pe.wait_ge(bank_free, it * NCB + (k + 1))
                    for s in range(PB):
                        h = k * PB + s
                        pe.wait_ge(hankel_in[h % NB], it * (16 * PB * NCB // NB) + 16 * (h // NB + 1))
                        for d in range(KC):
                            n = KC - d
                            u = resid[:].rearrange("p c (b s) -> p c b s", s=SEQ)[:, 0:n, :, bass.ds(it * (PB * NCB) + h, 1)]
                            a = (s * KC + d) * BATCH
                            mm = pe.matmul(psum[:, k, a:a + n * BATCH], hankel[:, h % NB, (KC - 1 - d) * P:(KC - d) * P],
                                           u.rearrange("p c b s -> p c (b s)"), start=(d == 0), stop=(d == KC - 1))
                        if s < PB - 1:
                            mm.then_inc(hankel_free, 1)
                    mm.then_inc(conv_done, 1)


def attention(nc, t, sb, sem, const, mm3, resid, psum, kept, y_hi, y_lo, wraw, raw_loaded):
    STEPS = 2 * NT
    TURNS = GROUPS // 2
    NPJ, NTL = 6, 6
    ctx = ExitStack()
    with ctx:
        w_hi = [kept[:, 0, 0:GW], sb(ctx, "w_hi1", [P, GW], F32R)]
        w_lo = [kept[:, 1, 0:GW], sb(ctx, "w_lo1", [P, GW], F32R)]
        qT = sb(ctx, "qT", [P, GH, TT])
        kT = sb(ctx, "kT", [P, GH, TT])
        v_tok = sb(ctx, "v_tok", [P, SUBS, GH * DH])
        NBK = GH * SUBS
        sc = sb(ctx, "sc", [P, NBK, SEQ])
        ex = sb(ctx, "ex", [P, NBK, SEQ])
        stat = sb(ctx, "stat", [P, 3, NBK])
        probT = sb(ctx, "probT", [P, NBK, P])
        o_hi = sb(ctx, "o_hi", [P, GH, TT], F32R)
        o_lo = sb(ctx, "o_lo", [P, GH, TT], F32R)

        hi_split, lo_split = sem(ctx, "hi_split"), sem(ctx, "lo_split")
        cleared = sem(ctx, "cleared")
        proj_done, proj_free = sem(ctx, "proj_done"), sem(ctx, "proj_free")
        scores_done = sem(ctx, "scores_done")
        shifted, exp_done = sem(ctx, "shifted"), sem(ctx, "exp_done")
        prob_ready, soft_step = sem(ctx, "prob_ready"), sem(ctx, "soft_step")
        pv_done, out_done = sem(ctx, "pv_done"), sem(ctx, "out_done")
        o_hi_done, tail_free = sem(ctx, "o_hi_done"), sem(ctx, "tail_free")
        block = ctx.enter_context(nc.Block())

        def weight(par, off, n=P):
            return w_hi[par][:, off:off + n], w_lo[par][:, off:off + n]

        @block.sync
        def _(sp):
            with sp.Fori(1, GROUPS + 1) as g:
                for p in range(NT):
                    sp.wait_ge(lo_split, g * NT + (p + 1 - NT))
                    sp.dma_start(wraw[:, p * PIECE:(p + 1) * PIECE],
                                 t["attn_w"][bass.ds(g, 1), :, p * PIECE:(p + 1) * PIECE]
                                 .rearrange("g p n -> (g p) n")).then_inc(raw_loaded[p], 16)

        def split_hi(act, group, par, p):
            act.wait_ge(raw_loaded[p], group * 16 + 16)
            act.activation(w_hi[par][:, p * PIECE:(p + 1) * PIECE], wraw[:, p * PIECE:(p + 1) * PIECE],
                           ACT.Copy).then_inc(hi_split, 1)

        @block.gpsimd
        def _(pool):
            pool.memset(probT[:], 0.0).then_inc(cleared, 1)
            pool.memset(v_tok[:], 0.0).then_inc(cleared, 1)
            pool.memset(w_hi[1][:, OOFF:].bitcast(F32), 0.0).then_inc(cleared, 1)
            pool.memset(w_lo[1][:, OOFF:].bitcast(F32), 0.0).then_inc(cleared, 1)

            def split_lo(group, par, p):
                pool.wait_ge(hi_split, group * NT + (p + 1))
                cols = slice(p * PIECE, (p + 1) * PIECE)
                pool.tensor_tensor(w_lo[par][:, cols], wraw[:, cols], w_hi[par][:, cols].bitcast(F32),
                                   ALU.subtract).then_inc(lo_split, 1)

            for p in range(NT):
                split_lo(0, 0, p)
            with pool.Fori(0, TURNS) as it:
                for j in range(STEPS):
                    split_lo(it * 2 + (j // NT + 1), (j // NT + 1) % 2, j % NT)

        @block.scalar
        def _(act):
            def evac_proj(S, e, dst):
                bank = e % 3
                act.wait_ge(proj_done, S * NPJ + (e + 1))
                act.activation(dst, psum[:, bank, :], ACT.Copy).then_inc(proj_free, 1)

            def o_high(S, a):
                act.wait_ge(pv_done, S * GH + (a + 1))
                act.activation(o_hi[:, a, :], psum[:, 5 + a, :], ACT.Copy).then_inc(o_hi_done, 1)

            def steps(it):
                for j in range(STEPS):
                    S = it * STEPS + j
                    evac_proj(S, 0, qT[:, 0, :])
                    evac_proj(S, 1, kT[:, 0, :])
                    o_high(S, 0)
                    o_high(S, 1)
                    evac_proj(S, 2, qT[:, 1, :])
                    split_hi(act, it * 2 + (j // NT + 1), (j // NT + 1) % 2, j % NT)
                    evac_proj(S, 3, kT[:, 1, :])
                    evac_proj(S, 4, v_tok[:, 0:2, :].rearrange("p s n -> p (s n)"))
                    act.wait_ge(shifted, S + 1)
                    act.activation(ex[:], sc[:], ACT.Exp).then_inc(exp_done, 1)
                    evac_proj(S, 5, v_tok[:, 2:4, :].rearrange("p s n -> p (s n)"))

            for p in range(NT):
                split_hi(act, 0, 0, p)
            act.sem_inc(proj_free, 3)
            act.wait_ge(cleared, 2)
            with act.Fori(0, TURNS) as it:
                steps(it)
            o_high(TURNS * STEPS, 0)
            o_high(TURNS * STEPS, 1)

        @block.vector
        def _(dve):
            NSOFT = 5

            def tail(S, tile):
                for a in range(GH):
                    dve.wait_ge(o_hi_done, S * GH + (a + 1))
                    dve.tensor_tensor(o_lo[:, a, :], psum[:, 5 + a, :], o_hi[:, a, :].bitcast(F32),
                                      ALU.subtract).then_inc(tail_free, 1)
                for m in range(KC):
                    bank = 5 + (GH + m) % 3
                    dve.wait_ge(out_done, S * KC + (m + 1))
                    part = resid[:, m, tile * TT:(tile + 1) * TT]
                    dve.tensor_tensor(part, psum[:, bank, :], part, ALU.add).then_inc(tail_free, 1)

            def softmax(S):
                n = [0]

                def then(ins):
                    n[0] += 1
                    ins.then_inc(soft_step, 1)
                    dve.wait_ge(soft_step, S * NSOFT + n[0])

                dve.wait_ge(scores_done, S + 1)
                blocks = psum[:, 3:5, :].rearrange("p a (s n) -> p (a s) n", n=P)
                for b in range(P // SEQ):
                    q = slice(b * SEQ, (b + 1) * SEQ)
                    ins = dve.scalar_tensor_tensor(
                        out=sc[q, :, :], in0=blocks[q, :, b * SEQ:(b + 1) * SEQ], scalar=SCALE0,
                        in1=const("causal_add")[q, :].unsqueeze(1).broadcast_to([SEQ, NBK, SEQ]),
                        op0=ALU.mult, op1=ALU.add)
                then(ins)
                top, total, inv = stat[:, 0, :], stat[:, 1, :], stat[:, 2, :]
                then(dve.tensor_reduce(top, sc[:], AX_X, ALU.max))
                dve.tensor_tensor(sc[:], sc[:], top.unsqueeze(2).broadcast_to([P, NBK, SEQ]),
                                  ALU.subtract).then_inc(shifted, 1)
                dve.wait_ge(exp_done, S + 1)
                then(dve.tensor_reduce(total, ex[:], AX_X, ALU.add))
                then(dve.reciprocal(inv, total))
                then(dve.tensor_tensor(ex[:], ex[:], inv.unsqueeze(2).broadcast_to([P, NBK, SEQ]), ALU.mult))
                for b in range(P // SEQ):
                    q = slice(b * SEQ, (b + 1) * SEQ)
                    ins = dve.transpose(probT[q, :, b * SEQ:(b + 1) * SEQ], ex[q, :, :])
                ins.then_inc(prob_ready, 1)
                assert n[0] == NSOFT

            dve.sem_inc(tail_free, 3)
            dve.wait_ge(cleared, 1)
            dve.sem_inc(prob_ready, 1)
            with dve.Fori(0, TURNS) as it:
                for j in range(STEPS):
                    tail(it * STEPS + j, (j - 1) % NT)
                    softmax(it * STEPS + j)
            tail(TURNS * STEPS, NT - 1)

        @block.tensor
        def _(pe):
            def proj_bank(S, e):
                pe.wait_ge(proj_free, S * NPJ + (e + 1))
                return psum[:, e % 3, :]

            def project(S, e, par, off, tile):
                bank = proj_bank(S, e)
                cols = slice(tile * TT, (tile + 1) * TT)
                for c in range(KC):
                    mm = mm3(pe, bank, weight(par, off + c * GH * DH), (y_hi[:, c, cols], y_lo[:, c, cols]),
                             c == 0, c == KC - 1)
                mm.then_inc(proj_done, 1)

            def values(S, e, par, tile, half):
                bank = proj_bank(S, e)
                for i in range(2):
                    at = tile * TT + (2 * half + i) * P
                    for c in range(KC):
                        out = bank[:, i * GH * DH:(i + 1) * GH * DH]
                        mm = mm3(pe, out, (y_hi[:, c, at:at + P], y_lo[:, c, at:at + P]),
                                 weight(par, VOFF + c * GH * DH, GH * DH), c == 0, c == KC - 1)
                mm.then_inc(proj_done, 1)

            def scores(S, a, e):
                pe.wait_ge(proj_free, S * NPJ + (3 + e + 1))
                for i in range(SUBS):
                    tok = slice(i * P, (i + 1) * P)
                    mm = pe.matmul(psum[:, 3 + a, tok], qT[:, a, tok], kT[:, a, tok], start=True, stop=True)
                if a == GH - 1:
                    mm.then_inc(scores_done, 1)

            def prob_times_v(S):
                for a in range(GH):
                    pe.wait_ge(tail_free, S * NTL + (a + 1))
                    if a == 0:
                        pe.wait_ge(prob_ready, S + 1)
                        pe.wait_ge(proj_free, S * NPJ + 3)
                    for i in range(SUBS):
                        mm = pe.matmul(psum[:, 5 + a, i * P:(i + 1) * P], v_tok[:, i, a * DH:(a + 1) * DH],
                                       probT[:, a * SUBS + i, :], start=True, stop=True)
                    mm.then_inc(pv_done, 1)

            def output(S, par):
                pe.wait_ge(tail_free, S * NTL + (3 + GH))
                for m in range(KC):
                    pe.wait_ge(tail_free, S * NTL + (GH + m + 1))
                    for a in range(GH):
                        mm = mm3(pe, psum[:, 5 + (GH + m) % 3, :], weight(par, OOFF + a * DIM + m * P),
                                 (o_hi[:, a, :], o_lo[:, a, :]), a == 0, a == GH - 1)
                    mm.then_inc(out_done, 1)

            pe.wait_ge(cleared, 4)
            with pe.Fori(0, TURNS) as it:
                for j in range(STEPS):
                    S, par, tile = it * STEPS + j, j // NT, j % NT
                    if tile == 0:
                        pe.wait_ge(lo_split, it * (2 * NT) + (par + 1) * NT)
                    project(S, 0, par, QOFF, tile)
                    project(S, 1, par, KOFF, tile)
                    prob_times_v(S)
                    project(S, 2, par, QOFF + DH, tile)
                    scores(S, 0, 1)
                    output(S, ((j - 1) // NT) % 2)
                    project(S, 3, par, KOFF + DH, tile)
                    values(S, 4, par, tile, 0)
                    scores(S, 1, 3)
                    values(S, 5, par, tile, 1)
            prob_times_v(TURNS * STEPS)
            output(TURNS * STEPS, 1)


def octonion_ffn(nc, t, sb, sem, overlaid, const, mm3, resid, psum, kept_raw, kept, gather_rows):
    ctx = ExitStack()
    with ctx:
        c2_hi, c2_lo = kept[:, 0, 0:C2_COLS], kept[:, 1, 0:C2_COLS]
        up_raw, up = overlaid(ctx, "up", [P, 2, KC, HID])
        down_raw, down = overlaid(ctx, "down", [P, HTP * DIM])
        small = sb(ctx, "small", [P, 24])
        label_i = sb(ctx, "label_i", [P, BATCH], I32)
        label_mask = sb(ctx, "label_mask", [P, 2, BATCH])
        adapter_i = sb(ctx, "adapter_i", [P, BATCH // ABATCH], I32)
        adapter_f = sb(ctx, "adapter_f", [P, BATCH // ABATCH])
        x_hi, x_lo = (sb(ctx, n, [P, KC, TT], F32R) for n in ("x_hi", "x_lo"))
        z_hi = x_hi
        zf, z = overlaid(ctx, "z", [P, KC, TOK])
        rank, rank_lo = overlaid(ctx, "rank_lo", [P, 2, TT])
        rank_hi = sb(ctx, "rank_hi", [P, 2, TT], F32R)
        work, work_r = overlaid(ctx, "work", [P, TERN_COLS])
        base = zf[:, KC - 1, 0:3 * OCT * OH * OD // P].rearrange("p (w n) -> p w n", w=3)
        gate, hid = (work[:, a * 2 * TT:(a + 1) * 2 * TT].rearrange("p (a n) -> p a n", n=TT) for a in (0, 1))
        h_hi, h_lo = (work_r[:, a * 2 * TT:(a + 1) * 2 * TT].rearrange("p (a n) -> p a n", n=TT) for a in (2, 3))

        base_in, tern_in = sem(ctx, "base_in"), [sem(ctx, f"tern_in{i}") for i in range(len(TERN))]
        sums_ready, sums_done = sem(ctx, "sums_ready"), sem(ctx, "sums_done")
        tern_step, tern_ready, signed = sem(ctx, "tern_step"), sem(ctx, "tern_ready"), sem(ctx, "signed")
        x_used, x_hi_done, x_ready = sem(ctx, "x_used"), sem(ctx, "x_hi_done"), sem(ctx, "x_ready")
        rank_done, masked, rank_hi_done, rank_ready = (sem(ctx, n) for n in ("rank_done", "masked", "rank_hi_done", "rank_ready"))
        z_done, z_saved = sem(ctx, "z_done"), sem(ctx, "z_saved")
        z_hi_done, z_ready = sem(ctx, "z_hi_done"), sem(ctx, "z_ready")
        up_done, gate_done, hid_done, h_hi_done, h_ready = (
            sem(ctx, n) for n in ("up_done", "gate_done", "hid_done", "h_hi_done", "h_ready"))
        down_done, down_free = sem(ctx, "down_done"), sem(ctx, "down_free")
        raw_in = sem(ctx, "l1_raw_in")
        passed = sem(ctx, "ffn_passed")
        adapter_in, adapter_step = sem(ctx, "adapter_in"), sem(ctx, "adapter_step")
        A_OFF, B_OFF = KC * DIM, KC * DIM + KC * 2 * P
        NSUM, NT_TERN = 7, 2 * len(TERN)

        def c2(off, n=P):
            return c2_hi[:, off:off + n], c2_lo[:, off:off + n]

        def piece(k):
            return work[:, TERN[k][0]:TERN[k][0] + TERN[k][1]]

        def tern_dst(k, tile, up, down):
            if k < 2:
                return up[:, k, bass.ds(tile, 1), :].rearrange("p c n -> p (c n)")
            w = TERN[k][1]
            return down[:, bass.ds(tile * (2 * w) + (k - 2) * w, w)]

        def cols(a, c, tile):
            return a[:, c, bass.ds(tile * TT, TT)]

        s_gate, s_up, s_down = small[:, 10:11], small[:, 11:12], small[:, 12:13]
        with nc.Block() as block:
            @block.sync
            def _(sp):
                sp.dma_start(small[:, 0:4], t["c2_bias"]).then_inc(base_in, 16)
                sp.dma_start(label_i[:], t["labels"]).then_inc(base_in, 16)
                sp.dma_start(adapter_i[:], t["adapters"]).then_inc(adapter_in, 16)
                sp.dma_start(base, t["oct_base"]).then_inc(base_in, 16)

                def load(tile, k):
                    a, w = TERN[k]
                    sp.dma_start(piece(k), t["oct_w"][bass.ds(tile, 1), :, a:a + w].rearrange("g p n -> (g p) n")
                                 ).then_inc(tern_in[k], 16)

                for k in range(len(TERN)):
                    load(0, k)
                with sp.Fori(1, NT) as tile:
                    for k in range(len(TERN)):
                        sp.wait_ge(tern_ready, tile * len(TERN) + (k + 1 - len(TERN)))
                        load(tile, k)
                sp.wait_ge(z_done, NT * KC)
                raw = kept_raw[:].rearrange("p a n -> p (a n)")
                for a, b in L1_PIECES:
                    sp.dma_start(raw[:, a:b], t["l1_w"][:, a:b]).then_inc(raw_in, 16)
                sp.wait_ge(raw_in, 16 * len(L1_PIECES))

            @block.scalar
            def _(act):
                def x_high(tile):
                    for c in range(KC):
                        wait_apart(act, x_used, tile * KC + (c + 1), passed)
                        act.activation(x_hi[:, c, :], cols(resid, c, tile), ACT.Copy).then_inc(x_hi_done, 1)

                def z_high(tile, c):
                    if c == 0:
                        wait_apart(act, up_done, tile * HT, passed)
                    act.activation(z_hi[:, c, :], cols(zf, c, tile), ACT.Copy).then_inc(z_hi_done, 1)

                def ranks_high(tile):
                    for k in range(2):
                        act.wait_ge(masked, tile * 2 + (k + 1))
                        act.activation(rank_hi[:, k, :], rank[:, k, :], ACT.Copy).then_inc(rank_hi_done, 1)

                def save_z(tile):
                    for m in range(KC):
                        wait_apart(act, z_done, tile * KC + (m + 1), passed)
                        act.activation(cols(zf, m, tile), psum[:, 4 + m, :], ACT.Identity,
                                       bias=small[:, m:m + 1]).then_inc(z_saved, 1)

                def hidden(tile, last):
                    for h in range(HT):
                        r = min(P, HID - h * P)
                        act.wait_ge(up_done, tile * HT + (h + 1))
                        act.activation(gate[0:r, h % 2, :], psum[0:r, 2 * (h % 2), :], ACT.Silu,
                                       scale=s_gate[0:r, :]).then_inc(gate_done, 1)
                        if h == HT - 1 and not last:
                            z_high(tile + 1, 0)
                        act.wait_ge(hid_done, tile * HT + (h + 1))
                        act.activation(h_hi[0:r, h % 2, :], hid[0:r, h % 2, :], ACT.Copy).then_inc(h_hi_done, 1)
                    if not last:
                        for c in range(1, KC):
                            z_high(tile + 1, c)

                act.sem_inc(z_saved, KC)
                x_high(0)
                act.wait_ge(sums_ready, 1)
                with act.Fori(0, NT - 1) as tile:
                    ranks_high(tile)
                    x_high(tile + 1)
                    save_z(tile)
                ranks_high(NT - 1)
                act.wait_ge(x_used, KC * (NT + 1))
                for c in range(KC):
                    act.activation(z_hi[:, c, :], zf[:, c, 0:TT], ACT.Copy).then_inc(z_hi_done, 1)
                save_z(NT - 1)
                with act.Fori(0, NT - 1) as tile:
                    hidden(tile, False)
                hidden(NT - 1, True)

            @block.vector
            def _(dve):
                n = [0]

                def then(ins, before=0):
                    n[0] += 1
                    ins.then_inc(tern_step, 1)
                    dve.wait_ge(tern_step, before + n[0])

                def x_low(tile):
                    for c in range(KC):
                        dve.wait_ge(x_hi_done, tile * KC + (c + 1))
                        dve.tensor_tensor(x_lo[:, c, :], cols(resid, c, tile),
                                          x_hi[:, c, :].bitcast(F32), ALU.subtract).then_inc(x_ready, 1)

                def z_low(tile, c):
                    dve.wait_ge(z_hi_done, tile * KC + (c + 1))
                    dve.tensor_tensor(cols(z, c, tile), cols(zf, c, tile), z_hi[:, c, :].bitcast(F32),
                                      ALU.subtract).then_inc(z_ready, 1)

                x_low(0)
                dve.wait_ge(base_in, 48)
                then(dve.tensor_reduce(small[:, 4:7], base, AX_X, ALU.add, apply_absolute_value=True))
                dve.sem_inc(sums_ready, 1)
                then(dve.tensor_copy(label_mask[:, 0, :], label_i[:]))
                for k in (1, 0):
                    then(dve.tensor_scalar(label_mask[:, k, :], label_mask[:, 0, :], const("labeler")[:, k:k + 1],
                                           0.5, ALU.is_equal, ALU.mult))
                assert n[0] == 4

                def ternary(tile, k):
                    w = min(k, 2)
                    dve.wait_ge(tern_in[k], tile * 16 + 16)
                    before = tile * NT_TERN + NSUM
                    n[0] = 2 * k
                    dst = tern_dst(k, tile, up_raw, down_raw)
                    then(dve.tensor_scalar(dst, piece(k), small[:, 13 + w:14 + w], None, ALU.is_gt), before)
                    then(dve.scalar_tensor_tensor(out=dst, in0=piece(k), scalar=small[:, 16 + w:17 + w],
                                                  in1=dst, op0=ALU.is_lt, op1=ALU.subtract), before)
                    dve.sem_inc(tern_ready, 1)

                def ranks(tile):
                    for k in range(2):
                        dve.wait_ge(rank_done, tile * 2 + (k + 1))
                        own = label_mask[:, k, bass.ds(tile * BPT, BPT)].unsqueeze(2).broadcast_to([P, BPT, SEQ])
                        dve.tensor_tensor(rank[:, k, :].rearrange("p (b s) -> p b s", s=SEQ),
                                          psum[:, k, :].rearrange("p (b s) -> p b s", s=SEQ), own,
                                          ALU.mult).then_inc(masked, 1)
                        dve.wait_ge(rank_hi_done, tile * 2 + (k + 1))
                        dve.tensor_tensor(rank_lo[:, k, :], rank[:, k, :], rank_hi[:, k, :].bitcast(F32),
                                          ALU.subtract).then_inc(rank_ready, 1)

                def hidden(tile, last):
                    for h in range(HT):
                        r = min(P, HID - h * P)
                        dve.wait_ge(gate_done, tile * HT + (h + 1))
                        dve.scalar_tensor_tensor(out=hid[0:r, h % 2, :], in0=psum[0:r, 2 * (h % 2) + 1, :],
                                                 scalar=s_up[0:r, :], in1=gate[0:r, h % 2, :],
                                                 op0=ALU.mult, op1=ALU.mult).then_inc(hid_done, 1)
                        dve.wait_ge(h_hi_done, tile * HT + (h + 1))
                        dve.tensor_tensor(h_lo[0:r, h % 2, :], hid[0:r, h % 2, :], h_hi[0:r, h % 2, :].bitcast(F32),
                                          ALU.subtract).then_inc(h_ready, 1)
                    if not last:
                        for c in range(KC):
                            z_low(tile + 1, c)
                    for m in range(KC):
                        dve.wait_ge(down_done, tile + 1)
                        part = cols(resid, m, tile)
                        dve.scalar_tensor_tensor(out=part, in0=psum[:, 4 + m, :], scalar=s_down, in1=part,
                                                 op0=ALU.mult, op1=ALU.add).then_inc(down_free, 1)

                ranks(0)
                dve.wait_ge(sums_done, 1)
                count = float(OCT * OH * OD)
                then(dve.tensor_scalar(small[:, 10:13], psum[:, 2, 0:3], 1.0 / count, None, ALU.mult))
                then(dve.tensor_scalar(small[:, 13:16], small[:, 10:13], 0.5, None, ALU.mult))
                then(dve.tensor_scalar(small[:, 16:19], small[:, 10:13], -0.5, None, ALU.mult))
                assert n[0] == NSUM
                for k in range(len(TERN)):
                    ternary(0, k)
                x_low(1)
                with dve.Fori(1, NT - 1) as tile:
                    ranks(tile)
                    for k in range(len(TERN)):
                        ternary(tile, k)
                    x_low(tile + 1)
                ranks(NT - 1)
                for k in range(len(TERN)):
                    ternary(NT - 1, k)
                for c in range(KC):
                    z_low(0, c)
                dve.sem_inc(down_free, KC)
                with dve.Fori(0, NT - 1) as tile:
                    hidden(tile, False)
                hidden(NT - 1, True)

            @block.gpsimd
            def _(pool):
                with pool.Fori(0, NT) as tile:
                    for k in range(len(TERN)):
                        pool.wait_ge(tern_ready, tile * len(TERN) + (k + 1))
                        w = TERN[k][1]
                        src, dst = tern_dst(k, tile, up_raw, down_raw), tern_dst(k, tile, up, down)
                        if k < 2:
                            run, sign = OH, const("sign_up")[:, bass.ds(tile * OCT, OCT)]
                        else:
                            run, sign = OD, const("sign_down")[:, bass.ds(tile * (2 * w // OD) + (k - 2) * (w // OD), w // OD)]
                        pool.tensor_tensor(dst.rearrange("p (k o) -> p k o", o=run),
                                           src.rearrange("p (k o) -> p k o", o=run),
                                           sign.unsqueeze(2).broadcast_to([P, w // run, run]), ALU.mult).then_inc(signed, 1)
                then, _, ts, _ = chained(pool, adapter_step)
                pool.wait_ge(adapter_in, 16)
                then(pool.tensor_copy(adapter_f[:], adapter_i[:]))
                ts(adapter_f[:], adapter_f[:], 0.0, ADA - 1.0, ALU.max, ALU.min)
                ts(adapter_f[:], adapter_f[:], float(AR), const("adapter_rank"), ALU.mult, ALU.add)
                then(pool.tensor_copy(gather_rows[:], adapter_f[:]))

            @block.tensor
            def _(pe):
                def lora_layer(tile, first):
                    for c in range(KC):
                        pe.wait_ge(x_ready, tile * KC + (c + 1))
                        x = x_hi[:, c, :], x_lo[:, c, :]
                        for k in range(2):
                            mm = mm3(pe, psum[:, k, :], c2(A_OFF + c * 2 * P + k * P), x, c == 0, c == KC - 1)
                            if c == KC - 1:
                                mm.then_inc(rank_done, 1)
                    for c in range(KC):
                        x = x_hi[:, c, :], x_lo[:, c, :]
                        for m in range(KC):
                            if c == 0:
                                pe.wait_ge(z_saved, tile * KC + (m + 1))
                            mm = mm3(pe, psum[:, 4 + m, :], c2(c * DIM + m * P), x, c == 0, False)
                        mm.then_inc(x_used, 1)
                    if first:
                        pe.wait_ge(sums_ready, 1)
                        pe.matmul(psum[:, 2, 0:3], const("ones"), small[:, 4:7], start=True, stop=True).then_inc(sums_done, 1)
                    for k in range(2):
                        pe.wait_ge(rank_ready, tile * 2 + (k + 1))
                        for m in range(KC):
                            mm = mm3(pe, psum[:, 4 + m, :], c2(B_OFF + m * P), (rank_hi[:, k, :], rank_lo[:, k, :]),
                                     False, k == 1)
                            if k == 1:
                                mm.then_inc(z_done, 1)

                pe.sem_inc(x_used, KC)
                lora_layer(0, True)
                with pe.Fori(1, NT) as tile:
                    lora_layer(tile, False)
                pe.wait_ge(signed, NT * len(TERN))
                pe.wait_ge(z_saved, KC * (NT + 1))
                with pe.Fori(0, NT) as tile:
                    def gate_up(h):
                        r = min(P, HID - h * P)
                        for c in range(KC):
                            if h == 0:
                                pe.wait_ge(z_ready, tile * KC + (c + 1))
                            for w in range(2):
                                out = psum[0:r, 2 * (h % 2) + w, :]
                                wt = up[:, w, c, h * P:h * P + r]
                                pe.matmul(out, wt, z_hi[:, c, :], start=(c == 0), stop=False)
                                mm = pe.matmul(out, wt, cols(z, c, tile), start=False, stop=(c == KC - 1))
                        mm.then_inc(up_done, 1)

                    def down_product(h):
                        r = min(P, HID - h * P)
                        pe.wait_ge(h_ready, tile * HT + (h + 1))
                        for m in range(KC):
                            if h == 0:
                                pe.wait_ge(down_free, tile * KC + (m + 1))
                            wt = down[0:r, h * DIM + m * P:h * DIM + (m + 1) * P]
                            pe.matmul(psum[:, 4 + m, :], wt, h_hi[0:r, h % 2, :], start=(h == 0), stop=False)
                            mm = pe.matmul(psum[:, 4 + m, :], wt, h_lo[0:r, h % 2, :], start=False, stop=(h == HT - 1))
                        if h == HT - 1:
                            mm.then_inc(down_done, 1)

                    gate_up(0)
                    for h in range(1, HT):
                        gate_up(h)
                        down_product(h - 1)
                    down_product(HT - 1)


def layer_one(nc, t, sb, sem, const, mm3, resid, psum, kept_raw, kept, gather_rows):
    ctx = ExitStack()
    with ctx:
        w_raw = kept_raw[:].rearrange("p a n -> p (a n)")
        w_lo = kept[:].rearrange("p a n -> p (a n)")
        w_hi = sb(ctx, "w1_hi", [P, L1_COLS], F32R)
        x_hi, x_lo = (sb(ctx, n, [P, KC, TT], F32R) for n in ("x1_hi", "x1_lo"))
        r_hi, r_lo = (sb(ctx, n, [P, TT], F32R) for n in ("r_hi", "r_lo"))
        wide = sb(ctx, "wide", [P, KC, TT])
        misc = sb(ctx, "misc", [P, 8, TT])
        rank, gate_T = misc[:, 0, :], misc[:, 1, :]
        bound, tok, att = misc[:, 2:4, :], misc[:, 4:6, :], misc[:, 6:8, :]
        logit_rows = sb(ctx, "logit_rows", [NE, TT])
        a_raw, b_raw = (sb(ctx, n, [P, AGROUPS, DIM]) for n in ("a_raw", "b_raw"))
        a_hi, a_lo, b_hi, b_lo = (sb(ctx, n, [P, AGROUPS, DIM], F32R) for n in ("a_hi", "a_lo", "b_hi", "b_lo"))
        rows_now = sb(ctx, "rows_now", [P, AGROUPS], U32)
        small = sb(ctx, "small1", [P, 96])
        ids_i = sb(ctx, "ids_i", [P, TOK // P], I32)
        ids = sb(ctx, "ids", [P, TOK // P])
        lang = sb(ctx, "lang", [P, TOK // P, NE])
        gat = sb(ctx, "gat", [P, 12, SUBS * NE])
        gat_i = sb(ctx, "gat_i", [P, SUBS * NE], U32)
        spread = sb(ctx, "spread", [P, SUBS, NE, ER])

        small_in = sem(ctx, "small_in")
        l1_hi_done, l1_ready, prep_step = sem(ctx, "l1_hi_done"), sem(ctx, "l1_ready"), sem(ctx, "prep_step")
        sums_done, bindings_ready = sem(ctx, "sums1_done"), sem(ctx, "bindings_ready")
        rows_copied, gathered = sem(ctx, "rows_copied"), sem(ctx, "gathered")
        a_turned, a_hi_done, a_ready = sem(ctx, "a_turned"), sem(ctx, "a_hi_done"), sem(ctx, "a_ready")
        b_hi_done, b_ready = sem(ctx, "b_hi_done"), sem(ctx, "b_ready")
        x_used, x0_ready = sem(ctx, "x1_used"), sem(ctx, "x0_ready")
        x_hi_done, x_ready = sem(ctx, "x1_hi_done"), sem(ctx, "x1_ready")
        rank_done, rank_masked = sem(ctx, "rank1_done"), sem(ctx, "rank_masked")
        r_hi_done, r_ready = sem(ctx, "r_hi_done"), sem(ctx, "r_ready")
        base_done, wide_done, bound_done = sem(ctx, "base_done"), sem(ctx, "wide_done"), sem(ctx, "bound_done")
        wide_free = sem(ctx, "wide_free")
        rows_done, rows_saved = sem(ctx, "rows_done"), sem(ctx, "rows_saved")
        turned, tok_done, s_done, sig_done, att_done = (
            sem(ctx, n) for n in ("turned", "tok_done", "s_done", "sig_done", "att_done"))
        pv_done, resid_done = sem(ctx, "pv1_done"), sem(ctx, "resid_done")
        logits_done, gate_step, e_done = sem(ctx, "logits_done"), sem(ctx, "gate_step"), sem(ctx, "e_done")
        spread_done, gateT_done, gateT_copied = sem(ctx, "spread_done"), sem(ctx, "gateT_done"), sem(ctx, "gateT_copied")
        h_done, gated, g_hi_done, g_ready = (sem(ctx, n) for n in ("h_done", "gated", "g_hi_done", "g_ready"))
        moe_done, c_hi_done, c_ready = sem(ctx, "moe_done"), sem(ctx, "c_hi_done"), sem(ctx, "c_ready")
        out_ready, out_stored = sem(ctx, "out_ready"), sem(ctx, "out_stored")
        act_passed, dve_passed = sem(ctx, "act_passed"), sem(ctx, "dve_passed")
        pool_passed, pe_passed = sem(ctx, "pool_passed"), sem(ctx, "pe_passed")

        def wt(block, off, n=P):
            a = L1_AT[block] + off
            return w_hi[:, a:a + n], w_lo[:, a:a + n]

        def mine(tile, m):
            return resid[:, m, bass.ds(tile * TT, TT)]

        NG, NS = 19, 20
        NM = 2
        with nc.Block() as block:
            @block.sync
            def _(sp):
                sp.dma_start(small[:, 0:32], t["l1_small"]).then_inc(small_in, 16)
                sp.dma_start(small[:, 68:76], t["router_bias"]).then_inc(small_in, 16)
                sp.dma_start(ids_i[:], t["languages"]).then_inc(small_in, 16)
                sp.sem_inc(wide_free, 1)
                with sp.Fori(0, NT) as tile:
                    for m in range(KC):
                        sp.wait_ge(out_ready, tile * KC + (KC + m + 1))
                        sp.dma_start(t["out"][m * P:(m + 1) * P, bass.ds(tile * TT, TT)], wide[:, m, :]).then_inc(out_stored, 16)
                    sp.wait_ge(out_stored, tile * (16 * KC) + 16 * KC)
                    sp.sem_inc(wide_free, 1)

            @block.gpsimd
            def _(pool):
                def gather(tile):
                    pool.tensor_copy(rows_now[:], gather_rows[:, bass.ds(tile * AGROUPS, AGROUPS)]).then_inc(rows_copied, 1)
                    wait_apart(pool, rows_copied, tile + 1, pool_passed)
                    for g in range(AGROUPS):
                        for dst, src in ((a_raw, t["ada_a"]), (b_raw, t["ada_b"])):
                            pool.indirect_dma_start(
                                out=dst[:, g, :], out_offset=None, in_=src,
                                in_offset=bass.IndirectOffsetOnAxis(ap=rows_now[:, g:g + 1], axis=0)).then_inc(gathered, 16)

                def low_parts(tile):
                    for c in range(KC):
                        pool.wait_ge(x_hi_done, tile * 2 * KC + (c + 1))
                        pool.tensor_tensor(x_lo[:, c, :], mine(tile, c), x_hi[:, c, :].bitcast(F32),
                                           ALU.subtract).then_inc(x0_ready, 1)
                    pool.wait_ge(b_hi_done, tile + 1)
                    pool.tensor_tensor(b_lo[:], b_raw[:], b_hi[:].bitcast(F32), ALU.subtract).then_inc(b_ready, 1)

                gather(0)
                with pool.Fori(0, NT - 1) as tile:
                    low_parts(tile)
                    pool.wait_ge(b_ready, tile + 1)
                    pool.wait_ge(a_turned, tile * AGROUPS + AGROUPS)
                    pool.wait_ge(gathered, tile * GATHERED + GATHERED)
                    gather(tile + 1)
                low_parts(NT - 1)

            @block.scalar
            def _(act):
                for a, b in L1_PIECES[:1]:
                    act.activation(w_hi[:, a:b], w_raw[:, a:b], ACT.Copy).then_inc(l1_hi_done, 1)
                with act.Fori(0, NT) as tile:
                    for c in range(KC):
                        wait_apart(act, x_used, tile * KC + (c + 1), act_passed)
                        act.activation(x_hi[:, c, :], mine(tile, c), ACT.Copy).then_inc(x_hi_done, 1)
                    for g in range(AGROUPS):
                        act.wait_ge(a_turned, tile * AGROUPS + (g + 1))
                        act.activation(a_hi[:, g, :], psum[:, g, :], ACT.Copy).then_inc(a_hi_done, 1)
                    act.wait_ge(gathered, tile * GATHERED + GATHERED)
                    act.activation(b_hi[:], b_raw[:], ACT.Copy).then_inc(b_hi_done, 1)
                    act.wait_ge(rank_masked, tile + 1)
                    act.activation(r_hi[:], rank, ACT.Copy).then_inc(r_hi_done, 1)
                    for m in range(KC):
                        act.wait_ge(base_done, tile * KC + (m + 1))
                        if m == 0:
                            act.wait_ge(wide_free, tile + 1)
                        act.activation(wide[:, m, :], psum[:, 4 + m, :], ACT.Identity,
                                       bias=small[:, m:m + 1]).then_inc(wide_done, 1)
                    for m in range(KC):
                        act.wait_ge(turned, tile * KC + (m + 1))
                        act.activation(tok[:, m % 2, :], psum[:, m % 2, :], ACT.Copy).then_inc(tok_done, 1)
                        act.wait_ge(s_done, tile * KC + (m + 1))
                        act.activation(att[:, m % 2, :], psum[:, 2 + m % 2, :], ACT.Sigmoid,
                                       scale=SCALE1).then_inc(sig_done, 1)
                    for m in range(KC):
                        wait_apart(act, resid_done, tile * KC + (m + 1), act_passed)
                        act.activation(x_hi[:, m, :], mine(tile, m), ACT.Copy).then_inc(x_hi_done, 1)
                    for layer in range(NM):
                        act.wait_ge(rows_done, tile * NM + (layer + 1))
                        act.activation(logit_rows[:], psum[0:NE, 3, :], ACT.Copy).then_inc(rows_saved, 1)
                        if layer == 0:
                            act.wait_ge(gate_step, tile * (NG + NS) + 11)
                            act.activation(gat[:, 2, 0:SUBS], gat[:, 2, 0:SUBS], ACT.Exp).then_inc(e_done, 1)
                        act.wait_ge(gateT_done, tile * NM + (layer + 1))
                        act.activation(gate_T, psum[:, 2, :], ACT.Copy).then_inc(gateT_copied, 1)
                        act.wait_ge(gated, tile * NM + (layer + 1))
                        act.activation(r_hi[:], rank, ACT.Copy).then_inc(g_hi_done, 1)
                        if layer == 0:
                            for m in range(KC):
                                act.wait_ge(moe_done, tile * KC * NM + (m + 1))
                                act.activation(x_hi[:, m, :], psum[:, 4 + m, :], ACT.Copy).then_inc(c_hi_done, 1)

            @block.vector
            def _(dve):
                def gate_chain(tile, first):
                    k = [0]

                    def then(*several):
                        for ins in several:
                            k[0] += 1
                            ins.then_inc(gate_step, 1)
                        dve.wait_ge(gate_step, tile * (NG + NS) + (first + k[0]))
                    return then, k

                def g(i, n=NE):
                    return gat[:, i, 0:SUBS * n].rearrange("p (s e) -> p s e", s=SUBS)

                def per(a):
                    return a.unsqueeze(2).broadcast_to([P, SUBS, NE])

                def row(a):
                    return a.unsqueeze(1).broadcast_to([P, SUBS, NE])

                def tt(then, out, a, b, op):
                    then(dve.tensor_tensor(out, a, b, op))

                def top2_gates(tile):
                    then, k = gate_chain(tile, 0)
                    dve.wait_ge(logits_done, tile * NM + 1)
                    lg, top, hot, gates = g(0), g(1), g(4), g(5)
                    tt(then, lg, psum[:, 0, 0:SUBS * NE].rearrange("p (s e) -> p s e", s=SUBS),
                       lang[:, bass.ds(tile * SUBS, SUBS), :], ALU.add)
                    dve.sem_inc(dve_passed, 1)
                    then(*[dve.max(top[:, s, :], lg[:, s, :]) for s in range(SUBS)])
                    dve.sem_inc(dve_passed, 1)
                    then(*[dve.max_index(gat_i[:, s * NE:(s + 1) * NE], top[:, s, :], lg[:, s, :]) for s in range(SUBS)])
                    then(dve.tensor_copy(g(6), gat_i[:].rearrange("p (s e) -> p s e", s=SUBS)))
                    e2, w1, w2 = gat[:, 2, 0:SUBS], gat[:, 3, 0:SUBS], gat[:, 3, SUBS:2 * SUBS]
                    tt(then, e2, top[:, :, 1], top[:, :, 0], ALU.subtract)
                    dve.wait_ge(e_done, tile + 1)
                    then(dve.tensor_scalar(w1, e2, 1.0, 0.5, ALU.add, ALU.mult))
                    then(dve.reciprocal(w1, w1))
                    tt(then, w2, w1, e2, ALU.mult)
                    tt(then, hot, row(const("iota")), per(g(6)[:, :, 0]), ALU.is_equal)
                    tt(then, gates, hot, per(w1), ALU.mult)
                    tt(then, hot, row(const("iota")), per(g(6)[:, :, 1]), ALU.is_equal)
                    tt(then, hot, hot, per(w2), ALU.mult)
                    tt(then, gates, gates, hot, ALU.add)
                    assert k[0] == NG, k
                    return gates

                def sparsemax_gates(tile):
                    then, k = gate_chain(tile, NG)
                    dve.wait_ge(logits_done, tile * NM + 2)
                    z, srt, cum, alt, sup = g(0), g(1), g(4), g(5), g(6)
                    tt(then, z, psum[:, 0, SUBS * NE:2 * SUBS * NE].rearrange("p (s e) -> p s e", s=SUBS),
                       row(small[:, 68:76]), ALU.add)
                    dve.sem_inc(dve_passed, 1)
                    then(*[dve.max(srt[:, s, :], z[:, s, :]) for s in range(SUBS)])
                    src = srt
                    for d, dst in ((1, cum), (2, alt), (4, cum)):
                        then(dve.tensor_copy(dst[:, :, 0:d], src[:, :, 0:d]))
                        tt(then, dst[:, :, d:], src[:, :, d:], src[:, :, 0:NE - d], ALU.add)
                        src = dst
                    tt(then, alt, srt, row(const("count")), ALU.mult)
                    then(dve.scalar_tensor_tensor(out=sup, in0=alt, scalar=1.0, in1=cum, op0=ALU.add, op1=ALU.is_gt))
                    kz, ts_, tau = gat[:, 2, 0:SUBS], gat[:, 2, SUBS:2 * SUBS], gat[:, 3, 0:SUBS]
                    then(dve.tensor_reduce(kz, sup, AX_X, ALU.add))
                    tt(then, alt, row(const("count")), per(kz), ALU.is_equal)
                    tt(then, alt, alt, cum, ALU.mult)
                    then(dve.tensor_reduce(ts_, alt, AX_X, ALU.add))
                    then(dve.reciprocal(kz, kz))
                    then(dve.scalar_tensor_tensor(out=tau, in0=ts_, scalar=-1.0, in1=kz, op0=ALU.add, op1=ALU.mult))
                    tt(then, z, z, per(tau), ALU.subtract)
                    assert k[0] == NS, k
                    return z

                def mask_att(dve, tile, m):
                    dve.wait_ge(sig_done, tile * KC + (m + 1))
                    dve.tensor_tensor(att[:, m % 2, :].rearrange("p (s n) -> p s n", n=P),
                                      att[:, m % 2, :].rearrange("p (s n) -> p s n", n=P),
                                      const("causal_mul").unsqueeze(1).broadcast_to([P, SUBS, P]),
                                      ALU.mult).then_inc(att_done, 1)

                def add_attention(dve, tile, m):
                    dve.wait_ge(pv_done, tile * KC + (m + 1))
                    dve.scalar_tensor_tensor(out=mine(tile, m), in0=psum[:, 4 + m, :], scalar=small[:, 12 + m:13 + m],
                                             in1=mine(tile, m), op0=ALU.mult, op1=ALU.add).then_inc(resid_done, 1)
                    dve.wait_ge(x_hi_done, tile * 2 * KC + (KC + m + 1))
                    dve.tensor_tensor(x_lo[:, m, :], mine(tile, m), x_hi[:, m, :].bitcast(F32),
                                      ALU.subtract).then_inc(x_ready, 1)

                dve.sem_inc(out_ready, KC)
                for k, (a, b) in enumerate(L1_PIECES):
                    if k == 0:
                        dve.wait_ge(l1_hi_done, 1)
                    else:
                        dve.tensor_copy(w_hi[:, a:b], w_raw[:, a:b]).then_inc(prep_step, 1)
                        dve.wait_ge(prep_step, k)
                    for q in range(a, b, DIM):
                        e = min(q + DIM, b)
                        ins = dve.tensor_tensor(w_lo[:, q:e], w_raw[:, q:e], w_hi[:, q:e].bitcast(F32), ALU.subtract)
                        ins.then_inc(l1_ready, 1)
                n = [len(L1_PIECES) - 1]

                def prep(ins):
                    n[0] += 1
                    ins.then_inc(prep_step, 1)
                    dve.wait_ge(prep_step, n[0])

                dve.wait_ge(small_in, 48)
                prep(dve.scalar_tensor_tensor(out=small[:, 32:44], in0=small[:, 20:32], scalar=-1.0,
                                              in1=small[:, 20:32], op0=ALU.mult, op1=ALU.max))
                prep(dve.tensor_scalar(small[:, 44:56], small[:, 20:32], 0.0, 2.0, ALU.is_ge, ALU.mult))
                prep(dve.tensor_scalar(small[:, 44:56], small[:, 44:56], 1.0, None, ALU.subtract))
                dve.sem_inc(bindings_ready, 1)
                prep(dve.tensor_copy(ids[:], ids_i[:]))
                prep(dve.tensor_tensor(lang[:], ids[:].unsqueeze(2).broadcast_to([P, TOK // P, NE]),
                                       const("iota").unsqueeze(1).broadcast_to([P, TOK // P, NE]), ALU.is_equal))
                prep(dve.tensor_scalar(lang[:], lang[:], 5.0, None, ALU.mult))

                def adapter_ranks(tile):
                    for g in range(AGROUPS):
                        dve.wait_ge(a_hi_done, tile * AGROUPS + (g + 1))
                        dve.tensor_tensor(a_lo[:, g, :], psum[:, g, :], a_hi[:, g, :].bitcast(F32),
                                          ALU.subtract).then_inc(a_ready, 1)
                    dve.wait_ge(rank_done, tile + 1)
                    dve.tensor_tensor(rank.rearrange("p (b s) -> p b s", s=SEQ),
                                      psum[:, 2, :].rearrange("p (b s) -> p b s", s=SEQ),
                                      const("own_batch").unsqueeze(2).broadcast_to([P, BPT, SEQ]),
                                      ALU.mult).then_inc(rank_masked, 1)
                    dve.wait_ge(r_hi_done, tile + 1)
                    dve.tensor_tensor(r_lo[:], rank, r_hi[:].bitcast(F32), ALU.subtract).then_inc(r_ready, 1)

                def bindings():
                    dve.wait_ge(sums_done, 1)
                    prep(dve.scalar_tensor_tensor(out=small[:, 56:68], in0=psum[:, 3, 0:12], scalar=1.0 / P,
                                                  in1=small[:, 44:56], op0=ALU.mult, op1=ALU.mult))
                    prep(dve.tensor_tensor(small[:, 8:12], small[:, 56:60], small[:, 60:64], ALU.mult))
                    prep(dve.tensor_copy(small[:, 12:16], small[:, 64:68]))

                bindings()
                with dve.Fori(0, NT) as tile:
                    adapter_ranks(tile)
                    for m in range(KC):
                        dve.wait_ge(wide_done, tile * KC + (m + 1))
                        if m >= 2:
                            dve.wait_ge(s_done, tile * KC + (m - 1))
                        dve.tensor_scalar(bound[:, m % 2, :], wide[:, m, :], small[:, 8 + m:9 + m], None,
                                          ALU.mult).then_inc(bound_done, 1)
                        if m >= 1:
                            mask_att(dve, tile, m - 1)
                    mask_att(dve, tile, KC - 1)
                    for m in range(KC):
                        add_attention(dve, tile, m)
                    for layer, gates_of in enumerate((top2_gates, sparsemax_gates)):
                        gates = gates_of(tile)
                        wide_gates = gates.unsqueeze(3).broadcast_to([P, SUBS, NE, ER])
                        if layer == 0:
                            dve.tensor_copy(spread[:], wide_gates).then_inc(spread_done, 1)
                        else:
                            dve.tensor_scalar(spread[:], wide_gates, 0.0, None, ALU.max).then_inc(spread_done, 1)
                        dve.wait_ge(h_done, tile * NM + (layer + 1))
                        dve.wait_ge(gateT_copied, tile * NM + (layer + 1))
                        dve.tensor_tensor(rank, psum[:, 1, :], gate_T, ALU.mult).then_inc(gated, 1)
                        dve.wait_ge(g_hi_done, tile * NM + (layer + 1))
                        dve.tensor_tensor(r_lo[:], rank, r_hi[:].bitcast(F32),
                                          ALU.subtract).then_inc(g_ready, 1)
                        for m in range(KC):
                            if layer == 0:
                                dve.wait_ge(c_hi_done, tile * KC + (m + 1))
                                dve.tensor_tensor(x_lo[:, m, :], psum[:, 4 + m, :], x_hi[:, m, :].bitcast(F32),
                                                  ALU.subtract).then_inc(c_ready, 1)
                            else:
                                dve.wait_ge(moe_done, tile * KC * NM + (KC + m + 1))
                                dve.scalar_tensor_tensor(out=wide[:, m, :], in0=psum[:, 4 + m, :],
                                                         scalar=small[:, 4 + m:5 + m], in1=mine(tile, m),
                                                         op0=ALU.add, op1=ALU.add).then_inc(out_ready, 1)

            @block.tensor
            def _(pe):
                def xs(c):
                    return x_hi[:, c, :], x_lo[:, c, :]

                pe.wait_ge(bindings_ready, 1)
                pe.matmul(psum[:, 3, 0:12], const("ones"), small[:, 32:44],
                          start=True, stop=True).then_inc(sums_done, 1)
                pe.sem_inc(x_used, KC)
                with pe.Fori(0, NT) as tile:
                    pe.wait_ge(gathered, tile * GATHERED + GATHERED)
                    for g in range(AGROUPS):
                        for c in range(KC):
                            tr = pe.transpose(psum[:, g, c * P:(c + 1) * P], a_raw[:, g, c * P:(c + 1) * P], const("ident"))
                        tr.then_inc(a_turned, 1)

                    def base(c):
                        pe.wait_ge(x0_ready, tile * KC + (c + 1))
                        if c == 0:
                            pe.wait_ge(l1_ready, KC)
                        for m in range(KC):
                            if c == 0:
                                pe.wait_ge(out_ready, tile * KC + (m + 1))
                            mm3(pe, psum[:, 4 + m, :], wt("Wc", c * DIM + m * P), xs(c), c == 0, False)

                    GT = TT // AGROUPS
                    base(0)
                    base(1)
                    pe.wait_ge(x0_ready, tile * KC + KC)
                    for g in range(AGROUPS):
                        pe.wait_ge(a_ready, tile * AGROUPS + (g + 1))
                        cols = slice(g * GT, (g + 1) * GT)
                        for c in range(KC):
                            mm = mm3(pe, psum[:, 2, cols], (a_hi[:, g, c * P:(c + 1) * P], a_lo[:, g, c * P:(c + 1) * P]),
                                     (x_hi[:, c, cols], x_lo[:, c, cols]), c == 0, c == KC - 1)
                    mm.then_inc(rank_done, 1)
                    base(2)
                    base(3)
                    pe.wait_ge(r_ready, tile + 1)
                    pe.wait_ge(b_ready, tile + 1)
                    for m in range(KC):
                        for g in range(AGROUPS):
                            cols = slice(g * GT, (g + 1) * GT)
                            mm = mm3(pe, psum[:, 4 + m, cols], (b_hi[:, g, m * P:(m + 1) * P], b_lo[:, g, m * P:(m + 1) * P]),
                                     (r_hi[:, cols], r_lo[:, cols]), False, g == AGROUPS - 1)
                        mm.then_inc(base_done, 1)

                    def turn_and_score(m):
                        if m >= 2:
                            pe.wait_ge(tok_done, tile * KC + (m - 1))
                            pe.wait_ge(sig_done, tile * KC + (m - 1))
                        pe.wait_ge(wide_done, tile * KC + (m + 1))
                        for i in range(SUBS):
                            tr = pe.transpose(psum[:, m % 2, i * P:(i + 1) * P], wide[:, m, i * P:(i + 1) * P], const("ident"))
                        tr.then_inc(turned, 1)
                        pe.wait_ge(bound_done, tile * KC + (m + 1))
                        for i in range(SUBS):
                            cols = slice(i * P, (i + 1) * P)
                            mm = pe.matmul(psum[:, 2 + m % 2, cols], bound[:, m % 2, cols], wide[:, m, cols], start=True, stop=True)
                        mm.then_inc(s_done, 1)

                    def attend(m):
                        pe.wait_ge(tok_done, tile * KC + (m + 1))
                        pe.wait_ge(att_done, tile * KC + (m + 1))
                        for i in range(SUBS):
                            cols = slice(i * P, (i + 1) * P)
                            mm = pe.matmul(psum[:, 4 + m, cols], tok[:, m % 2, cols], att[:, m % 2, cols], start=True, stop=True)
                        mm.then_inc(pv_done, 1)

                    turn_and_score(0)
                    for m in range(1, KC):
                        turn_and_score(m)
                        attend(m - 1)
                    attend(KC - 1)

                    for layer, (W, A, B, R) in enumerate((("W2", "A2", "B2", "R2"), ("Wf", "Af", "Bf", "Rf"))):
                        def expert_ranks_and_logits(c):
                            if layer == 0:
                                pe.wait_ge(x_ready, tile * KC + (c + 1))
                            else:
                                pe.wait_ge(c_ready, tile * KC + (c + 1))
                            mm = mm3(pe, psum[:, 1, :], wt(A, c * P), xs(c), c == 0, c == KC - 1)
                            if c == KC - 1:
                                mm.then_inc(h_done, 1)
                            mm = mm3(pe, psum[0:NE, 3, :], wt(R, c * NE, NE), xs(c), c == 0, c == KC - 1)
                            if c == KC - 1:
                                mm.then_inc(rows_done, 1)

                        def base_product(c):
                            for m in range(KC):
                                mm = mm3(pe, psum[:, 4 + m, :], wt(W, c * DIM + m * P), xs(c), c == 0, False)
                            if layer == 1:
                                mm.then_inc(x_used, 1)

                        pe.wait_ge(l1_ready, L1_SPLITS)
                        for c in range(KC):
                            expert_ranks_and_logits(c)
                        wait_apart(pe, rows_saved, tile * NM + (layer + 1), pe_passed)
                        for i in range(SUBS):
                            at = (layer * SUBS + i) * NE
                            tr = pe.transpose(psum[:, 0, at:at + NE], logit_rows[:, i * P:(i + 1) * P], const("ident")[0:NE, 0:NE])
                        tr.then_inc(logits_done, 1)
                        for c in range(KC):
                            base_product(c)
                        pe.wait_ge(spread_done, tile * NM + (layer + 1))
                        for i in range(SUBS):
                            tr = pe.transpose(psum[:, 2, i * P:(i + 1) * P], spread[:, i, :, :].rearrange("p e r -> p (e r)"),
                                              const("ident"))
                        tr.then_inc(gateT_done, 1)
                        pe.wait_ge(g_ready, tile * NM + (layer + 1))
                        for m in range(KC):
                            mm3(pe, psum[:, 4 + m, :], wt(B, m * P), (r_hi[:], r_lo[:]), False, True).then_inc(moe_done, 1)


def kernel(**inputs):
    import concourse.bacc as bacc
    from concourse.bass_utils import run_bass_kernel_spmd

    a = {k: np.asarray(v) for k, v in inputs.items()}
    f32 = np.float32

    def chunks(w, width=None):
        return w.reshape(KC, P, -1).transpose(1, 0, 2).reshape(P, -1)

    def flipped(w):
        return w.reshape(KC, P, -1)[:, ::-1].reshape(KC * P, -1)

    def both(w):
        return np.concatenate([w.T, w.T], 0)

    arrays = {}
    arrays["xT"] = a["x"].reshape(TOK, DIM).T
    log_dt = np.broadcast_to(a["L0_cond_log_dt"], (P, SEQ))
    C = a["L0_cond_C"]
    arrays["s4d"] = np.stack([log_dt, both(a["L0_cond_log_A_real"]), both(a["L0_cond_A_imag"]),
                              both(C[..., 0]), both(C[..., 1])], 1)
    skip = np.zeros((LI, SEQ, LJ), f32)
    skip[LI - 1, :, LJ - 1] = a["L0_cond_D"]
    arrays["skip"] = skip.reshape(LI, -1)
    arrays["zeros"] = np.zeros((SEQ, P), f32)
    arrays["lengths"] = np.broadcast_to(a["itok_B_78_3631"].astype(np.int32), (P, BATCH))
    arrays["consts"] = constant_table()[0]

    wq = flipped(a["L0_attn_wq"].reshape(DIM, HEADS, DQ)[:, :, :DH].reshape(DIM, HEADS * DH))
    wkv = flipped(a["L0_attn_wkv"])
    wo = a["L0_attn_wo"].reshape(GROUPS, GH, DH, DIM)

    def grouped(w):
        return w.reshape(KC, P, GROUPS, GH * DH).transpose(2, 1, 0, 3).reshape(GROUPS, P, -1)

    arrays["attn_w"] = np.concatenate([
        grouped(wq), grouped(wkv[:, :HEADS * DH]), grouped(wkv[:, HEADS * DH:2 * HEADS * DH]),
        wo.transpose(0, 2, 1, 3).reshape(GROUPS, P, -1)], 2)

    lora_a = a["L0_cond2_lora_A"].transpose(1, 0, 2).reshape(DIM, LAB * LR)
    lora_a = np.concatenate([lora_a, np.zeros((DIM, 2 * P - LAB * LR), f32)], 1)
    lora_b = np.tile(a["L0_cond2_lora_B"].T, (P // LR, 1))
    c2_w = np.concatenate([chunks(a["L0_cond2_weight"].T), chunks(lora_a), lora_b,
                           np.zeros((P, GW - C2_COLS), f32)], 1)
    arrays["attn_w"] = np.concatenate([arrays["attn_w"], c2_w[None]], 0)
    arrays["c2_bias"] = a["L0_cond2_bias"].reshape(KC, P).T
    arrays["labels"] = np.broadcast_to(a["itok_B_0_4"].astype(np.int32), (P, BATCH))
    j_of, _ = octonion_table()
    ffn = [a["L0_ffn_w_gate"], a["L0_ffn_w_up"], a["L0_ffn_w_down"]]
    arrays["oct_base"] = np.stack([w.reshape(P, -1) for w in ffn], 1)
    gate_up = [w[j_of].transpose(0, 3, 1, 2).reshape(KC, P, HID) for w in ffn[:2]]
    dn = ffn[2][j_of].transpose(0, 3, 1, 2).reshape(HID, DIM)
    dn = np.concatenate([dn, np.zeros((HTP * P - HID, DIM), f32)], 0)
    dn = dn.reshape(NT, HTP // NT, P, DIM).transpose(0, 2, 1, 3).reshape(NT, P, -1)
    arrays["oct_w"] = np.concatenate(gate_up + [dn], 2)

    arrays["ada_a"] = a["L1_cond_lora_A_w"].reshape(ADA * AR, DIM)
    arrays["ada_b"] = a["L1_cond_lora_B_w"].transpose(0, 2, 1).reshape(ADA * AR, DIM)
    blocks = {
        "Wc": chunks(a["L1_cond_base_weight"].T),
        "W2": chunks(a["L1_cond2_W"].T), "Wf": chunks(a["L1_ffn_W_base"].T),
        "A2": chunks(a["L1_cond2_A"].reshape(NE * ER, DIM).T),
        "B2": a["L1_cond2_B"].transpose(0, 2, 1).reshape(NE * ER, DIM),
        "Af": chunks(a["L1_ffn_lora_A"].transpose(1, 0, 2).reshape(DIM, NE * ER)),
        "Bf": a["L1_ffn_lora_B"].reshape(NE * ER, DIM),
        "R2": chunks(a["L1_cond2_Wr"].T), "Rf": chunks(a["L1_ffn_W_router"].T),
    }
    arrays["l1_w"] = np.concatenate([blocks[n] for n, _ in L1_BLOCKS], 1)
    small = np.zeros((P, 32), f32)
    small[:, 0:4] = a["L1_cond_base_bias"].reshape(KC, P).T
    small[:, 4:8] = a["L1_ffn_b_base"].reshape(KC, P).T
    small[:, 20:24], small[:, 24:28], small[:, 28:32] = (a[f"L1_attn_bv_{n}"].T for n in "qkv")
    arrays["l1_small"] = small
    arrays["router_bias"] = np.broadcast_to(a["L1_ffn_b_router"], (P, NE))
    arrays["adapters"] = np.repeat(a["itok_B_6_15"].astype(np.int32), AR).reshape(BATCH // ABATCH, P).T
    arrays["languages"] = np.repeat(a["itok_B_0_7"].astype(np.int32), SEQ).reshape(TOK // P, P).T

    nc = bacc.Bacc("TRN2", target_bir_lowering=False, num_devices=1)
    given, handles = {}, {}
    for name, v in arrays.items():
        v = np.ascontiguousarray(v)
        given[f"in_{name}"] = v
        handles[name] = nc.dram_tensor(f"in_{name}", v.shape, mybir.dt.from_np(v.dtype), kind="ExternalInput").ap()
    handles["out"] = nc.dram_tensor("outT", (DIM, TOK), F32, kind="ExternalOutput").ap()
    build_program(nc, handles)
    r = run_bass_kernel_spmd(nc, [given], core_ids=[0])
    return r.results[0]["outT"].T.reshape(BATCH, SEQ, DIM)
```

```python
from contextlib import ExitStack

import numpy as np
import concourse.bass as bass
from concourse import mybir

F32 = mybir.dt.float32
F32R = mybir.dt.float32r
I32 = mybir.dt.int32
U32 = mybir.dt.uint32
ACT = mybir.ActivationFunctionType
ALU = mybir.AluOpType
AX_X = mybir.AxisListType.X

P = 128
BATCH, SEQ, DIM = 64, 32, 512
TOK = BATCH * SEQ
KC = DIM // P
TT = 512
NT = TOK // TT
SUBS = TT // P
BPT = TT // SEQ
HEADS, DH, DQ = 32, 128, 192
GH = 2
GROUPS = HEADS // GH
GW = 3 * KC * GH * DH + GH * DIM
PIECE = GW // NT
QOFF, KOFF, VOFF, OOFF = 0, KC * GH * DH, 2 * KC * GH * DH, 3 * KC * GH * DH
NST = 64
LI, LJ = 16, 32
RROW = DIM + P
OCT, OH, OD = 8, 170, 64
HID = OCT * OH
HT = -(-HID // P)
HTP = -(-HT // NT) * NT
TERN_DOWN = HTP // NT * DIM // 2
TERN = [(0, HID), (HID, HID), (2 * HID, TERN_DOWN), (2 * HID + TERN_DOWN, TERN_DOWN)]
TERN_COLS = 2 * HID + 2 * TERN_DOWN
LAB, LR = 5, 32
ADA, AR = 32, 16
ABATCH = P // AR
AGROUPS = BPT // ABATCH
GATHERED = 16 * 2 * AGROUPS
NE, ER = 8, 16
LOGITS_AT, GATES_AT = 3, 11
ID_COLS = BATCH + BATCH // ABATCH + TOK // P
SCALE0 = float(DQ) ** -0.5
SCALE1 = float(P) ** -0.5 * 4.0
NEG = -1e30
MAGIC = 12582912.0
LN2_HI, LN2_LO = 0.693359375, -2.12194440e-4
TWO_PI = (6.28125, 1.9350051879882812e-3, 3.019915978e-7)
PI_IN = 3.1415925


def octonion_table():
    s = np.zeros((8, 8, 8), np.float32)
    s[0, 0, 0] = 1.0
    for i in range(1, 8):
        s[0, i, i] = s[i, 0, i] = 1.0
        s[i, i, 0] = -1.0
    for a, b, c in [(1, 2, 3), (1, 4, 5), (1, 7, 6), (2, 4, 6), (2, 5, 7), (3, 4, 7), (3, 6, 5)]:
        for x, y, z in ((a, b, c), (b, c, a), (c, a, b)):
            s[x, y, z] = 1.0
            s[y, x, z] = -1.0
    return np.abs(s).argmax(0), s.sum(0)


def constant_table():
    p = np.arange(P)
    part = p // NST
    li = LJ * (LI - 1 - np.arange(LI))
    lj = LJ - 1 - np.arange(LJ)
    lags = np.concatenate([li, li, lj])
    quarter = np.zeros((P, 2 * LI + LJ))
    quarter[:, :LI] = (1 + part)[:, None]
    quarter[:, LI:2 * LI] = (2 + part)[:, None]
    quarter[:, 2 * LI:] = (1 - part)[:, None]
    q = p % SEQ
    j_of, sign = octonion_table()
    sign_up = np.stack([np.stack([-sign[2 * c + x // OD] for x in p]) for c in range(KC)], 1)
    unit = np.minimum(p[:, None] + P * np.arange(HTP)[None], HID - 1)
    sign_down = -sign[unit // OH]
    fields = {
        "lags": np.broadcast_to(lags, (P, len(lags))),
        "turns": quarter / 4,
        "angles": quarter * (np.pi / 2),
        "feature": P * np.arange(KC)[None] + (P - 1 - p)[:, None],
        "causal_add": np.where(np.arange(SEQ)[None] <= q[:, None], 0.0, NEG),
        "causal_mul": (p[:, None] // SEQ == p[None] // SEQ) * (p[:, None] <= p[None]),
        "ident": np.eye(P),
        "ones": np.ones((P, P)),
        "labeler": np.stack([p // LR, np.full(P, P // LR)], 1),
        "own_batch": (p // AR)[:, None] == np.arange(BPT)[None] % ABATCH,
        "adapter_rank": (p % AR)[:, None],
        "iota": np.broadcast_to(np.arange(NE), (P, NE)),
        "count": np.broadcast_to(1 + np.arange(NE), (P, NE)),
        "sign_up": sign_up.reshape(P, -1),
        "sign_down": sign_down.reshape(P, -1),
    }
    at, n = {}, 0
    for name, a in fields.items():
        at[name] = (n, n + a.shape[1])
        n += a.shape[1]
    return np.concatenate(list(fields.values()), 1).astype(np.float32), at


L1_BLOCKS = [("Wc", KC * DIM), ("W2", KC * DIM), ("Wf", KC * DIM), ("A2", KC * P), ("B2", DIM),
             ("Af", KC * P), ("Bf", DIM), ("R2", KC * NE), ("Rf", KC * NE)]
L1_AT, _n = {}, 0
for _name, _w in L1_BLOCKS:
    L1_AT[_name] = _n
    _n += _w
L1_COLS = _n
L1_PIECES = [(a, min(a + KC * DIM, L1_COLS)) for a in range(0, L1_COLS, KC * DIM)]
C2_COLS = KC * DIM + KC * LAB * LR + DIM


def build_program(nc, t):
    _, CONST = constant_table()
    ctx = ExitStack()
    with ctx:
        def sb(stack, name, shape, dt=F32):
            return stack.enter_context(nc.sbuf_tensor(name, shape, dt))

        def sem(stack, name):
            return stack.enter_context(nc.semaphore(name))

        def overlaid(stack, name, shape):
            with nc.sbuf_tensor(f"{name}_f32", shape, F32) as plain:
                pass
            return plain, sb(stack, name, shape, F32R)

        resid = sb(ctx, "resid", [P, KC, TOK])
        consts = sb(ctx, "consts", [P, t["consts"].shape[1]])
        psum = ctx.enter_context(nc.psum_tensor("psum", [P, 8, TT], F32))
        kernel_rows = nc.dram_tensor("kernel_rows", [SEQ, RROW], F32, kind="Internal").ap()

        def const(name):
            a, b = CONST[name]
            return consts[:, a:b]

        def mm3(pe, out, w, x, start, stop):
            pe.matmul(out, w[0], x[0], start=start, stop=False)
            pe.matmul(out, w[0], x[1], start=False, stop=False)
            return pe.matmul(out, w[1], x[0], start=False, stop=stop)

        later = {
            "ffn": sb(ctx, "ffn_small", [P, 24]),
            "l1": sb(ctx, "l1_small", [P, 64]),
            "label_mask": sb(ctx, "label_mask", [P, 2, BATCH]),
            "rows": sb(ctx, "gather_rows", [P, BATCH // ABATCH], U32),
            "lang": sb(ctx, "lang", [P, TOK // P, NE]),
            "rows_now": sb(ctx, "rows_now", [P, AGROUPS], U32),
            "rows_copied": sem(ctx, "rows_copied"), "gathered": sem(ctx, "gathered"),
            "passed": sem(ctx, "gather_passed"),
        }
        kept_raw, kept = overlaid(ctx, "kept", [P, 2, L1_COLS // 2])
        attn = ctx.enter_context(ExitStack())
        y_hi = sb(attn, "y_hi", [P, KC, TOK], F32R)
        y_lo = sb(attn, "y_lo", [P, KC, TOK], F32R)
        wraw = sb(attn, "wraw", [P, GW])
        raw_loaded = [sem(attn, f"raw_loaded{i}") for i in range(NT)]
        s4d_and_convolution(nc, t, sb, sem, const, consts, resid, psum, kernel_rows, kept, later, y_hi, y_lo, wraw, raw_loaded)
        attention(nc, t, sb, sem, const, mm3, resid, psum, kept, y_hi, y_lo, wraw, raw_loaded)
        attn.close()
        later["ranks_raw"], later["ranks"] = overlaid(ctx, "ranks", [P, 4, TT])
        octonion_ffn(nc, t, sb, sem, overlaid, const, mm3, resid, psum, kept_raw, kept, later)
        layer_one(nc, t, sb, sem, const, mm3, resid, psum, kept_raw, kept, later)


def wait_apart(engine, semaphore, value, passed):
    engine.wait_ge(semaphore, value)
    engine.sem_inc(passed, 1)


def chained(engine, semaphore):
    n = [0]

    def then(ins):
        n[0] += 1
        ins.then_inc(semaphore, 1)
        engine.wait_ge(semaphore, n[0])

    def tt(out, a, b, op):
        then(engine.tensor_tensor(out, a, b, op))

    def ts(out, a, s1, s2, op0, op1=None):
        then(engine.tensor_scalar(out, a, s1, s2, op0, *(() if op1 is None else (op1,))))

    def stt(out, a, s, b, op0, op1):
        then(engine.scalar_tensor_tensor(out=out, in0=a, scalar=s, in1=b, op0=op0, op1=op1))

    return then, tt, ts, stt


def exp_minus_1(then, tt, ts, stt, engine, x, em1, two_k, tmp):
    t0, t1, t2 = tmp
    ts(t0, x, 1.4426950408889634, MAGIC, ALU.mult, ALU.add)
    ts(t0, t0, MAGIC, None, ALU.subtract)
    stt(t1, t0, -LN2_HI, x, ALU.mult, ALU.add)
    stt(t1, t0, -LN2_LO, t1, ALU.mult, ALU.add)
    ts(t0, t0, 127.0, 8388608.0, ALU.add, ALU.mult)
    then(engine.tensor_copy(two_k.bitcast(I32), t0))
    ts(t2, t1, 1 / 40320.0, 1 / 5040.0, ALU.mult, ALU.add)
    tt(t2, t2, t1, ALU.mult)
    for c in (1 / 720.0, 1 / 120.0, 1 / 24.0, 1 / 6.0, 0.5, 1.0):
        stt(t2, t2, c, t1, ALU.add, ALU.mult)
    tt(t2, t2, two_k, ALU.mult)
    ts(t0, two_k, 1.0, None, ALU.subtract)
    tt(em1, t2, t0, ALU.add)


def s4d_and_convolution(nc, t, sb, sem, const, consts, resid, psum, kernel_rows, kept, later, y_hi, y_lo, wraw,
                        raw_loaded):
    ctx = ExitStack()
    with ctx:
        NW = 2 * LI + LJ
        HALF = SEQ // 2
        NB = 4
        PB, NCB = TT // (KC * BATCH), 4
        prm = sb(ctx, "prm", [P, 5, SEQ])
        sk = sb(ctx, "sk", [P, 21, 2 * SEQ])
        dt, ar = sk[:, 0, 0:SEQ], sk[:, 0, SEQ:]
        ai, cr, ci = prm[:, 2, :], prm[:, 3, :], prm[:, 4, :]
        da, db, inv = sk[:, 5, 0:SEQ], sk[:, 6, 0:SEQ], sk[:, 18, 0:SEQ]
        ctr, cti = sk[:, 19, 0:SEQ], sk[:, 20, 0:SEQ]
        lensi = sb(ctx, "lensi", [P, BATCH], I32)
        lens = sb(ctx, "lens", [P, BATCH])
        mask = sb(ctx, "mask", [P, KC, BATCH])
        theta = sb(ctx, "theta", [P, SEQ, NW])
        turns = sb(ctx, "turns", [P, SEQ, NW])
        mag = sb(ctx, "mag", [P, SEQ, LI + LJ])
        left = sb(ctx, "left", [P, SEQ, LI])
        right = sb(ctx, "right", [P, SEQ, LJ])
        skip = sb(ctx, "skip", [LI, SEQ * LJ])
        rows = sb(ctx, "rows", [LI, SEQ * LJ])
        hankel = sb(ctx, "hankel", [P, NB, DIM])
        ymask = sb(ctx, "ymask", [P, 2, TT])

        prm_in, params_in, x_in, const_in = (sem(ctx, n) for n in ("prm_in", "params_in", "x_in", "const_in"))
        step, pool_step = sem(ctx, "s4d_step"), sem(ctx, "pool_step")
        small_ready, ct_ready = sem(ctx, "small_ready"), sem(ctx, "ct_ready")
        trig_ready, trig_done = sem(ctx, "trig_ready"), sem(ctx, "trig_done")
        mag_ready, mag_done = sem(ctx, "mag_ready"), sem(ctx, "mag_done")
        factors_ready, kernels_done = sem(ctx, "factors_ready"), sem(ctx, "kernels_done")
        rows_ready, rows_stored = sem(ctx, "rows_ready"), sem(ctx, "rows_stored")
        hankel_in = [sem(ctx, f"hankel_in{i}") for i in range(NB)]
        hankel_free = sem(ctx, "hankel_free")
        conv_done, bank_free = sem(ctx, "conv_done"), sem(ctx, "bank_free")
        y_lo_done = sem(ctx, "y_lo_done")
        masked, y_hi_done, ymask_free = sem(ctx, "masked"), sem(ctx, "y_hi_done"), sem(ctx, "ymask_free")
        overlapping = bass.AP(tensor=kernel_rows.tensor, offset=0, ap=[[RROW, SEQ], [1, P], [1, DIM]])
        base = theta[:].rearrange("p h n -> p (h n)")[:, 0:3 * OCT * OH * OD // P].rearrange("p (w n) -> p w n", w=3)
        ids_i = sb(ctx, "ids_i", [P, ID_COLS], I32)
        ids = sb(ctx, "ids", [P, ID_COLS])
        ffn, l1 = later["ffn"], later["l1"]
        later_in = sem(ctx, "later_in")
        w0_hi_done, sums_ready, sums_done = sem(ctx, "w0_hi_done"), sem(ctx, "sums_ready"), sem(ctx, "sums_done")
        block = ctx.enter_context(nc.Block())

        def low_part(it, k, s):
            at = bass.ds(it * (PB * NCB) + (k * PB + s), 1)
            of = lambda y: y.rearrange("p c (b s) -> p c b s", s=SEQ)[:, :, :, at].rearrange("p c b s -> p c (b s)")
            return (of(y_lo[:]), ymask[:, k % 2, s * KC * BATCH:(s + 1) * KC * BATCH].rearrange("p (c b) -> p c b", c=KC),
                    of(y_hi[:].bitcast(F32)))

        @block.sync
        def _(sp):
            sp.dma_start(prm[:], t["s4d"]).then_inc(prm_in, 16)
            sp.dma_start(consts[:], t["consts"]).then_inc(const_in, 16)
            sp.dma_start(skip[:], t["skip"]).then_inc(params_in, 16)
            sp.dma_start(lensi[:], t["lengths"]).then_inc(params_in, 16)
            sp.dma_start(kernel_rows[:, DIM:RROW], t["zeros"]).then_inc(rows_stored, 16)
            for c in range(KC):
                sp.dma_start(resid[:, c, :], t["xT"][c * P:(c + 1) * P, :]).then_inc(x_in, 16)
            for p in range(NT):
                sp.dma_start(wraw[:, p * PIECE:(p + 1) * PIECE],
                             t["attn_w"][0, :, p * PIECE:(p + 1) * PIECE]).then_inc(raw_loaded[p], 16)
            sp.dma_start(ffn[:, 0:4], t["c2_bias"]).then_inc(later_in, 16)
            sp.dma_start(l1[:, 0:32], t["l1_small"]).then_inc(later_in, 16)
            sp.dma_start(l1[:, 56:64], t["router_bias"]).then_inc(later_in, 16)
            sp.dma_start(ids_i[:], t["ids"]).then_inc(later_in, 16)

            def store_rows(half):
                sp.wait_ge(rows_ready, half + 1)
                sp.dma_start(kernel_rows[half * HALF:(half + 1) * HALF, 0:DIM].rearrange("h (i j) -> i h j", i=LI),
                             rows[:, half * HALF * LJ:(half + 1) * HALF * LJ].rearrange("i (h j) -> i h j", h=HALF)
                             ).then_inc(rows_stored, 16)

            def load_hankel(h, b):
                src = overlapping[bass.ds(h, 1), :, :].rearrange("h p n -> (h p) n")
                sp.dma_start(hankel[:, b, :], src).then_inc(hankel_in[b], 16)

            def load_four(it):
                for b in range(NB):
                    used = hankel_free if b % PB < PB - 1 else conv_done
                    sp.wait_ge(used, (it - 1) * (NB // PB) + (b // PB + 1))
                    load_hankel(it * NB + b, b)

            store_rows(0)
            sp.wait_ge(rows_stored, 32)
            for b in range(NB):
                load_hankel(b, b)
            with sp.Fori(1, HALF // NB - 1) as it:
                load_four(it)
            sp.wait_ge(factors_ready, 2)
            sp.dma_start(base, t["oct_base"]).then_inc(later_in, 16)
            store_rows(1)
            load_four(HALF // NB - 1)
            sp.wait_ge(rows_stored, 48)
            with sp.Fori(HALF // NB, SEQ // NB) as it:
                load_four(it)

        @block.vector
        def _(dve):
            then, tt, ts, stt = chained(dve, step)

            def per_lag(a, n):
                return a.unsqueeze(2).broadcast_to([P, a.shape[1], n])

            def per_position(a, n=HALF):
                return a.unsqueeze(1).broadcast_to([P, n, a.shape[1]])

            dve.wait_ge(prm_in, 16)
            logs = prm[:, 0:2, :].rearrange("p a h -> p (a h)")
            exp_minus_1(then, tt, ts, stt, dve, logs, sk[:, 0, :], sk[:, 1, :], [sk[:, i, :] for i in (2, 3, 4)])
            ts(sk[:, 0, :], sk[:, 0, :], 1.0, None, ALU.add)
            stt(da, ar, -1.0, dt, ALU.mult, ALU.mult)
            dve.sem_inc(small_ready, 1)
            tt(db, ai, dt, ALU.mult)
            ang, turn = sk[:, 7, :], sk[:, 2, :]
            then(dve.tensor_copy(ang[:, 0:SEQ], db))
            ts(ang[:, SEQ:], db, 0.5, None, ALU.mult)
            ts(turn, ang, 0.15915494309189535, MAGIC, ALU.mult, ALU.add)
            ts(turn, turn, MAGIC, None, ALU.subtract)
            for part in TWO_PI:
                stt(ang, turn, -part, ang, ALU.mult, ALU.add)
            ts(ang, ang, PI_IN, -PI_IN, ALU.min, ALU.max)
            dve.sem_inc(small_ready, 1)
            dve.wait_ge(const_in, 16)
            tt(mag[:], per_lag(da, LI + LJ), per_position(const("lags")[:, LI:], SEQ), ALU.mult)
            dve.sem_inc(mag_ready, 1)
            tt(sk[:, 3, 0:SEQ], ar, ar, ALU.mult)
            tt(sk[:, 4, 0:SEQ], ai, ai, ALU.mult)
            tt(sk[:, 3, 0:SEQ], sk[:, 3, 0:SEQ], sk[:, 4, 0:SEQ], ALU.add)
            then(dve.reciprocal(inv, sk[:, 3, 0:SEQ]))
            dve.sem_inc(small_ready, 1)

            def tables(half, between=None):
                part = slice(half * HALF, (half + 1) * HALF)
                th, tn = theta[:, part, :], turns[:, part, :]
                tt(th, per_lag(db[:, part], NW), per_position(const("lags")), ALU.mult)
                stt(tn, th, 0.15915494309189535, per_position(const("turns")), ALU.mult, ALU.add)
                if between:
                    between()
                ts(tn, tn, MAGIC, MAGIC, ALU.add, ALU.subtract)
                for p in TWO_PI:
                    stt(th, tn, -p, th, ALU.mult, ALU.add)
                tt(th, th, per_position(const("angles")), ALU.add)
                ts(th, th, PI_IN, -PI_IN, ALU.min, ALU.max)
                dve.sem_inc(trig_ready, 1)

            def factors(half):
                part = slice(half * HALF, (half + 1) * HALF)
                dve.wait_ge(trig_done, half + 2)
                tt(right[:, part, :], theta[:, part, 2 * LI:], mag[:, part, LI:], ALU.mult)
                dve.wait_ge(ct_ready, 1)
                lf, tn = left[:, part, :], turns[:, part, 0:LI]
                tt(lf, theta[:, part, 0:LI], per_lag(ctr[:, part], LI), ALU.mult)
                tt(tn, theta[:, part, LI:2 * LI], per_lag(cti[:, part], LI), ALU.mult)
                tt(lf, lf, tn, ALU.add)
                tt(lf, lf, mag[:, part, 0:LI], ALU.mult)
                dve.sem_inc(factors_ready, 1)

            def kernels(half):
                dve.wait_ge(kernels_done, half + 1)
                cols = slice(half * HALF * LJ, (half + 1) * HALF * LJ)
                tt(rows[:, cols], psum[0:LI, 5 + half, :], skip[:, cols], ALU.add)
                dve.sem_inc(rows_ready, 1)

            def mask_turn(it):
                for k in range(NCB):
                    dve.wait_ge(conv_done, it * NCB + (k + 1))
                    dve.wait_ge(ymask_free, it * NCB + (k + 1))
                    dve.tensor_tensor(ymask[:, k % 2, :].rearrange("p (s n) -> p s n", s=PB),
                                      psum[:, k, :].rearrange("p (s n) -> p s n", s=PB),
                                      mask[:].rearrange("p c b -> p (c b)").unsqueeze(1)
                                      .broadcast_to([P, PB, KC * BATCH]), ALU.mult).then_inc(masked, 1)
                    dve.wait_ge(masked, it * NCB + (k + 1))
                    dve.sem_inc(bank_free, 1)
                    if k:
                        second_low(it, k - 1)
                second_low(it, NCB - 1)

            def second_low(it, k):
                dve.wait_ge(y_hi_done, it * (PB * NCB) + (k * PB + PB))
                dve.tensor_tensor(*low_part(it, k, PB - 1), ALU.subtract).then_inc(y_lo_done, 1)
                dve.wait_ge(y_lo_done, it * NCB + (k + 1))

            tables(0)
            dve.wait_ge(mag_done, 1)
            factors(0)
            dve.sem_inc(bank_free, NCB)
            dve.wait_ge(params_in, 32)
            tables(1, between=lambda: kernels(0))
            factors(1)
            then(dve.tensor_copy(lens[:], lensi[:]))
            for c in range(KC):
                ts(mask[:, c, :], lens[:], const("feature")[:, c:c + 1], None, ALU.is_gt)
            mask_turn(0)
            kernels(1)

            dve.wait_ge(later_in, 16 * 5)
            then(dve.tensor_reduce(ffn[:, 4:7], base, AX_X, ALU.add, apply_absolute_value=True))
            stt(l1[:, 32:44], l1[:, 20:32], -1.0, l1[:, 20:32], ALU.mult, ALU.max)
            dve.sem_inc(sums_ready, 1)
            ts(l1[:, 44:56], l1[:, 20:32], 0.0, 2.0, ALU.is_ge, ALU.mult)
            ts(l1[:, 44:56], l1[:, 44:56], 1.0, None, ALU.subtract)
            then(dve.tensor_copy(ids[:], ids_i[:]))
            for k in range(2):
                ts(later["label_mask"][:, k, :], ids[:, 0:BATCH], const("labeler")[:, k:k + 1], 0.5, ALU.is_equal, ALU.mult)
            rows_f = ids[:, BATCH:BATCH + BATCH // ABATCH]
            ts(rows_f, rows_f, 0.0, ADA - 1.0, ALU.max, ALU.min)
            ts(rows_f, rows_f, float(AR), const("adapter_rank"), ALU.mult, ALU.add)
            then(dve.tensor_copy(later["rows"][:], rows_f))
            lang = later["lang"][:]
            tt(lang, ids[:, BATCH + BATCH // ABATCH:].unsqueeze(2).broadcast_to([P, TOK // P, NE]),
               const("iota").unsqueeze(1).broadcast_to([P, TOK // P, NE]), ALU.is_equal)
            ts(lang, lang, 5.0, None, ALU.mult)

            with dve.Fori(1, SEQ // (PB * NCB) - 1) as it:
                mask_turn(it)
            dve.wait_ge(sums_done, 2)
            ts(ffn[:, 10:13], psum[:, 4, 0:3], 1.0 / float(OCT * OH * OD), None, ALU.mult)
            ts(ffn[:, 13:16], ffn[:, 10:13], 0.5, None, ALU.mult)
            ts(ffn[:, 16:19], ffn[:, 10:13], -0.5, None, ALU.mult)
            stt(l1[:, 32:44], psum[:, 4, 4:16], 1.0 / P, l1[:, 44:56], ALU.mult, ALU.mult)
            tt(l1[:, 8:12], l1[:, 32:36], l1[:, 36:40], ALU.mult)
            then(dve.tensor_copy(l1[:, 12:16], l1[:, 40:44]))
            mask_turn(SEQ // (PB * NCB) - 1)

        @block.scalar
        def _(act):
            act.wait_ge(small_ready, 2)
            act.activation(sk[:, 8, :], sk[:, 7, :], ACT.Sin).then_inc(trig_done, 1)
            act.wait_ge(mag_ready, 1)
            act.activation(mag[:], mag[:], ACT.Exp).then_inc(mag_done, 1)
            def sines(half):
                part = slice(half * HALF, (half + 1) * HALF)
                act.wait_ge(trig_ready, half + 1)
                act.activation(theta[:, part, :], theta[:, part, :], ACT.Sin).then_inc(trig_done, 1)

            sines(0)
            for p in range(NT):
                act.wait_ge(raw_loaded[p], 16)
                at = slice(p * PIECE, (p + 1) * PIECE)
                act.activation(kept[:, 0, at], wraw[:, at], ACT.Copy).then_inc(w0_hi_done, 1)
            sines(1)
            with act.Fori(0, SEQ // (PB * NCB)) as it:
                for k in range(NCB):
                    act.wait_ge(masked, it * NCB + (k + 1))
                    for s in range(PB):
                        dst = y_hi[:].rearrange("p c (b s) -> p c b s", s=SEQ)[:, :, :, bass.ds(it * (PB * NCB) + (k * PB + s), 1)]
                        act.activation(dst.rearrange("p c b s -> p c (b s)"), ymask[:, k % 2, s * KC * BATCH:(s + 1) * KC * BATCH]
                                       .rearrange("p (c b) -> p c b", c=KC), ACT.Copy).then_inc(y_hi_done, 1)

        @block.gpsimd
        def _(pool):
            then, tt, ts, _ = chained(pool, pool_step)

            def stt(out, a, scalar, other, op0, op1):
                ts(b, a, scalar, None, op0)
                tt(out, b, other, op1)


            pool.wait_ge(small_ready, 1)
            em1, vers, e1r, e1i, cosb, ur, ui, a, b = (sk[:, i, 0:SEQ] for i in range(9, 18))
            exp_minus_1(then, tt, ts, stt, pool, da, em1, vers, [e1r, e1i, cosb])
            pool.wait_ge(trig_done, 1)
            s1, s2 = sk[:, 8, 0:SEQ], sk[:, 8, SEQ:]
            tt(vers, s2, s2, ALU.mult)
            ts(vers, vers, -2.0, None, ALU.mult)
            ts(cosb, vers, 1.0, None, ALU.add)
            tt(e1r, em1, cosb, ALU.mult)
            tt(e1r, e1r, vers, ALU.add)
            ts(e1i, em1, 1.0, None, ALU.add)
            tt(e1i, e1i, s1, ALU.mult)
            tt(ur, cr, e1r, ALU.mult)
            tt(a, ci, e1i, ALU.mult)
            tt(ur, ur, a, ALU.subtract)
            tt(ui, cr, e1i, ALU.mult)
            tt(a, ci, e1r, ALU.mult)
            tt(ui, ui, a, ALU.add)
            pool.wait_ge(small_ready, 3)
            tt(a, ui, ai, ALU.mult)
            tt(b, ur, ar, ALU.mult)
            tt(a, a, b, ALU.subtract)
            tt(a, a, inv, ALU.mult)
            ts(ctr, a, 2.0, None, ALU.mult)
            tt(a, ur, ai, ALU.mult)
            tt(b, ui, ar, ALU.mult)
            tt(a, a, b, ALU.add)
            tt(a, a, inv, ALU.mult)
            ts(cti, a, -2.0, None, ALU.mult)
            pool.sem_inc(ct_ready, 1)
            for p in range(NT):
                pool.wait_ge(w0_hi_done, p + 1)
                at = slice(p * PIECE, (p + 1) * PIECE)
                pool.tensor_tensor(kept[:, 1, at], wraw[:, at], kept[:, 0, at].bitcast(F32), ALU.subtract)
            pool.sem_inc(ymask_free, 2)
            with pool.Fori(0, SEQ // (PB * NCB)) as it:
                for k in range(NCB):
                    pool.wait_ge(y_hi_done, it * (PB * NCB) + (k * PB + PB - 1))
                    pool.tensor_tensor(*low_part(it, k, 0), ALU.subtract).then_inc(ymask_free, 1)

        @block.tensor
        def _(pe):
            def kernels(half):
                pe.wait_ge(factors_ready, half + 1)
                for h in range(HALF):
                    mm = pe.matmul(psum[0:LI, 5 + half, h * LJ:(h + 1) * LJ], left[:, half * HALF + h, :],
                                   right[:, half * HALF + h, :], start=True, stop=True)
                mm.then_inc(kernels_done, 1)

            def convolve(it):
                for k in range(NCB):
                    pe.wait_ge(bank_free, it * NCB + (k + 1))
                    for s in range(PB):
                        h = k * PB + s
                        pe.wait_ge(hankel_in[h % NB], it * (16 * PB * NCB // NB) + 16 * (h // NB + 1))
                        for d in range(KC):
                            n = KC - d
                            u = resid[:].rearrange("p c (b s) -> p c b s", s=SEQ)[:, 0:n, :, bass.ds(it * (PB * NCB) + h, 1)]
                            a = (s * KC + d) * BATCH
                            mm = pe.matmul(psum[:, k, a:a + n * BATCH], hankel[:, h % NB, (KC - 1 - d) * P:(KC - d) * P],
                                           u.rearrange("p c b s -> p c (b s)"), start=(d == 0), stop=(d == KC - 1))
                        if s < PB - 1:
                            mm.then_inc(hankel_free, 1)
                    mm.then_inc(conv_done, 1)

            kernels(0)
            pe.wait_ge(x_in, 16 * KC)
            convolve(0)
            kernels(1)
            with pe.Fori(1, SEQ // (PB * NCB) - 1) as it:
                convolve(it)
            pe.wait_ge(sums_ready, 1)
            pe.matmul(psum[:, 4, 0:3], const("ones"), ffn[:, 4:7], start=True, stop=True).then_inc(sums_done, 1)
            pe.matmul(psum[:, 4, 4:16], const("ones"), l1[:, 32:44], start=True, stop=True).then_inc(sums_done, 1)
            convolve(SEQ // (PB * NCB) - 1)


def attention(nc, t, sb, sem, const, mm3, resid, psum, kept, y_hi, y_lo, wraw, raw_loaded):
    STEPS = 2 * NT
    TURNS = GROUPS // 2
    NPJ, NTL = 6, 6
    ctx = ExitStack()
    with ctx:
        w_hi = [kept[:, 0, 0:GW], sb(ctx, "w_hi1", [P, GW], F32R)]
        w_lo = [kept[:, 1, 0:GW], sb(ctx, "w_lo1", [P, GW], F32R)]
        qT = sb(ctx, "qT", [P, GH, TT])
        kT = sb(ctx, "kT", [P, GH, TT])
        v_tok = sb(ctx, "v_tok", [P, SUBS, GH * DH])
        NBK = GH * SUBS
        sc = sb(ctx, "sc", [P, NBK, SEQ])
        ex = sb(ctx, "ex", [P, NBK, SEQ])
        stat = sb(ctx, "stat", [P, 3, NBK])
        probT = sb(ctx, "probT", [P, NBK, P])
        o_hi = sb(ctx, "o_hi", [P, GH, TT], F32R)
        o_lo = sb(ctx, "o_lo", [P, GH, TT], F32R)

        hi_split, lo_split = sem(ctx, "hi_split"), sem(ctx, "lo_split")
        cleared, out_cleared = sem(ctx, "cleared"), sem(ctx, "out_cleared")
        proj_done, proj_free = sem(ctx, "proj_done"), sem(ctx, "proj_free")
        scores_done = sem(ctx, "scores_done")
        shifted, exp_done = sem(ctx, "shifted"), sem(ctx, "exp_done")
        prob_ready, soft_step = sem(ctx, "prob_ready"), sem(ctx, "soft_step")
        pv_done, out_done = sem(ctx, "pv_done"), sem(ctx, "out_done")
        o_hi_done, tail_free = sem(ctx, "o_hi_done"), sem(ctx, "tail_free")
        block = ctx.enter_context(nc.Block())

        def weight(par, off, n=P):
            return w_hi[par][:, off:off + n], w_lo[par][:, off:off + n]

        @block.sync
        def _(sp):
            with sp.Fori(1, GROUPS + 1) as g:
                for p in range(NT):
                    sp.wait_ge(lo_split, g * NT + (p + 1 - NT))
                    sp.dma_start(wraw[:, p * PIECE:(p + 1) * PIECE],
                                 t["attn_w"][bass.ds(g, 1), :, p * PIECE:(p + 1) * PIECE]
                                 .rearrange("g p n -> (g p) n")).then_inc(raw_loaded[p], 16)

        def split_hi(act, group, par, p):
            act.wait_ge(raw_loaded[p], group * 16 + 16)
            act.activation(w_hi[par][:, p * PIECE:(p + 1) * PIECE], wraw[:, p * PIECE:(p + 1) * PIECE],
                           ACT.Copy).then_inc(hi_split, 1)

        @block.gpsimd
        def _(pool):
            pool.memset(w_hi[1][:, OOFF:].bitcast(F32), 0.0).then_inc(out_cleared, 1)
            pool.memset(w_lo[1][:, OOFF:].bitcast(F32), 0.0).then_inc(out_cleared, 1)
            pool.sem_inc(lo_split, NT)

            def split_lo(group, par, p):
                pool.wait_ge(hi_split, group * NT + (p + 1))
                cols = slice(p * PIECE, (p + 1) * PIECE)
                pool.tensor_tensor(w_lo[par][:, cols], wraw[:, cols], w_hi[par][:, cols].bitcast(F32),
                                   ALU.subtract).then_inc(lo_split, 1)

            with pool.Fori(0, TURNS) as it:
                for j in range(STEPS):
                    split_lo(it * 2 + (j // NT + 1), (j // NT + 1) % 2, j % NT)

        @block.scalar
        def _(act):
            def evac_proj(S, e, dst):
                bank = e % 3
                act.wait_ge(proj_done, S * NPJ + (e + 1))
                act.activation(dst, psum[:, bank, :], ACT.Copy).then_inc(proj_free, 1)

            def o_high(S, a):
                act.wait_ge(pv_done, S * GH + (a + 1))
                act.activation(o_hi[:, a, :], psum[:, 5 + a, :], ACT.Copy).then_inc(o_hi_done, 1)

            def steps(it):
                for j in range(STEPS):
                    S = it * STEPS + j
                    evac_proj(S, 0, qT[:, 0, :])
                    evac_proj(S, 1, kT[:, 0, :])
                    o_high(S, 0)
                    o_high(S, 1)
                    evac_proj(S, 2, qT[:, 1, :])
                    split_hi(act, it * 2 + (j // NT + 1), (j // NT + 1) % 2, j % NT)
                    evac_proj(S, 3, kT[:, 1, :])
                    act.wait_ge(shifted, S + 1)
                    act.activation(ex[:], sc[:], ACT.Exp).then_inc(exp_done, 1)
                    evac_proj(S, 4, v_tok[:, 0:2, :].rearrange("p s n -> p (s n)"))
                    evac_proj(S, 5, v_tok[:, 2:4, :].rearrange("p s n -> p (s n)"))

            act.sem_inc(hi_split, NT)
            act.sem_inc(proj_free, 3)
            act.wait_ge(cleared, 2)
            with act.Fori(0, TURNS) as it:
                steps(it)
            o_high(TURNS * STEPS, 0)
            o_high(TURNS * STEPS, 1)

        @block.vector
        def _(dve):
            NSOFT = 5

            def tail(S, tile):
                for a in range(GH):
                    dve.wait_ge(o_hi_done, S * GH + (a + 1))
                    dve.tensor_tensor(o_lo[:, a, :], psum[:, 5 + a, :], o_hi[:, a, :].bitcast(F32),
                                      ALU.subtract).then_inc(tail_free, 1)
                for m in range(KC):
                    bank = 5 + (GH + m) % 3
                    dve.wait_ge(out_done, S * KC + (m + 1))
                    part = resid[:, m, tile * TT:(tile + 1) * TT]
                    dve.tensor_tensor(part, psum[:, bank, :], part, ALU.add).then_inc(tail_free, 1)

            def softmax(S):
                n = [0]

                def then(ins):
                    n[0] += 1
                    ins.then_inc(soft_step, 1)
                    dve.wait_ge(soft_step, S * NSOFT + n[0])

                dve.wait_ge(scores_done, S + 1)
                blocks = psum[:, 3:5, :].rearrange("p a (s n) -> p (a s) n", n=P)
                for b in range(P // SEQ):
                    q = slice(b * SEQ, (b + 1) * SEQ)
                    ins = dve.scalar_tensor_tensor(
                        out=sc[q, :, :], in0=blocks[q, :, b * SEQ:(b + 1) * SEQ], scalar=SCALE0,
                        in1=const("causal_add")[q, :].unsqueeze(1).broadcast_to([SEQ, NBK, SEQ]),
                        op0=ALU.mult, op1=ALU.add)
                then(ins)
                top, total, inv = stat[:, 0, :], stat[:, 1, :], stat[:, 2, :]
                then(dve.tensor_reduce(top, sc[:], AX_X, ALU.max))
                dve.tensor_tensor(sc[:], sc[:], top.unsqueeze(2).broadcast_to([P, NBK, SEQ]),
                                  ALU.subtract).then_inc(shifted, 1)
                dve.wait_ge(exp_done, S + 1)
                then(dve.tensor_reduce(total, ex[:], AX_X, ALU.add))
                then(dve.reciprocal(inv, total))
                then(dve.tensor_tensor(ex[:], ex[:], inv.unsqueeze(2).broadcast_to([P, NBK, SEQ]), ALU.mult))
                for b in range(P // SEQ):
                    q = slice(b * SEQ, (b + 1) * SEQ)
                    ins = dve.transpose(probT[q, :, b * SEQ:(b + 1) * SEQ], ex[q, :, :])
                ins.then_inc(prob_ready, 1)
                assert n[0] == NSOFT

            dve.memset(probT[:], 0.0).then_inc(cleared, 1)
            dve.memset(v_tok[:], 0.0).then_inc(cleared, 1)
            dve.sem_inc(tail_free, 3)
            dve.wait_ge(cleared, 2)
            dve.sem_inc(prob_ready, 1)
            with dve.Fori(0, TURNS) as it:
                for j in range(STEPS):
                    tail(it * STEPS + j, (j - 1) % NT)
                    softmax(it * STEPS + j)
            tail(TURNS * STEPS, NT - 1)

        @block.tensor
        def _(pe):
            def proj_bank(S, e):
                pe.wait_ge(proj_free, S * NPJ + (e + 1))
                return psum[:, e % 3, :]

            def project(S, e, par, off, tile):
                bank = proj_bank(S, e)
                cols = slice(tile * TT, (tile + 1) * TT)
                for c in range(KC):
                    mm = mm3(pe, bank, weight(par, off + c * GH * DH), (y_hi[:, c, cols], y_lo[:, c, cols]),
                             c == 0, c == KC - 1)
                mm.then_inc(proj_done, 1)

            def values(S, e, par, tile, half):
                bank = proj_bank(S, e)
                for i in range(2):
                    at = tile * TT + (2 * half + i) * P
                    for c in range(KC):
                        out = bank[:, i * GH * DH:(i + 1) * GH * DH]
                        mm = mm3(pe, out, (y_hi[:, c, at:at + P], y_lo[:, c, at:at + P]),
                                 weight(par, VOFF + c * GH * DH, GH * DH), c == 0, c == KC - 1)
                mm.then_inc(proj_done, 1)

            def scores(S, a, e):
                pe.wait_ge(proj_free, S * NPJ + (3 + e + 1))
                for i in range(SUBS):
                    tok = slice(i * P, (i + 1) * P)
                    mm = pe.matmul(psum[:, 3 + a, tok], qT[:, a, tok], kT[:, a, tok], start=True, stop=True)
                if a == GH - 1:
                    mm.then_inc(scores_done, 1)

            def prob_times_v(S):
                for a in range(GH):
                    pe.wait_ge(tail_free, S * NTL + (a + 1))
                    if a == 0:
                        pe.wait_ge(prob_ready, S + 1)
                        pe.wait_ge(proj_free, S * NPJ + 3)
                    for i in range(SUBS):
                        mm = pe.matmul(psum[:, 5 + a, i * P:(i + 1) * P], v_tok[:, i, a * DH:(a + 1) * DH],
                                       probT[:, a * SUBS + i, :], start=True, stop=True)
                    mm.then_inc(pv_done, 1)

            def output(S, par):
                pe.wait_ge(tail_free, S * NTL + (3 + GH))
                for m in range(KC):
                    pe.wait_ge(tail_free, S * NTL + (GH + m + 1))
                    for a in range(GH):
                        mm = mm3(pe, psum[:, 5 + (GH + m) % 3, :], weight(par, OOFF + a * DIM + m * P),
                                 (o_hi[:, a, :], o_lo[:, a, :]), a == 0, a == GH - 1)
                    mm.then_inc(out_done, 1)

            with pe.Fori(0, TURNS) as it:
                for j in range(STEPS):
                    S, par, tile = it * STEPS + j, j // NT, j % NT
                    if tile == 0:
                        pe.wait_ge(lo_split, it * (2 * NT) + (par + 1) * NT)
                    project(S, 0, par, QOFF, tile)
                    project(S, 1, par, KOFF, tile)
                    if j == 0:
                        pe.wait_ge(cleared, 2)
                        pe.wait_ge(out_cleared, 2)
                    prob_times_v(S)
                    project(S, 2, par, QOFF + DH, tile)
                    scores(S, 0, 1)
                    project(S, 3, par, KOFF + DH, tile)
                    output(S, ((j - 1) // NT) % 2)
                    scores(S, 1, 3)
                    values(S, 4, par, tile, 0)
                    values(S, 5, par, tile, 1)
            prob_times_v(TURNS * STEPS)
            output(TURNS * STEPS, 1)


def gather_adapters(pool, t, later, tile):
    now, raw = later["rows_now"], later["ranks_raw"]
    pool.tensor_copy(now[:], later["rows"][:, bass.ds(tile * AGROUPS, AGROUPS)]).then_inc(later["rows_copied"], 1)
    wait_apart(pool, later["rows_copied"], tile + 1, later["passed"])
    for i, src in enumerate((t["ada_a"], t["ada_b"])):
        for g in range(AGROUPS):
            pool.indirect_dma_start(out=raw[:, i * AGROUPS + g, :], out_offset=None, in_=src,
                                    in_offset=bass.IndirectOffsetOnAxis(ap=now[:, g:g + 1], axis=0)
                                    ).then_inc(later["gathered"], 16)


def octonion_ffn(nc, t, sb, sem, overlaid, const, mm3, resid, psum, kept_raw, kept, later):
    ctx = ExitStack()
    with ctx:
        fifth_a = kept[:, 0, C2_COLS:C2_COLS + KC * 2 * LR]
        c2_hi, c2_lo = kept[:, 0, 0:C2_COLS], kept[:, 1, 0:C2_COLS]
        up_raw, up = overlaid(ctx, "up", [P, 2, KC, HID])
        down_raw, down = overlaid(ctx, "down", [P, HTP * DIM])
        small, label_mask = later["ffn"], later["label_mask"]
        x_hi, x_lo = (sb(ctx, n, [P, KC, TT], F32R) for n in ("x_hi", "x_lo"))
        z_hi = x_hi
        zf, z = overlaid(ctx, "z", [P, KC, TOK])
        ranks_raw, ranks = later["ranks_raw"], later["ranks"]
        rank, fifth, rank_lo, rank_hi = ranks_raw[:, 0, :], ranks_raw[0:2 * LR, 1, :], ranks[:, 0, :], ranks[:, 2, :]
        work, work_r = overlaid(ctx, "work", [P, TERN_COLS])
        gate = work[:, 0:2 * TT].rearrange("p (a n) -> p a n", n=TT)
        hid = work[:, 2 * TT:5 * TT].rearrange("p (a n) -> p a n", n=TT)
        h_lo = work_r[:, 2 * TT:5 * TT].rearrange("p (a n) -> p a n", n=TT)
        h_hi = work_r[:, 5 * TT:8 * TT].rearrange("p (a n) -> p a n", n=TT)

        fifth_ready = sem(ctx, "fifth_ready")
        tern_in = [sem(ctx, f"tern_in{i}") for i in range(len(TERN))]
        tern_step, tern_ready, signed = sem(ctx, "tern_step"), sem(ctx, "tern_ready"), sem(ctx, "signed")
        x_used, x_hi_done, x_ready = sem(ctx, "x_used"), sem(ctx, "x_hi_done"), sem(ctx, "x_ready")
        rank_done, masked, rank_hi_done, rank_ready = (sem(ctx, n) for n in ("rank_done", "masked", "rank_hi_done", "rank_ready"))
        z_done, z_saved = sem(ctx, "z_done"), sem(ctx, "z_saved")
        z_hi_done, z_ready = sem(ctx, "z_hi_done"), sem(ctx, "z_ready")
        up_done, gate_done, hid_done, h_hi_done, h_ready = (
            sem(ctx, n) for n in ("up_done", "gate_done", "hid_done", "h_hi_done", "h_ready"))
        down_done, down_free = sem(ctx, "down_done"), sem(ctx, "down_free")
        raw_in = sem(ctx, "l1_raw_in")
        passed = sem(ctx, "ffn_passed")
        A_OFF, B_OFF = KC * DIM, KC * DIM + KC * LAB * LR
        LINKS = 2 * len(TERN)

        def c2(off, n=P):
            return c2_hi[:, off:off + n], c2_lo[:, off:off + n]

        def piece(k):
            return work[:, TERN[k][0]:TERN[k][0] + TERN[k][1]]

        def tern_dst(k, tile, up, down):
            if k < 2:
                return up[:, k, bass.ds(tile, 1), :].rearrange("p c n -> p (c n)")
            w = TERN[k][1]
            return down[:, bass.ds(tile * (2 * w) + (k - 2) * w, w)]

        def cols(a, c, tile):
            return a[:, c, bass.ds(tile * TT, TT)]

        s_gate, s_up, s_down = small[:, 10:11], small[:, 11:12], small[:, 12:13]
        with nc.Block() as block:
            @block.sync
            def _(sp):
                def load(tile, k):
                    a, w = TERN[k]
                    sp.dma_start(piece(k), t["oct_w"][bass.ds(tile, 1), :, a:a + w].rearrange("g p n -> (g p) n")
                                 ).then_inc(tern_in[k], 16)

                for k in range(len(TERN)):
                    load(0, k)
                with sp.Fori(1, NT) as tile:
                    for k in range(len(TERN)):
                        sp.wait_ge(tern_ready, tile * len(TERN) + (k + 1 - len(TERN)))
                        load(tile, k)
                sp.wait_ge(z_done, NT * KC)
                raw = kept_raw[:].rearrange("p a n -> p (a n)")
                for a, b in L1_PIECES:
                    sp.dma_start(raw[:, a:b], t["l1_w"][:, a:b]).then_inc(raw_in, 16)
                sp.wait_ge(raw_in, 16 * len(L1_PIECES))

            @block.scalar
            def _(act):
                def x_high(tile):
                    for c in range(KC):
                        wait_apart(act, x_used, tile * KC + (c + 1), passed)
                        act.activation(x_hi[:, c, :], cols(resid, c, tile), ACT.Copy).then_inc(x_hi_done, 1)

                def z_high(tile, c):
                    if c == 0:
                        wait_apart(act, up_done, tile * HT, passed)
                    act.activation(z_hi[:, c, :], cols(zf, c, tile), ACT.Copy).then_inc(z_hi_done, 1)

                def ranks_high(tile):
                    act.wait_ge(masked, tile * 3 + 3)
                    act.activation(rank_hi, rank, ACT.Copy).then_inc(rank_hi_done, 1)

                def save_z(tile):
                    for m in range(KC):
                        wait_apart(act, z_done, tile * KC + (m + 1), passed)
                        act.activation(cols(zf, m, tile), psum[:, 4 + m, :], ACT.Identity,
                                       bias=small[:, m:m + 1]).then_inc(z_saved, 1)

                def hidden(tile, last):
                    for h in range(HT):
                        r = min(P, HID - h * P)
                        act.wait_ge(up_done, tile * HT + (h + 1))
                        act.activation(gate[0:r, h % 2, :], psum[0:r, 2 * (h % 2), :], ACT.Silu,
                                       scale=s_gate[0:r, :]).then_inc(gate_done, 1)
                        if h == HT - 1 and not last:
                            z_high(tile + 1, 0)
                        act.wait_ge(hid_done, tile * HT + (h + 1))
                        act.activation(h_hi[0:r, h % 3, :], hid[0:r, h % 3, :], ACT.Copy).then_inc(h_hi_done, 1)
                    if not last:
                        for c in range(1, KC):
                            z_high(tile + 1, c)

                act.sem_inc(z_saved, KC)
                x_high(0)
                with act.Fori(0, NT - 1) as tile:
                    ranks_high(tile)
                    x_high(tile + 1)
                    save_z(tile)
                ranks_high(NT - 1)
                act.wait_ge(x_used, KC * (NT + 1))
                for c in range(KC):
                    act.activation(z_hi[:, c, :], zf[:, c, 0:TT], ACT.Copy).then_inc(z_hi_done, 1)
                save_z(NT - 1)
                with act.Fori(0, NT - 1) as tile:
                    hidden(tile, False)
                hidden(NT - 1, True)

            @block.vector
            def _(dve):
                def x_low(tile, chunks=range(KC)):
                    for c in chunks:
                        dve.wait_ge(x_hi_done, tile * KC + (c + 1))
                        dve.tensor_tensor(x_lo[:, c, :], cols(resid, c, tile),
                                          x_hi[:, c, :].bitcast(F32), ALU.subtract).then_inc(x_ready, 1)

                def z_low(tile, c):
                    dve.wait_ge(z_hi_done, tile * KC + (c + 1))
                    dve.tensor_tensor(cols(z, c, tile), cols(zf, c, tile), z_hi[:, c, :].bitcast(F32),
                                      ALU.subtract).then_inc(z_ready, 1)

                for i in range(2):
                    dve.tensor_copy(fifth_a.rearrange("p (c a r) -> p c a r", c=KC, a=2)[:, :, i, :],
                                    kept[:, i, A_OFF:B_OFF].bitcast(F32).rearrange("p (c r) -> p c r", c=KC)[:, :, P:]
                                    ).then_inc(fifth_ready, 1)
                x_low(0)

                def ternary(tile, k):
                    w = min(k, 2)
                    dve.wait_ge(tern_in[k], tile * 16 + 16)
                    dst = tern_dst(k, tile, up_raw, down_raw)
                    dve.tensor_scalar(dst, piece(k), small[:, 13 + w:14 + w], None, ALU.is_gt).then_inc(tern_step, 1)
                    dve.wait_ge(tern_step, tile * LINKS + (2 * k + 1))
                    dve.scalar_tensor_tensor(out=dst, in0=piece(k), scalar=small[:, 16 + w:17 + w], in1=dst,
                                             op0=ALU.is_lt, op1=ALU.subtract).then_inc(tern_step, 1)
                    dve.wait_ge(tern_step, tile * LINKS + (2 * k + 2))
                    dve.sem_inc(tern_ready, 1)

                def mask_ranks(tile):
                    def mine(k, rows):
                        return label_mask[0:rows, k, bass.ds(tile * BPT, BPT)].unsqueeze(2).broadcast_to([rows, BPT, SEQ])

                    for k, dst, rows in ((0, rank, P), (1, fifth, 2 * LR)):
                        dve.wait_ge(rank_done, tile * 2 + (k + 1))
                        dve.tensor_tensor(dst.rearrange("p (b s) -> p b s", s=SEQ),
                                          psum[0:rows, k, :].rearrange("p (b s) -> p b s", s=SEQ), mine(k, rows),
                                          ALU.mult).then_inc(masked, 1)
                    dve.wait_ge(masked, tile * 3 + 2)
                    dve.tensor_tensor(rank[0:2 * LR, :], rank[0:2 * LR, :], fifth, ALU.add).then_inc(masked, 1)
                    dve.wait_ge(rank_hi_done, tile + 1)
                    dve.tensor_tensor(rank_lo, rank, rank_hi.bitcast(F32), ALU.subtract).then_inc(rank_ready, 1)

                def hidden(tile, last):
                    for h in range(HT):
                        r = min(P, HID - h * P)
                        dve.wait_ge(gate_done, tile * HT + (h + 1))
                        dve.scalar_tensor_tensor(out=hid[0:r, h % 3, :], in0=psum[0:r, 2 * (h % 2) + 1, :],
                                                 scalar=s_up[0:r, :], in1=gate[0:r, h % 2, :],
                                                 op0=ALU.mult, op1=ALU.mult).then_inc(hid_done, 1)
                        dve.wait_ge(h_hi_done, tile * HT + (h + 1))
                        dve.tensor_tensor(h_lo[0:r, h % 3, :], hid[0:r, h % 3, :], h_hi[0:r, h % 3, :].bitcast(F32),
                                          ALU.subtract).then_inc(h_ready, 1)
                    if not last:
                        for c in range(KC):
                            z_low(tile + 1, c)
                    for m in range(KC):
                        dve.wait_ge(down_done, tile * KC + (m + 1))
                        part = cols(resid, m, tile)
                        dve.scalar_tensor_tensor(out=part, in0=psum[:, 4 + m, :], scalar=s_down, in1=part,
                                                 op0=ALU.mult, op1=ALU.add).then_inc(down_free, 1)

                with dve.Fori(0, NT - 1) as tile:
                    mask_ranks(tile)
                    for k in range(len(TERN) - 1):
                        ternary(tile, k)
                    x_low(tile + 1, range(KC // 2))
                    ternary(tile, len(TERN) - 1)
                    x_low(tile + 1, range(KC // 2, KC))
                mask_ranks(NT - 1)
                for k in range(len(TERN)):
                    ternary(NT - 1, k)
                for c in range(KC):
                    z_low(0, c)
                dve.sem_inc(down_free, KC)
                with dve.Fori(0, NT - 1) as tile:
                    hidden(tile, False)
                hidden(NT - 1, True)

            @block.gpsimd
            def _(pool):
                with pool.Fori(0, NT) as tile:
                    for k in range(len(TERN)):
                        pool.wait_ge(tern_ready, tile * len(TERN) + (k + 1))
                        w = TERN[k][1]
                        src, dst = tern_dst(k, tile, up_raw, down_raw), tern_dst(k, tile, up, down)
                        if k < 2:
                            run, sign = OH, const("sign_up")[:, bass.ds(tile * OCT, OCT)]
                        else:
                            run, sign = OD, const("sign_down")[:, bass.ds(tile * (2 * w // OD) + (k - 2) * (w // OD), w // OD)]
                        pool.tensor_tensor(dst.rearrange("p (k o) -> p k o", o=run),
                                           src.rearrange("p (k o) -> p k o", o=run),
                                           sign.unsqueeze(2).broadcast_to([P, w // run, run]), ALU.mult).then_inc(signed, 1)
                pool.wait_ge(z_done, NT * KC)
                gather_adapters(pool, t, later, 0)

            @block.tensor
            def _(pe):
                pe.sem_inc(x_used, KC)
                pe.wait_ge(fifth_ready, 2)
                with pe.Fori(0, NT) as tile:
                    for c in range(KC):
                        pe.wait_ge(x_ready, tile * KC + (c + 1))
                        x = x_hi[:, c, :], x_lo[:, c, :]
                        mm = mm3(pe, psum[:, 0, :], c2(A_OFF + c * LAB * LR), x, c == 0, c == KC - 1)
                        if c == KC - 1:
                            mm.then_inc(rank_done, 1)
                        for i in range(2):
                            mm = pe.matmul(psum[0:2 * LR, 1, :], fifth_a[:, c * 2 * LR:(c + 1) * 2 * LR], x[i],
                                           start=(c == 0 and i == 0), stop=(c == KC - 1 and i == 1))
                        if c == KC - 1:
                            mm.then_inc(rank_done, 1)
                    for c in range(KC):
                        x = x_hi[:, c, :], x_lo[:, c, :]
                        for m in range(KC):
                            if c == 0:
                                pe.wait_ge(z_saved, tile * KC + (m + 1))
                            mm = mm3(pe, psum[:, 4 + m, :], c2(c * DIM + m * P), x, c == 0, False)
                        mm.then_inc(x_used, 1)
                    pe.wait_ge(rank_ready, tile + 1)
                    for m in range(KC):
                        mm3(pe, psum[:, 4 + m, :], c2(B_OFF + m * P), (rank_hi, rank_lo), False, True).then_inc(z_done, 1)
                pe.wait_ge(signed, NT * len(TERN) - 2)
                with pe.Fori(0, NT) as tile:
                    def gate_up(h):
                        r = min(P, HID - h * P)
                        if h >= 2:
                            pe.wait_ge(hid_done, tile * HT + (h - 1))
                        for c in range(KC):
                            if h == 0:
                                pe.wait_ge(z_ready, tile * KC + (c + 1))
                            for w in range(2):
                                out = psum[0:r, 2 * (h % 2) + w, :]
                                wt = up[:, w, c, h * P:h * P + r]
                                pe.matmul(out, wt, z_hi[:, c, :], start=(c == 0), stop=False)
                                mm = pe.matmul(out, wt, cols(z, c, tile), start=False, stop=(c == KC - 1))
                        mm.then_inc(up_done, 1)

                    def down_product(h):
                        r = min(P, HID - h * P)
                        pe.wait_ge(h_ready, tile * HT + (h + 1))
                        if h == 0:
                            pe.wait_ge(z_saved, KC * (NT + 1))
                            pe.wait_ge(signed, NT * len(TERN))
                        for m in range(KC):
                            if h == 0:
                                pe.wait_ge(down_free, tile * KC + (m + 1))
                            wt = down[0:r, h * DIM + m * P:h * DIM + (m + 1) * P]
                            pe.matmul(psum[:, 4 + m, :], wt, h_hi[0:r, h % 3, :], start=(h == 0), stop=False)
                            mm = pe.matmul(psum[:, 4 + m, :], wt, h_lo[0:r, h % 3, :], start=False, stop=(h == HT - 1))
                            if h == HT - 1:
                                mm.then_inc(down_done, 1)

                    gate_up(0)
                    gate_up(1)
                    for h in range(2, HT):
                        gate_up(h)
                        down_product(h - 2)
                    down_product(HT - 2)
                    down_product(HT - 1)


def layer_one(nc, t, sb, sem, const, mm3, resid, psum, kept_raw, kept, later):
    NM = 2
    ctx = ExitStack()
    with ctx:
        w_raw = kept_raw[:].rearrange("p a n -> p (a n)")
        w_lo = kept[:].rearrange("p a n -> p (a n)")
        w_hi = sb(ctx, "w1_hi", [P, L1_COLS], F32R)
        x_hi, x_lo = (sb(ctx, n, [P, KC, TT], F32R) for n in ("x1_hi", "x1_lo"))
        r_hi, r_lo = (sb(ctx, n, [P, TT], F32R) for n in ("r_hi", "r_lo"))
        wide = sb(ctx, "wide", [P, KC, TT])
        misc = sb(ctx, "misc", [P, 2, TT])
        rank, gate_T = misc[:, 0, :], misc[:, 1, :]
        bound, tok, att = (sb(ctx, n, [P, KC, TT]) for n in ("bound", "tok", "att"))
        logit_rows = sb(ctx, "logit_rows", [2 * NE, TT])
        probe = sb(ctx, "probe", [P, 1])
        table_kept = sem(ctx, "table_kept")
        routers = sb(ctx, "routers", [P, NM, KC, 2, NE], F32R)
        a_raw, b_raw = later["ranks_raw"][:, 0:AGROUPS, :], later["ranks_raw"][:, AGROUPS:, :]
        a_hi, a_lo, b_hi, b_lo = (sb(ctx, n, [P, AGROUPS, DIM], F32R) for n in ("a_hi", "a_lo", "b_hi", "b_lo"))
        small, lang = later["l1"], later["lang"]
        gat = sb(ctx, "gat", [P, 12, SUBS * NE])
        gat_i = sb(ctx, "gat_i", [P, SUBS * NE], U32)
        spread = sb(ctx, "spread", [P, SUBS, NE, ER])

        l1_hi_done, l1_ready, prep_step = sem(ctx, "l1_hi_done"), sem(ctx, "l1_ready"), sem(ctx, "prep_step")
        l1_pool_ready = sem(ctx, "l1_pool_ready")
        gathered = later["gathered"]
        a_turned, a_hi_done, a_ready = sem(ctx, "a_turned"), sem(ctx, "a_hi_done"), sem(ctx, "a_ready")
        b_hi_done, b_ready = sem(ctx, "b_hi_done"), sem(ctx, "b_ready")
        x_used, x0_ready = sem(ctx, "x1_used"), sem(ctx, "x0_ready")
        x_hi_done, x_ready = sem(ctx, "x1_hi_done"), sem(ctx, "x1_ready")
        rank_done, rank_masked = sem(ctx, "rank1_done"), sem(ctx, "rank_masked")
        r_hi_done, r_ready = sem(ctx, "r_hi_done"), sem(ctx, "r_ready")
        base_done, wide_done, bound_done = sem(ctx, "base_done"), sem(ctx, "wide_done"), sem(ctx, "bound_done")
        wide_free = sem(ctx, "wide_free")
        rows_done, rows_saved = sem(ctx, "rows_done"), sem(ctx, "rows_saved")
        turned, tok_done, s_done, sig_done, att_done = (
            sem(ctx, n) for n in ("turned", "tok_done", "s_done", "sig_done", "att_done"))
        pv_done, resid_done = sem(ctx, "pv1_done"), sem(ctx, "resid_done")
        logits_done, gate_step, e_done = sem(ctx, "logits_done"), sem(ctx, "gate_step"), sem(ctx, "e_done")
        spread_done, gateT_done, gateT_copied = sem(ctx, "spread_done"), sem(ctx, "gateT_done"), sem(ctx, "gateT_copied")
        h_done, gated, g_hi_done, g_ready = (sem(ctx, n) for n in ("h_done", "gated", "g_hi_done", "g_ready"))
        moe_done, c_hi_done, c_ready = sem(ctx, "moe_done"), sem(ctx, "c_hi_done"), sem(ctx, "c_ready")
        out_ready, out_stored = sem(ctx, "out_ready"), sem(ctx, "out_stored")
        act_passed, dve_passed = sem(ctx, "act_passed"), sem(ctx, "dve_passed")
        pe_passed = sem(ctx, "pe_passed")

        def wt(block, off, n=P):
            a = L1_AT[block] + off
            return w_hi[:, a:a + n], w_lo[:, a:a + n]

        def mine(tile, m):
            return resid[:, m, bass.ds(tile * TT, TT)]

        NG, NS = 19, 21
        with nc.Block() as block:
            @block.sync
            def _(sp):
                sp.sem_inc(wide_free, 1)
                with sp.Fori(0, NT) as tile:
                    for m in range(KC):
                        sp.wait_ge(out_ready, tile * KC + (KC + m + 1))
                        sp.dma_start(t["out"][m * P:(m + 1) * P, bass.ds(tile * TT, TT)], wide[:, m, :]).then_inc(out_stored, 16)
                    sp.wait_ge(out_stored, tile * (16 * KC) + 16 * KC)
                    sp.sem_inc(wide_free, 1)

            @block.gpsimd
            def _(pool):
                def low_parts(tile):
                    for c in range(KC):
                        pool.wait_ge(x_hi_done, tile * 2 * KC + (c + 1))
                        pool.tensor_tensor(x_lo[:, c, :], mine(tile, c), x_hi[:, c, :].bitcast(F32),
                                           ALU.subtract).then_inc(x0_ready, 1)
                    pool.wait_ge(b_hi_done, tile + 1)
                    pool.tensor_tensor(b_lo[:], b_raw, b_hi[:].bitcast(F32), ALU.subtract).then_inc(b_ready, 1)

                def next_gather(tile):
                    pool.wait_ge(b_ready, tile + 1)
                    pool.wait_ge(a_turned, tile * AGROUPS + AGROUPS)
                    pool.wait_ge(gathered, tile * GATHERED + GATHERED)
                    gather_adapters(pool, t, later, tile + 1)

                low_parts(0)
                for k, (a, b) in enumerate(L1_PIECES[1:]):
                    pool.wait_ge(prep_step, k + 1)
                    pool.tensor_tensor(w_lo[:, a:b], w_raw[:, a:b], w_hi[:, a:b].bitcast(F32),
                                       ALU.subtract).then_inc(l1_pool_ready, 1)
                pool.wait_ge(l1_pool_ready, len(L1_PIECES) - 1)
                for i, w in enumerate((w_hi[:], w_lo)):
                    pool.tensor_copy(routers[:, :, :, i, :], w[:, L1_AT["R2"]:].bitcast(F32)
                                     .rearrange("p (l c e) -> p l c e", l=NM, c=KC)).then_inc(l1_pool_ready, 1)
                next_gather(0)
                with pool.Fori(1, NT - 1) as tile:
                    low_parts(tile)
                    next_gather(tile)
                low_parts(NT - 1)

            @block.scalar
            def _(act):
                def x_high(tile, c):
                    wait_apart(act, x_used, tile * KC + (c + 1), act_passed)
                    act.activation(x_hi[:, c, :], mine(tile, c), ACT.Copy).then_inc(x_hi_done, 1)

                def work(tile):
                    act.activation(probe[:], const("count")[:, 0:1], ACT.Sigmoid).then_inc(table_kept, 1)
                    act.wait_ge(table_kept, tile + 1)
                    for g in range(AGROUPS):
                        act.wait_ge(a_turned, tile * AGROUPS + (g + 1))
                        act.activation(a_hi[:, g, :], psum[:, g, :], ACT.Copy).then_inc(a_hi_done, 1)
                    act.wait_ge(gathered, tile * GATHERED + GATHERED)
                    act.activation(b_hi[:], b_raw, ACT.Copy).then_inc(b_hi_done, 1)
                    act.wait_ge(rank_masked, tile + 1)
                    act.activation(r_hi[:], rank, ACT.Copy).then_inc(r_hi_done, 1)
                    for m in range(KC):
                        act.wait_ge(base_done, tile * KC + (m + 1))
                        if m == 0:
                            act.wait_ge(wide_free, tile + 1)
                        act.activation(wide[:, m, :], psum[:, 4 + m, :], ACT.Identity,
                                       bias=small[:, m:m + 1]).then_inc(wide_done, 1)
                    for m in range(KC):
                        act.wait_ge(turned, tile * KC + (m + 1))
                        act.activation(tok[:, m, :], psum[:, m % 2, :], ACT.Copy).then_inc(tok_done, 1)
                        act.wait_ge(s_done, tile * KC + (m + 1))
                        act.activation(att[:, m, :], psum[:, 2 + m % 2, :], ACT.Sigmoid,
                                       scale=SCALE1).then_inc(sig_done, 1)
                    for m in range(KC):
                        wait_apart(act, resid_done, tile * KC + (m + 1), act_passed)
                        act.activation(x_hi[:, m, :], mine(tile, m), ACT.Copy).then_inc(x_hi_done, 1)
                    for layer in range(NM):
                        act.wait_ge(rows_done, tile * NM + (layer + 1))
                        act.activation(logit_rows[:], psum[0:2 * NE, 3, :], ACT.Copy).then_inc(rows_saved, 1)
                        if layer == 0:
                            act.wait_ge(gate_step, tile * (NG + NS) + 12)
                            act.activation(gat[:, 2, 0:SUBS], gat[:, 2, 0:SUBS], ACT.Sigmoid).then_inc(e_done, 1)
                        act.wait_ge(gateT_done, tile * NM + (layer + 1))
                        act.activation(gate_T, psum[:, 2, :], ACT.Copy).then_inc(gateT_copied, 1)
                        act.wait_ge(gated, tile * NM + (layer + 1))
                        act.activation(r_hi[:], rank, ACT.Copy).then_inc(g_hi_done, 1)
                        if layer == 0:
                            for m in range(KC):
                                act.wait_ge(moe_done, tile * KC * NM + (m + 1))
                                act.activation(x_hi[:, m, :], psum[:, 4 + m, :], ACT.Copy).then_inc(c_hi_done, 1)

                for c in range(KC):
                    at = slice(c * DIM, (c + 1) * DIM)
                    act.activation(w_hi[:, at], w_raw[:, at], ACT.Copy).then_inc(l1_hi_done, 1)
                    x_high(0, c)
                with act.Fori(0, NT - 1) as tile:
                    work(tile)
                    for c in range(KC):
                        x_high(tile + 1, c)
                work(NT - 1)

            @block.vector
            def _(dve):
                def gate_chain(tile, first):
                    k = [0]

                    def then(*several):
                        for ins in several:
                            k[0] += 1
                            ins.then_inc(gate_step, 1)
                        dve.wait_ge(gate_step, tile * (NG + NS) + (first + k[0]))
                    return then, k

                def g(i, n=NE):
                    return gat[:, i, 0:SUBS * n].rearrange("p (s e) -> p s e", s=SUBS)

                def per(a):
                    return a.unsqueeze(2).broadcast_to([P, SUBS, NE])

                def row(a):
                    return a.unsqueeze(1).broadcast_to([P, SUBS, NE])

                def tt(then, out, a, b, op):
                    then(dve.tensor_tensor(out, a, b, op))

                def top2_gates(tile):
                    then, k = gate_chain(tile, 0)
                    dve.wait_ge(logits_done, tile * NM + 1)
                    lg, top, hot, gates = g(0), g(1), g(4), g(5)
                    both = psum[:, 0, 0:SUBS * 2 * NE].rearrange("p (s a e) -> p s a e", s=SUBS, a=2)
                    tt(then, lg, both[:, :, 1, :], lang[:, bass.ds(tile * SUBS, SUBS), :], ALU.add)
                    tt(then, lg, both[:, :, 0, :], lg, ALU.add)
                    dve.sem_inc(dve_passed, 1)
                    then(*[dve.max(top[:, s, :], lg[:, s, :]) for s in range(SUBS)])
                    dve.sem_inc(dve_passed, 1)
                    then(*[dve.max_index(gat_i[:, s * NE:(s + 1) * NE], top[:, s, :], lg[:, s, :]) for s in range(SUBS)])
                    then(dve.tensor_copy(g(6), gat_i[:].rearrange("p (s e) -> p s e", s=SUBS)))
                    e2, w1, w2 = gat[:, 2, 0:SUBS], gat[:, 3, 0:SUBS], gat[:, 3, SUBS:2 * SUBS]
                    tt(then, e2, top[:, :, 1], top[:, :, 0], ALU.subtract)
                    dve.wait_ge(e_done, tile + 1)
                    then(dve.tensor_scalar(w2, e2, 2.0, None, ALU.mult))
                    then(dve.tensor_scalar(w1, e2, -2.0, 2.0, ALU.mult, ALU.add))
                    tt(then, hot, row(const("iota")), per(g(6)[:, :, 0]), ALU.is_equal)
                    tt(then, gates, hot, per(w1), ALU.mult)
                    tt(then, hot, row(const("iota")), per(g(6)[:, :, 1]), ALU.is_equal)
                    tt(then, hot, hot, per(w2), ALU.mult)
                    tt(then, gates, gates, hot, ALU.add)
                    assert k[0] == NG, k
                    return gates

                def sparsemax_gates(tile):
                    then, k = gate_chain(tile, NG)
                    dve.wait_ge(logits_done, tile * NM + 2)
                    z, srt, cum, alt, sup = g(0), g(1), g(4), g(5), g(6)
                    both = psum[:, 0, SUBS * 2 * NE:2 * SUBS * 2 * NE].rearrange("p (s a e) -> p s a e", s=SUBS, a=2)
                    tt(then, z, both[:, :, 1, :], row(small[:, 56:64]), ALU.add)
                    tt(then, z, both[:, :, 0, :], z, ALU.add)
                    dve.sem_inc(dve_passed, 1)
                    then(*[dve.max(srt[:, s, :], z[:, s, :]) for s in range(SUBS)])
                    src = srt
                    for d, dst in ((1, cum), (2, alt), (4, cum)):
                        then(dve.tensor_copy(dst[:, :, 0:d], src[:, :, 0:d]))
                        tt(then, dst[:, :, d:], src[:, :, d:], src[:, :, 0:NE - d], ALU.add)
                        src = dst
                    tt(then, alt, srt, row(const("count")), ALU.mult)
                    then(dve.scalar_tensor_tensor(out=sup, in0=alt, scalar=1.0, in1=cum, op0=ALU.add, op1=ALU.is_gt))
                    kz, ts_, tau = gat[:, 2, 0:SUBS], gat[:, 2, SUBS:2 * SUBS], gat[:, 3, 0:SUBS]
                    then(dve.tensor_reduce(kz, sup, AX_X, ALU.add))
                    tt(then, alt, row(const("count")), per(kz), ALU.is_equal)
                    tt(then, alt, alt, cum, ALU.mult)
                    then(dve.tensor_reduce(ts_, alt, AX_X, ALU.add))
                    then(dve.reciprocal(kz, kz))
                    then(dve.scalar_tensor_tensor(out=tau, in0=ts_, scalar=-1.0, in1=kz, op0=ALU.add, op1=ALU.mult))
                    tt(then, z, z, per(tau), ALU.subtract)
                    assert k[0] == NS, k
                    return z

                def mask_att(dve, tile, m):
                    dve.wait_ge(sig_done, tile * KC + (m + 1))
                    dve.tensor_tensor(att[:, m, :].rearrange("p (s n) -> p s n", n=P),
                                      att[:, m, :].rearrange("p (s n) -> p s n", n=P),
                                      const("causal_mul").unsqueeze(1).broadcast_to([P, SUBS, P]),
                                      ALU.mult).then_inc(att_done, 1)

                def add_attention(tile, m):
                    dve.wait_ge(pv_done, tile * KC + (m + 1))
                    dve.scalar_tensor_tensor(out=mine(tile, m), in0=psum[:, 4 + m, :], scalar=small[:, 12 + m:13 + m],
                                             in1=mine(tile, m), op0=ALU.mult, op1=ALU.add).then_inc(resid_done, 1)

                def x_low(tile, m):
                    dve.wait_ge(x_hi_done, tile * 2 * KC + (KC + m + 1))
                    dve.tensor_tensor(x_lo[:, m, :], mine(tile, m), x_hi[:, m, :].bitcast(F32),
                                      ALU.subtract).then_inc(x_ready, 1)

                dve.sem_inc(out_ready, KC)
                for c in range(KC):
                    at = slice(c * DIM, (c + 1) * DIM)
                    dve.wait_ge(l1_hi_done, c + 1)
                    dve.tensor_tensor(w_lo[:, at], w_raw[:, at], w_hi[:, at].bitcast(F32), ALU.subtract).then_inc(l1_ready, 1)
                for k, (a, b) in enumerate(L1_PIECES[1:]):
                    dve.tensor_copy(w_hi[:, a:b], w_raw[:, a:b]).then_inc(prep_step, 1)

                def adapter_ranks(tile):
                    for g in range(AGROUPS):
                        dve.wait_ge(a_hi_done, tile * AGROUPS + (g + 1))
                        dve.tensor_tensor(a_lo[:, g, :], psum[:, g, :], a_hi[:, g, :].bitcast(F32),
                                          ALU.subtract).then_inc(a_ready, 1)
                    dve.wait_ge(rank_done, tile + 1)
                    dve.tensor_tensor(rank.rearrange("p (b s) -> p b s", s=SEQ),
                                      psum[:, 2, :].rearrange("p (b s) -> p b s", s=SEQ),
                                      const("own_batch").unsqueeze(2).broadcast_to([P, BPT, SEQ]),
                                      ALU.mult).then_inc(rank_masked, 1)
                    dve.wait_ge(r_hi_done, tile + 1)
                    dve.tensor_tensor(r_lo[:], rank, r_hi[:].bitcast(F32), ALU.subtract).then_inc(r_ready, 1)

                with dve.Fori(0, NT) as tile:
                    adapter_ranks(tile)
                    for m in range(KC):
                        dve.wait_ge(wide_done, tile * KC + (m + 1))
                        dve.tensor_scalar(bound[:, m, :], wide[:, m, :], small[:, 8 + m:9 + m], None,
                                          ALU.mult).then_inc(bound_done, 1)
                    for m in range(KC - 1):
                        mask_att(dve, tile, m)
                    add_attention(tile, 0)
                    mask_att(dve, tile, KC - 1)
                    for m in range(1, KC):
                        add_attention(tile, m)
                        x_low(tile, m - 1)
                    x_low(tile, KC - 1)
                    for layer, gates_of in enumerate((top2_gates, sparsemax_gates)):
                        gates = gates_of(tile)
                        wide_gates = gates.unsqueeze(3).broadcast_to([P, SUBS, NE, ER])
                        if layer == 0:
                            dve.tensor_copy(spread[:], wide_gates).then_inc(spread_done, 1)
                        else:
                            dve.tensor_scalar(spread[:], wide_gates, 0.0, None, ALU.max).then_inc(spread_done, 1)
                        dve.wait_ge(h_done, tile * NM + (layer + 1))
                        dve.wait_ge(gateT_copied, tile * NM + (layer + 1))
                        dve.tensor_tensor(rank, psum[:, 1, :], gate_T, ALU.mult).then_inc(gated, 1)
                        dve.wait_ge(g_hi_done, tile * NM + (layer + 1))
                        dve.tensor_tensor(r_lo[:], rank, r_hi[:].bitcast(F32),
                                          ALU.subtract).then_inc(g_ready, 1)
                        for m in range(KC):
                            if layer == 0:
                                dve.wait_ge(c_hi_done, tile * KC + (m + 1))
                                dve.tensor_tensor(x_lo[:, m, :], psum[:, 4 + m, :], x_hi[:, m, :].bitcast(F32),
                                                  ALU.subtract).then_inc(c_ready, 1)
                            else:
                                dve.wait_ge(moe_done, tile * KC * NM + (KC + m + 1))
                                dve.scalar_tensor_tensor(out=wide[:, m, :], in0=psum[:, 4 + m, :],
                                                         scalar=small[:, 4 + m:5 + m], in1=mine(tile, m),
                                                         op0=ALU.add, op1=ALU.add).then_inc(out_ready, 1)

            @block.tensor
            def _(pe):
                def xs(c):
                    return x_hi[:, c, :], x_lo[:, c, :]

                pe.sem_inc(x_used, KC)
                with pe.Fori(0, NT) as tile:
                    def base(c):
                        pe.wait_ge(x0_ready, tile * KC + (c + 1))
                        pe.wait_ge(l1_ready, c + 1)
                        for m in range(KC):
                            if c == 0:
                                pe.wait_ge(out_ready, tile * KC + (m + 1))
                            mm3(pe, psum[:, 4 + m, :], wt("Wc", c * DIM + m * P), xs(c), c == 0, False)

                    GT = TT // AGROUPS
                    pe.wait_ge(gathered, tile * GATHERED + GATHERED)
                    for g in range(AGROUPS):
                        for c in range(KC):
                            tr = pe.transpose(psum[:, g, c * P:(c + 1) * P], a_raw[:, g, c * P:(c + 1) * P], const("ident"))
                        tr.then_inc(a_turned, 1)
                    base(0)
                    base(1)
                    pe.wait_ge(x0_ready, tile * KC + KC)
                    for g in range(AGROUPS):
                        pe.wait_ge(a_ready, tile * AGROUPS + (g + 1))
                        cols = slice(g * GT, (g + 1) * GT)
                        for c in range(KC):
                            mm = mm3(pe, psum[:, 2, cols], (a_hi[:, g, c * P:(c + 1) * P], a_lo[:, g, c * P:(c + 1) * P]),
                                     (x_hi[:, c, cols], x_lo[:, c, cols]), c == 0, c == KC - 1)
                    mm.then_inc(rank_done, 1)
                    base(2)
                    base(3)
                    pe.wait_ge(r_ready, tile + 1)
                    pe.wait_ge(b_ready, tile + 1)
                    for m in range(KC):
                        for g in range(AGROUPS):
                            cols = slice(g * GT, (g + 1) * GT)
                            mm = mm3(pe, psum[:, 4 + m, cols], (b_hi[:, g, m * P:(m + 1) * P], b_lo[:, g, m * P:(m + 1) * P]),
                                     (r_hi[:, cols], r_lo[:, cols]), False, g == AGROUPS - 1)
                        mm.then_inc(base_done, 1)

                    def turn_and_score(m):
                        if m >= 2:
                            pe.wait_ge(tok_done, tile * KC + (m - 1))
                            pe.wait_ge(sig_done, tile * KC + (m - 1))
                        pe.wait_ge(wide_done, tile * KC + (m + 1))
                        for i in range(SUBS):
                            tr = pe.transpose(psum[:, m % 2, i * P:(i + 1) * P], wide[:, m, i * P:(i + 1) * P], const("ident"))
                        tr.then_inc(turned, 1)
                        pe.wait_ge(bound_done, tile * KC + (m + 1))
                        for i in range(SUBS):
                            cols = slice(i * P, (i + 1) * P)
                            mm = pe.matmul(psum[:, 2 + m % 2, cols], bound[:, m, cols], wide[:, m, cols], start=True, stop=True)
                        mm.then_inc(s_done, 1)

                    def attend(m):
                        pe.wait_ge(tok_done, tile * KC + (m + 1))
                        pe.wait_ge(att_done, tile * KC + (m + 1))
                        for i in range(SUBS):
                            cols = slice(i * P, (i + 1) * P)
                            mm = pe.matmul(psum[:, 4 + m, cols], tok[:, m, cols], att[:, m, cols], start=True, stop=True)
                        mm.then_inc(pv_done, 1)

                    for m in range(KC):
                        turn_and_score(m)
                        if m >= 2:
                            attend(m - 2)
                    attend(KC - 2)
                    attend(KC - 1)

                    for layer, (W, A, B) in enumerate((("W2", "A2", "B2"), ("Wf", "Af", "Bf"))):
                        def expert_ranks_and_logits(c):
                            if layer == 0:
                                pe.wait_ge(x_ready, tile * KC + (c + 1))
                            else:
                                pe.wait_ge(c_ready, tile * KC + (c + 1))
                            mm = mm3(pe, psum[:, 1, :], wt(A, c * P), xs(c), c == 0, c == KC - 1)
                            if c == KC - 1:
                                mm.then_inc(h_done, 1)
                            for i in range(2):
                                mm = pe.matmul(psum[0:2 * NE, 3, :], routers[:, layer, c, :, :].rearrange("p a e -> p (a e)"), xs(c)[i],
                                               start=(c == 0 and i == 0), stop=(c == KC - 1 and i == 1))
                            if c == KC - 1:
                                mm.then_inc(rows_done, 1)

                        def base_products(first, last):
                            for c, m in [(n // KC, n % KC) for n in range(first, last)]:
                                mm = mm3(pe, psum[:, 4 + m, :], wt(W, c * DIM + m * P), xs(c), c == 0, False)
                                if layer == 1 and m == KC - 1:
                                    mm.then_inc(x_used, 1)

                        pe.wait_ge(l1_pool_ready, len(L1_PIECES) + 1)
                        for c in range(KC):
                            expert_ranks_and_logits(c)
                        base_products(0, LOGITS_AT)
                        wait_apart(pe, rows_saved, tile * NM + (layer + 1), pe_passed)
                        for i in range(SUBS):
                            at = (layer * SUBS + i) * 2 * NE
                            tr = pe.transpose(psum[:, 0, at:at + 2 * NE], logit_rows[:, i * P:(i + 1) * P],
                                              const("ident")[0:2 * NE, 0:2 * NE])
                        tr.then_inc(logits_done, 1)
                        base_products(LOGITS_AT, GATES_AT)
                        pe.wait_ge(spread_done, tile * NM + (layer + 1))
                        for i in range(SUBS):
                            tr = pe.transpose(psum[:, 2, i * P:(i + 1) * P], spread[:, i, :, :].rearrange("p e r -> p (e r)"),
                                              const("ident"))
                        tr.then_inc(gateT_done, 1)
                        base_products(GATES_AT, KC * KC)
                        pe.wait_ge(g_ready, tile * NM + (layer + 1))
                        for m in range(KC):
                            mm3(pe, psum[:, 4 + m, :], wt(B, m * P), (r_hi[:], r_lo[:]), False, True).then_inc(moe_done, 1)


def kernel(**inputs):
    import concourse.bacc as bacc
    from concourse.bass_utils import run_bass_kernel_spmd

    a = {k: np.asarray(v) for k, v in inputs.items()}
    f32 = np.float32

    def chunks(w, width=None):
        return w.reshape(KC, P, -1).transpose(1, 0, 2).reshape(P, -1)

    def flipped(w):
        return w.reshape(KC, P, -1)[:, ::-1].reshape(KC * P, -1)

    def both(w):
        return np.concatenate([w.T, w.T], 0)

    arrays = {}
    arrays["xT"] = a["x"].reshape(TOK, DIM).T
    log_dt = np.broadcast_to(a["L0_cond_log_dt"], (P, SEQ))
    C = a["L0_cond_C"]
    arrays["s4d"] = np.stack([log_dt, both(a["L0_cond_log_A_real"]), both(a["L0_cond_A_imag"]),
                              both(C[..., 0]), both(C[..., 1])], 1)
    skip = np.zeros((LI, SEQ, LJ), f32)
    skip[LI - 1, :, LJ - 1] = a["L0_cond_D"]
    arrays["skip"] = skip.reshape(LI, -1)
    arrays["zeros"] = np.zeros((SEQ, P), f32)
    arrays["lengths"] = np.broadcast_to(a["itok_B_78_3631"].astype(np.int32), (P, BATCH))
    arrays["consts"] = constant_table()[0]

    wq = flipped(a["L0_attn_wq"].reshape(DIM, HEADS, DQ)[:, :, :DH].reshape(DIM, HEADS * DH))
    wkv = flipped(a["L0_attn_wkv"])
    wo = a["L0_attn_wo"].reshape(GROUPS, GH, DH, DIM)

    def grouped(w):
        return w.reshape(KC, P, GROUPS, GH * DH).transpose(2, 1, 0, 3).reshape(GROUPS, P, -1)

    arrays["attn_w"] = np.concatenate([
        grouped(wq), grouped(wkv[:, :HEADS * DH]), grouped(wkv[:, HEADS * DH:2 * HEADS * DH]),
        wo.transpose(0, 2, 1, 3).reshape(GROUPS, P, -1)], 2)

    lora_a = a["L0_cond2_lora_A"].transpose(1, 0, 2).reshape(DIM, LAB * LR)
    lora_b = np.tile(a["L0_cond2_lora_B"].T, (P // LR, 1))
    c2_w = np.concatenate([chunks(a["L0_cond2_weight"].T), chunks(lora_a), lora_b,
                           np.zeros((P, GW - C2_COLS), f32)], 1)
    arrays["attn_w"] = np.concatenate([arrays["attn_w"], c2_w[None]], 0)
    arrays["c2_bias"] = a["L0_cond2_bias"].reshape(KC, P).T
    j_of, _ = octonion_table()
    ffn = [a["L0_ffn_w_gate"], a["L0_ffn_w_up"], a["L0_ffn_w_down"]]
    arrays["oct_base"] = np.stack([w.reshape(P, -1) for w in ffn], 1)
    gate_up = [w[j_of].transpose(0, 3, 1, 2).reshape(KC, P, HID) for w in ffn[:2]]
    dn = ffn[2][j_of].transpose(0, 3, 1, 2).reshape(HID, DIM)
    dn = np.concatenate([dn, np.zeros((HTP * P - HID, DIM), f32)], 0)
    dn = dn.reshape(NT, HTP // NT, P, DIM).transpose(0, 2, 1, 3).reshape(NT, P, -1)
    arrays["oct_w"] = np.concatenate(gate_up + [dn], 2)

    arrays["ada_a"] = a["L1_cond_lora_A_w"].reshape(ADA * AR, DIM)
    arrays["ada_b"] = a["L1_cond_lora_B_w"].transpose(0, 2, 1).reshape(ADA * AR, DIM)
    blocks = {
        "Wc": chunks(a["L1_cond_base_weight"].T),
        "W2": chunks(a["L1_cond2_W"].T), "Wf": chunks(a["L1_ffn_W_base"].T),
        "A2": chunks(a["L1_cond2_A"].reshape(NE * ER, DIM).T),
        "B2": a["L1_cond2_B"].transpose(0, 2, 1).reshape(NE * ER, DIM),
        "Af": chunks(a["L1_ffn_lora_A"].transpose(1, 0, 2).reshape(DIM, NE * ER)),
        "Bf": a["L1_ffn_lora_B"].reshape(NE * ER, DIM),
        "R2": chunks(a["L1_cond2_Wr"].T), "Rf": chunks(a["L1_ffn_W_router"].T),
    }
    arrays["l1_w"] = np.concatenate([blocks[n] for n, _ in L1_BLOCKS], 1)
    small = np.zeros((P, 32), f32)
    small[:, 0:4] = a["L1_cond_base_bias"].reshape(KC, P).T
    small[:, 4:8] = a["L1_ffn_b_base"].reshape(KC, P).T
    small[:, 20:24], small[:, 24:28], small[:, 28:32] = (a[f"L1_attn_bv_{n}"].T for n in "qkv")
    arrays["l1_small"] = small
    arrays["router_bias"] = np.broadcast_to(a["L1_ffn_b_router"], (P, NE))
    arrays["ids"] = np.concatenate([
        np.broadcast_to(a["itok_B_0_4"].astype(np.int32), (P, BATCH)),
        np.repeat(a["itok_B_6_15"].astype(np.int32), AR).reshape(BATCH // ABATCH, P).T,
        np.repeat(a["itok_B_0_7"].astype(np.int32), SEQ).reshape(TOK // P, P).T], 1)

    nc = bacc.Bacc("TRN2", target_bir_lowering=False, num_devices=1)
    given, handles = {}, {}
    for name, v in arrays.items():
        v = np.ascontiguousarray(v)
        given[f"in_{name}"] = v
        handles[name] = nc.dram_tensor(f"in_{name}", v.shape, mybir.dt.from_np(v.dtype), kind="ExternalInput").ap()
    handles["out"] = nc.dram_tensor("outT", (DIM, TOK), F32, kind="ExternalOutput").ap()
    build_program(nc, handles)
    r = run_bass_kernel_spmd(nc, [given], core_ids=[0])
    return r.results[0]["outT"].T.reshape(BATCH, SEQ, DIM)
```
